# Optimizing a Trainium2 kernel written in Bass

```python
import numpy as np
import jax
import jax.numpy as jnp

def _softmax(x, axis=-1):
    return jax.nn.softmax(x, axis=axis)

def _gelu(x):
    return jax.nn.gelu(x, approximate=True)

def _silu(x):
    return jax.nn.silu(x)

def _sigmoid(x):
    return jax.nn.sigmoid(x)

def _layernorm(x, axis=-1, eps=1e-05):
    m = jnp.mean(x, axis=axis, keepdims=True)
    v = jnp.var(x, axis=axis, keepdims=True)
    return (x - m) / jnp.sqrt(v + eps)

def _scatter_add(tgt, idx, src, axis=0):
    return tgt.at[idx].add(src)

def _segment_sum(src, seg, n):
    return jax.ops.segment_sum(src, seg, n)
kernel_name = 'mk_gnn_preln_d4_gnn_r16_9cd523'

def setup_inputs(seed: int=0):
    np.random.seed(seed)
    _w = jnp.asarray

    def _rec_inputs():
        import jax
        import jax.numpy as jnp
        _gk = jax.random.key(seed)
        x = -0.0002117 + 1 * jax.random.normal(jax.random.fold_in(_gk, 1), (625, 512), jnp.float32)
        src = jax.random.randint(jax.random.fold_in(_gk, 2), (20000,), 0, 625, jnp.int32)
        dst = jnp.minimum((625 * jax.random.uniform(jax.random.fold_in(_gk, 3), (20000,)) ** 2.0).astype(jnp.int32), 9999)
        _o = jnp.argsort(dst, stable=True)
        src = src[_o]
        dst = dst[_o]
        edge_weight = jax.random.uniform(jax.random.fold_in(_gk, 12), (20000,), jnp.float32, 0.0, 1)
        node_vec1 = jax.random.uniform(jax.random.fold_in(_gk, 13), (625, 1), jnp.float32, 0.0, 0.999957)
        return (x, src, dst, edge_weight, node_vec1)
    x, src, dst, edge_weight, node_vec1 = _rec_inputs()

    def _L0_gnn_setup():
        import jax, jax.numpy as jnp
        import numpy as np
        N = 3125
        E = 100000
        F_IN = 512
        H = 128
        key = jax.random.key(seed)
        k0, k1, k2, k3 = jax.random.split(key, 4)
        x = jax.random.normal(k0, (N, F_IN), dtype=jnp.float32)
        edge_index = jax.random.randint(k1, (2, E), 0, N, dtype=jnp.int32)
        edge_weight = jnp.ones((E,), dtype=jnp.float32)
        W_conv = jax.random.normal(k2, (F_IN, H), dtype=jnp.float32) * np.sqrt(2.0 / (F_IN + H)).astype(np.float32)
        b_conv = jnp.zeros((H,), dtype=jnp.float32)
        W_lin = jax.random.normal(k3, (H, F_IN), dtype=jnp.float32) * np.sqrt(2.0 / (H + F_IN)).astype(np.float32)
        b_lin = jnp.zeros((F_IN,), dtype=jnp.float32)
        return {'x': x, 'edge_index': edge_index, 'edge_weight': edge_weight, 'W_conv': W_conv, 'b_conv': b_conv, 'W_lin': W_lin, 'b_lin': b_lin}
    _L0_gnn_all = _L0_gnn_setup()
    _L0_gnn_in = {k: v for k, v in _L0_gnn_all.items() if k in ('W_conv', 'b_conv', 'W_lin', 'b_lin')}
    del _L0_gnn_all

    def _L1_gnn_setup():
        import jax, jax.numpy as jnp
        import numpy as np
        N_NODES = 625
        N_EDGES = 10000
        D_IN = 512
        D_OUT = 512
        key = jax.random.key(seed)
        k_x, k_e, k_wl, k_wr = jax.random.split(key, 4)
        x = jax.random.normal(k_x, (N_NODES, D_IN), dtype=jnp.float32)
        edge_index = jax.random.randint(k_e, (2, N_EDGES), 0, N_NODES, dtype=jnp.int64)
        scale = 1.0 / np.sqrt(D_IN)
        W_l = jax.random.normal(k_wl, (D_IN, D_OUT), dtype=jnp.float32) * scale
        W_r = jax.random.normal(k_wr, (D_IN, D_OUT), dtype=jnp.float32) * scale
        b = jnp.zeros((D_OUT,), dtype=jnp.float32)
        return {'x': x, 'edge_index': edge_index, 'W_l': W_l, 'W_r': W_r, 'b': b}
    _L1_gnn_all = _L1_gnn_setup()
    _L1_gnn_in = {k: v for k, v in _L1_gnn_all.items() if k in ('W_l', 'W_r', 'b')}
    del _L1_gnn_all

    def _L2_gnn_setup():
        import jax, jax.numpy as jnp
        import numpy as np
        N_NODES = 40962
        LATENT_DIM = 512
        N_EDGES = 40962
        NUM_BLOCKS = 4
        NUM_HEADS = 4
        NUM_FREQ = 32
        BASE_PERIOD = 16
        NOISE_EMB_DIM = 16
        EPS = 1e-05

        def _cond_layer_norm(x, cond, sw, sb, bw, bb):
            mu = jnp.mean(x, axis=-1, keepdims=True)
            var = jnp.var(x, axis=-1, keepdims=True)
            xn = (x - mu) * jax.lax.rsqrt(var + EPS)
            scale = cond @ sw + sb
            bias = cond @ bw + bb
            return xn * (1.0 + scale) + bias

        def _sparse_attention(x, src, dst, wq, bq, wk, bk, wv, bv, wo, bo):
            N, D = x.shape
            H, Dh = (NUM_HEADS, D // NUM_HEADS)
            q = (x @ wq + bq).reshape(N, H, Dh) * Dh ** (-0.5)
            k = (x @ wk + bk).reshape(N, H, Dh)
            v = (x @ wv + bv).reshape(N, H, Dh)
            scores = jnp.einsum('ehd,ehd->eh', q[src], k[dst])
            smax = jax.ops.segment_max(scores, src, num_segments=N)
            ex = jnp.exp(scores - smax[src])
            denom = jax.ops.segment_sum(ex, src, num_segments=N)
            attn = ex / denom[src]
            out = jax.ops.segment_sum(attn[:, :, None] * v[dst], src, num_segments=N)
            return out.reshape(N, D) @ wo + bo

        def _forward(x, edge_index, noise_levels, f_w1, f_b1, f_w2, f_b2, s1_w, s1_b, b1_w, b1_b, wq, bq, wk, bk, wv, bv, wo, bo, s2_w, s2_b, b2_w, b2_b, m_w1, m_b1, m_w2, m_b2):
            src, dst = (edge_index[0], edge_index[1])
            freqs = jnp.arange(1, NUM_FREQ + 1, dtype=x.dtype) * (2.0 * np.pi / BASE_PERIOD)
            ph = noise_levels * freqs
            emb = jnp.concatenate([jnp.sin(ph), jnp.cos(ph)], axis=-1)
            cond = jax.nn.silu(emb @ f_w1 + f_b1) @ f_w2 + f_b2
            for i in range(NUM_BLOCKS):
                y = _cond_layer_norm(x, cond, s1_w[i], s1_b[i], b1_w[i], b1_b[i])
                y = _sparse_attention(y, src, dst, wq[i], bq[i], wk[i], bk[i], wv[i], bv[i], wo[i], bo[i])
                x = x + y
                y = _cond_layer_norm(x, cond, s2_w[i], s2_b[i], b2_w[i], b2_b[i])
                y = jax.nn.relu(y @ m_w1[i] + m_b1[i]) @ m_w2[i] + m_b2[i]
                x = x + y
            return x
        key = jax.random.key(seed)
        ks = jax.random.split(key, 20)

        def w(k, shape, s=0.02):
            return jax.random.normal(k, shape, dtype=jnp.float32) * s
        D, B, C = (LATENT_DIM, NUM_BLOCKS, NOISE_EMB_DIM)
        z = lambda *s: jnp.zeros(s, jnp.float32)
        return {'latent_mesh_nodes': jax.random.normal(ks[0], (N_NODES, D), dtype=jnp.float32), 'edge_index': jax.random.randint(ks[1], (2, N_EDGES), 0, N_NODES, dtype=jnp.int32), 'noise_levels': jax.random.uniform(ks[2], (N_NODES, 1), dtype=jnp.float32), 'f_w1': w(ks[3], (2 * NUM_FREQ, C)), 'f_b1': z(C), 'f_w2': w(ks[4], (C, C)), 'f_b2': z(C), 's1_w': w(ks[5], (B, C, D)), 's1_b': z(B, D), 'b1_w': w(ks[6], (B, C, D)), 'b1_b': z(B, D), 'wq': w(ks[7], (B, D, D)), 'bq': z(B, D), 'wk': w(ks[8], (B, D, D)), 'bk': z(B, D), 'wv': w(ks[9], (B, D, D)), 'bv': z(B, D), 'wo': w(ks[10], (B, D, D)), 'bo': z(B, D), 's2_w': w(ks[11], (B, C, D)), 's2_b': z(B, D), 'b2_w': w(ks[12], (B, C, D)), 'b2_b': z(B, D), 'm_w1': w(ks[13], (B, D, D)), 'm_b1': z(B, D), 'm_w2': w(ks[14], (B, D, D)), 'm_b2': z(B, D)}
    _L2_gnn_all = _L2_gnn_setup()
    _L2_gnn_in = {k: v for k, v in _L2_gnn_all.items() if k in ('f_w1', 'f_b1', 'f_w2', 'f_b2', 's1_w', 's1_b', 'b1_w', 'b1_b', 'wq', 'bq', 'wk', 'bk', 'wv', 'bv', 'wo', 'bo', 's2_w', 's2_b', 'b2_w', 'b2_b', 'm_w1', 'm_b1', 'm_w2', 'm_b2')}
    del _L2_gnn_all

    def _L3_gnn_setup():
        import jax, jax.numpy as jnp
        import numpy as np
        N_NODES = 3125
        N_EDGES = 50000
        IN_DIM = 512
        HIDDEN = 512
        HEADS = 4
        C_HEAD = HIDDEN // (2 * HEADS)
        NEG_SLOPE = 0.2
        BN_EPS = 1e-05

        def gat_conv(x, src, dst, W, att_src, att_dst, bias):
            N = x.shape[0]
            h = jnp.einsum('nd,dhc->nhc', x, W)
            a_s = jnp.sum(h * att_src, axis=-1)
            a_d = jnp.sum(h * att_dst, axis=-1)
            e = jax.nn.leaky_relu(a_s[src] + a_d[dst], NEG_SLOPE)
            m = jax.ops.segment_max(e, dst, num_segments=N)
            m = jnp.where(jnp.isfinite(m), m, 0.0)
            ex = jnp.exp(e - m[dst])
            denom = jax.ops.segment_sum(ex, dst, num_segments=N)
            alpha = ex / (denom[dst] + 1e-16)
            out = jax.ops.segment_sum(alpha[:, :, None] * h[src], dst, num_segments=N)
            return out.reshape(N, HEADS * C_HEAD) + bias
        key = jax.random.key(seed)
        ks = jax.random.split(key, 12)
        glorot = lambda k, shape, fan: jax.random.normal(k, shape, jnp.float32) * np.sqrt(2.0 / fan)
        inp = {'x': jax.random.normal(ks[0], (N_NODES, IN_DIM), jnp.float32), 'edge_index': jax.random.randint(ks[1], (2, N_EDGES), 0, N_NODES, dtype=jnp.int32).astype(jnp.int64), 'W_f': glorot(ks[2], (IN_DIM, HEADS, C_HEAD), IN_DIM), 'att_src_f': glorot(ks[3], (HEADS, C_HEAD), C_HEAD), 'att_dst_f': glorot(ks[4], (HEADS, C_HEAD), C_HEAD), 'bias_f': jnp.zeros((HEADS * C_HEAD,), jnp.float32), 'W_b': glorot(ks[5], (IN_DIM, HEADS, C_HEAD), IN_DIM), 'att_src_b': glorot(ks[6], (HEADS, C_HEAD), C_HEAD), 'att_dst_b': glorot(ks[7], (HEADS, C_HEAD), C_HEAD), 'bias_b': jnp.zeros((HEADS * C_HEAD,), jnp.float32), 'W_fuse': glorot(ks[8], (HIDDEN, HIDDEN), HIDDEN), 'b_fuse': jnp.zeros((HIDDEN,), jnp.float32), 'bn_gamma': jnp.ones((HIDDEN,), jnp.float32), 'bn_beta': jnp.zeros((HIDDEN,), jnp.float32)}
        return inp
    _L3_gnn_all = _L3_gnn_setup()
    _L3_gnn_in = {k: v for k, v in _L3_gnn_all.items() if k in ('W_f', 'att_src_f', 'att_dst_f', 'bias_f', 'W_b', 'att_src_b', 'att_dst_b', 'bias_b', 'W_fuse', 'b_fuse', 'bn_gamma', 'bn_beta')}
    del _L3_gnn_all
    return {'x': x, 'src': src, 'dst': dst, 'edge_weight': edge_weight, 'node_vec1': node_vec1, 'L0_gnn_W_conv': _L0_gnn_in['W_conv'], 'L0_gnn_b_conv': _L0_gnn_in['b_conv'], 'L0_gnn_W_lin': _L0_gnn_in['W_lin'], 'L0_gnn_b_lin': _L0_gnn_in['b_lin'], 'L1_gnn_W_l': _L1_gnn_in['W_l'], 'L1_gnn_W_r': _L1_gnn_in['W_r'], 'L1_gnn_b': _L1_gnn_in['b'], 'L2_gnn_f_w1': _L2_gnn_in['f_w1'], 'L2_gnn_f_b1': _L2_gnn_in['f_b1'], 'L2_gnn_f_w2': _L2_gnn_in['f_w2'], 'L2_gnn_f_b2': _L2_gnn_in['f_b2'], 'L2_gnn_s1_w': _L2_gnn_in['s1_w'], 'L2_gnn_s1_b': _L2_gnn_in['s1_b'], 'L2_gnn_b1_w': _L2_gnn_in['b1_w'], 'L2_gnn_b1_b': _L2_gnn_in['b1_b'], 'L2_gnn_wq': _L2_gnn_in['wq'], 'L2_gnn_bq': _L2_gnn_in['bq'], 'L2_gnn_wk': _L2_gnn_in['wk'], 'L2_gnn_bk': _L2_gnn_in['bk'], 'L2_gnn_wv': _L2_gnn_in['wv'], 'L2_gnn_bv': _L2_gnn_in['bv'], 'L2_gnn_wo': _L2_gnn_in['wo'], 'L2_gnn_bo': _L2_gnn_in['bo'], 'L2_gnn_s2_w': _L2_gnn_in['s2_w'], 'L2_gnn_s2_b': _L2_gnn_in['s2_b'], 'L2_gnn_b2_w': _L2_gnn_in['b2_w'], 'L2_gnn_b2_b': _L2_gnn_in['b2_b'], 'L2_gnn_m_w1': _L2_gnn_in['m_w1'], 'L2_gnn_m_b1': _L2_gnn_in['m_b1'], 'L2_gnn_m_w2': _L2_gnn_in['m_w2'], 'L2_gnn_m_b2': _L2_gnn_in['m_b2'], 'L3_gnn_W_f': _L3_gnn_in['W_f'], 'L3_gnn_att_src_f': _L3_gnn_in['att_src_f'], 'L3_gnn_att_dst_f': _L3_gnn_in['att_dst_f'], 'L3_gnn_bias_f': _L3_gnn_in['bias_f'], 'L3_gnn_W_b': _L3_gnn_in['W_b'], 'L3_gnn_att_src_b': _L3_gnn_in['att_src_b'], 'L3_gnn_att_dst_b': _L3_gnn_in['att_dst_b'], 'L3_gnn_bias_b': _L3_gnn_in['bias_b'], 'L3_gnn_W_fuse': _L3_gnn_in['W_fuse'], 'L3_gnn_b_fuse': _L3_gnn_in['b_fuse'], 'L3_gnn_bn_gamma': _L3_gnn_in['bn_gamma'], 'L3_gnn_bn_beta': _L3_gnn_in['bn_beta']}

def reference(x, src, dst, edge_weight, node_vec1, L0_gnn_W_conv, L0_gnn_b_conv, L0_gnn_W_lin, L0_gnn_b_lin, L1_gnn_W_l, L1_gnn_W_r, L1_gnn_b, L2_gnn_f_w1, L2_gnn_f_b1, L2_gnn_f_w2, L2_gnn_f_b2, L2_gnn_s1_w, L2_gnn_s1_b, L2_gnn_b1_w, L2_gnn_b1_b, L2_gnn_wq, L2_gnn_bq, L2_gnn_wk, L2_gnn_bk, L2_gnn_wv, L2_gnn_bv, L2_gnn_wo, L2_gnn_bo, L2_gnn_s2_w, L2_gnn_s2_b, L2_gnn_b2_w, L2_gnn_b2_b, L2_gnn_m_w1, L2_gnn_m_b1, L2_gnn_m_w2, L2_gnn_m_b2, L3_gnn_W_f, L3_gnn_att_src_f, L3_gnn_att_dst_f, L3_gnn_bias_f, L3_gnn_W_b, L3_gnn_att_src_b, L3_gnn_att_dst_b, L3_gnn_bias_b, L3_gnn_W_fuse, L3_gnn_b_fuse, L3_gnn_bn_gamma, L3_gnn_bn_beta):
    import jax
    import jax.numpy as jnp

    def _L0_gnn_ref(x, edge_index, edge_weight, W_conv, b_conv, W_lin, b_lin):
        import jax, jax.numpy as jnp
        import numpy as np
        N = 3125
        E = 100000
        F_IN = 512
        H = 128
        n = x.shape[0]
        src, dst = (edge_index[0], edge_index[1])
        loop = jnp.arange(n, dtype=edge_index.dtype)
        src_f = jnp.concatenate([src, loop])
        dst_f = jnp.concatenate([dst, loop])
        w = jnp.concatenate([edge_weight, jnp.ones((n,), x.dtype)])
        deg = jax.ops.segment_sum(w, dst_f, num_segments=n)
        dinv = jnp.where(deg > 0, jax.lax.rsqrt(deg), 0.0)
        norm = dinv[src_f] * w * dinv[dst_f]
        h = x @ W_conv
        agg = jax.ops.segment_sum(h[src_f] * norm[:, None], dst_f, num_segments=n) + b_conv
        return agg @ W_lin + b_lin

    def _L1_gnn_ref(x, edge_index, W_l, W_r, b):
        import jax, jax.numpy as jnp
        import numpy as np
        N_NODES = 625
        N_EDGES = 10000
        D_IN = 512
        D_OUT = 512
        src = edge_index[0]
        dst = edge_index[1]
        n = x.shape[0]
        msg = x[src]
        agg = jax.ops.segment_sum(msg, dst, num_segments=n)
        deg = jax.ops.segment_sum(jnp.ones((src.shape[0],), x.dtype), dst, num_segments=n)
        mean = agg / jnp.maximum(deg, 1.0)[:, None]
        h = mean @ W_l + b + x @ W_r
        return h * jax.nn.sigmoid(h)

    def _L2_gnn_ref(latent_mesh_nodes, edge_index, noise_levels, f_w1, f_b1, f_w2, f_b2, s1_w, s1_b, b1_w, b1_b, wq, bq, wk, bk, wv, bv, wo, bo, s2_w, s2_b, b2_w, b2_b, m_w1, m_b1, m_w2, m_b2):
        import jax, jax.numpy as jnp
        import numpy as np
        N_NODES = 40962
        LATENT_DIM = 512
        N_EDGES = 40962
        NUM_BLOCKS = 4
        NUM_HEADS = 4
        NUM_FREQ = 32
        BASE_PERIOD = 16
        NOISE_EMB_DIM = 16
        EPS = 1e-05

        def _cond_layer_norm(x, cond, sw, sb, bw, bb):
            mu = jnp.mean(x, axis=-1, keepdims=True)
            var = jnp.var(x, axis=-1, keepdims=True)
            xn = (x - mu) * jax.lax.rsqrt(var + EPS)
            scale = cond @ sw + sb
            bias = cond @ bw + bb
            return xn * (1.0 + scale) + bias

        def _sparse_attention(x, src, dst, wq, bq, wk, bk, wv, bv, wo, bo):
            N, D = x.shape
            H, Dh = (NUM_HEADS, D // NUM_HEADS)
            q = (x @ wq + bq).reshape(N, H, Dh) * Dh ** (-0.5)
            k = (x @ wk + bk).reshape(N, H, Dh)
            v = (x @ wv + bv).reshape(N, H, Dh)
            scores = jnp.einsum('ehd,ehd->eh', q[src], k[dst])
            smax = jax.ops.segment_max(scores, src, num_segments=N)
            ex = jnp.exp(scores - smax[src])
            denom = jax.ops.segment_sum(ex, src, num_segments=N)
            attn = ex / denom[src]
            out = jax.ops.segment_sum(attn[:, :, None] * v[dst], src, num_segments=N)
            return out.reshape(N, D) @ wo + bo

        def _forward(x, edge_index, noise_levels, f_w1, f_b1, f_w2, f_b2, s1_w, s1_b, b1_w, b1_b, wq, bq, wk, bk, wv, bv, wo, bo, s2_w, s2_b, b2_w, b2_b, m_w1, m_b1, m_w2, m_b2):
            src, dst = (edge_index[0], edge_index[1])
            freqs = jnp.arange(1, NUM_FREQ + 1, dtype=x.dtype) * (2.0 * np.pi / BASE_PERIOD)
            ph = noise_levels * freqs
            emb = jnp.concatenate([jnp.sin(ph), jnp.cos(ph)], axis=-1)
            cond = jax.nn.silu(emb @ f_w1 + f_b1) @ f_w2 + f_b2
            for i in range(NUM_BLOCKS):
                y = _cond_layer_norm(x, cond, s1_w[i], s1_b[i], b1_w[i], b1_b[i])
                y = _sparse_attention(y, src, dst, wq[i], bq[i], wk[i], bk[i], wv[i], bv[i], wo[i], bo[i])
                x = x + y
                y = _cond_layer_norm(x, cond, s2_w[i], s2_b[i], b2_w[i], b2_b[i])
                y = jax.nn.relu(y @ m_w1[i] + m_b1[i]) @ m_w2[i] + m_b2[i]
                x = x + y
            return x
        return _forward(latent_mesh_nodes, edge_index, noise_levels, f_w1, f_b1, f_w2, f_b2, s1_w, s1_b, b1_w, b1_b, wq, bq, wk, bk, wv, bv, wo, bo, s2_w, s2_b, b2_w, b2_b, m_w1, m_b1, m_w2, m_b2)

    def _L3_gnn_ref(x, edge_index, W_f, att_src_f, att_dst_f, bias_f, W_b, att_src_b, att_dst_b, bias_b, W_fuse, b_fuse, bn_gamma, bn_beta):
        import jax, jax.numpy as jnp
        import numpy as np
        N_NODES = 3125
        N_EDGES = 50000
        IN_DIM = 512
        HIDDEN = 512
        HEADS = 4
        C_HEAD = HIDDEN // (2 * HEADS)
        NEG_SLOPE = 0.2
        BN_EPS = 1e-05

        def gat_conv(x, src, dst, W, att_src, att_dst, bias):
            N = x.shape[0]
            h = jnp.einsum('nd,dhc->nhc', x, W)
            a_s = jnp.sum(h * att_src, axis=-1)
            a_d = jnp.sum(h * att_dst, axis=-1)
            e = jax.nn.leaky_relu(a_s[src] + a_d[dst], NEG_SLOPE)
            m = jax.ops.segment_max(e, dst, num_segments=N)
            m = jnp.where(jnp.isfinite(m), m, 0.0)
            ex = jnp.exp(e - m[dst])
            denom = jax.ops.segment_sum(ex, dst, num_segments=N)
            alpha = ex / (denom[dst] + 1e-16)
            out = jax.ops.segment_sum(alpha[:, :, None] * h[src], dst, num_segments=N)
            return out.reshape(N, HEADS * C_HEAD) + bias
        src, dst = (edge_index[0], edge_index[1])
        fwd = gat_conv(x, src, dst, W_f, att_src_f, att_dst_f, bias_f)
        bwd = gat_conv(x, dst, src, W_b, att_src_b, att_dst_b, bias_b)
        combined = jnp.concatenate([fwd, bwd], axis=1)
        fused = combined @ W_fuse + b_fuse
        mean = jnp.mean(fused, axis=0)
        var = jnp.mean(jnp.square(fused - mean), axis=0)
        normed = (fused - mean) * jax.lax.rsqrt(var + BN_EPS) * bn_gamma + bn_beta
        return jax.nn.relu(normed)
    edge_index = jnp.stack([src, dst])
    h = jnp.maximum(_layernorm(x, axis=-1), 0.0)
    x = x + _L0_gnn_ref(h, edge_index, edge_weight, L0_gnn_W_conv, L0_gnn_b_conv, L0_gnn_W_lin, L0_gnn_b_lin)
    h = jnp.maximum(_layernorm(x, axis=-1), 0.0)
    x = x + _L1_gnn_ref(h, edge_index, L1_gnn_W_l, L1_gnn_W_r, L1_gnn_b)
    h = jnp.maximum(_layernorm(x, axis=-1), 0.0)
    x = x + _L2_gnn_ref(h, edge_index, node_vec1, L2_gnn_f_w1, L2_gnn_f_b1, L2_gnn_f_w2, L2_gnn_f_b2, L2_gnn_s1_w, L2_gnn_s1_b, L2_gnn_b1_w, L2_gnn_b1_b, L2_gnn_wq, L2_gnn_bq, L2_gnn_wk, L2_gnn_bk, L2_gnn_wv, L2_gnn_bv, L2_gnn_wo, L2_gnn_bo, L2_gnn_s2_w, L2_gnn_s2_b, L2_gnn_b2_w, L2_gnn_b2_b, L2_gnn_m_w1, L2_gnn_m_b1, L2_gnn_m_w2, L2_gnn_m_b2)
    h = jnp.maximum(_layernorm(x, axis=-1), 0.0)
    x = x + _L3_gnn_ref(h, edge_index, L3_gnn_W_f, L3_gnn_att_src_f, L3_gnn_att_dst_f, L3_gnn_bias_f, L3_gnn_W_b, L3_gnn_att_src_b, L3_gnn_att_dst_b, L3_gnn_bias_b, L3_gnn_W_fuse, L3_gnn_b_fuse, L3_gnn_bn_gamma, L3_gnn_bn_beta)
    return x

_drawn_inputs = setup_inputs


def setup_inputs(seed=0):
    import zlib

    import numpy as np

    out = dict(_drawn_inputs(seed))
    spreads = {'L0_gnn_b_conv': (0.0, 0.1),
     'L0_gnn_b_lin': (0.0, 0.1),
     'L1_gnn_b': (0.0, 0.1),
     'L2_gnn_f_b1': (0.0, 0.8),
     'L2_gnn_f_b2': (0.0, 0.8),
     'L2_gnn_s1_b': (0.0, 0.641),
     'L2_gnn_b1_b': (0.0, 0.349),
     'L2_gnn_bq': (0.0, 0.8),
     'L2_gnn_bk': (0.0, 0.8),
     'L2_gnn_bv': (0.0, 0.1),
     'L2_gnn_bo': (0.0, 0.1),
     'L2_gnn_s2_b': (0.0, 0.47),
     'L2_gnn_b2_b': (0.0, 0.476),
     'L2_gnn_m_b1': (0.0, 0.1),
     'L2_gnn_m_b2': (0.0, 0.1),
     'L3_gnn_bias_f': (0.0, 0.8),
     'L3_gnn_bias_b': (0.0, 0.8),
     'L3_gnn_b_fuse': (0.0, 0.8),
     'L3_gnn_bn_gamma': (1.0, 0.2),
     'L3_gnn_bn_beta': (0.0, 0.1)}
    factors = {'node_vec1': 8.0,
     'L2_gnn_f_w1': 8.0,
     'L2_gnn_f_w2': 8.0,
     'L2_gnn_s1_w': 8.0,
     'L2_gnn_b1_w': 8.0,
     'L2_gnn_wq': 7.789,
     'L2_gnn_wk': 7.469,
     'L2_gnn_s2_w': 8.0,
     'L2_gnn_b2_w': 8.0}
    for name, (base, spread) in spreads.items():
        noise = np.random.default_rng([zlib.crc32(name.encode()), seed]).standard_normal(out[name].shape)
        drawn = base * np.exp(spread * noise) if base else spread * noise
        out[name] = jnp.asarray(drawn.astype(out[name].dtype))
    for name, factor in factors.items():
        out[name] = (out[name] * factor).astype(out[name].dtype)
    return out
```

```python
from contextlib import ExitStack

import numpy as np

import concourse.bass as bass
from concourse import mybir

F32 = mybir.dt.float32
F32R = mybir.dt.float32r
BF16 = mybir.dt.bfloat16
F16 = mybir.dt.float16
I32 = mybir.dt.int32
ALU = mybir.AluOpType
ACT = mybir.ActivationFunctionType
AX = mybir.AxisListType

P = 128
N = 625
NT = (N + P - 1) // P
NP = NT * P
TAIL = N - (NT - 1) * P
HALF = NP // 2
D = 512
KT = D // P
E = 20000
GROUP = 512
CH = GROUP // P
NG = (E + GROUP - 1) // GROUP
ELAST = E - (NG - 1) * GROUP
WIN = 64
ACCW = NP + WIN
BLOCKS = 4
HEADS = 4
DH = D // HEADS
L3H = 4
L3C = D // (2 * L3H)
NJ = 2 * L3H
NF = 32
C16 = 16
EPS = 1e-5
NOEDGE = -1e30
RING = 6
STAGE = 2
LAG = 3

PRE_BIG = ["src", "w", "base", "dst", "vec", "z1", "cond"] + [f"l0_{t}" for t in range(NT)]
MID_BIG = ["agg"] + [f"l1_{t}" for t in range(NT)]


def norm_order(ln):
    return [f"c{ln}_0", f"c{ln}_1", f"t{ln}_0", f"c{ln}_2", f"t{ln}_1", f"c{ln}_3", f"t{ln}_2",
            f"c{ln}_4", f"t{ln}_3", f"t{ln}_4"]


def attention_order():
    steps = []
    for k in range(HEADS * NT + LAG):
        if k < HEADS * NT:
            steps.append(("S", k))
        kk = k - LAG
        if kk >= NT and kk % NT == 0:
            steps.append(("PV", kk // NT - 1))
        if kk >= 0:
            steps.append(("T", kk))
    steps.append(("PV", HEADS - 1))
    return steps


ATT = attention_order()
BLOCK_BIG = (norm_order(0) + [f"q{h}" for h in range(HEADS)] + [f"k{h}" for h in range(HEADS)]
             + [f"v{t}" for t in range(NT)] + [f"{a}{b}" for a, b in ATT] + norm_order(1)
             + [f"m{o}" for o in range(KT)])
L3_BIG = ([f"l3_{t}" for t in range(NT)] + [f"mt{t}" for t in range(NT)] + ["as"]
          + [f"am{j}" for j in range(NJ)] + ["vt"]
          + ["vb0"] + sum([[f"vb{j + 1}", f"va{j}"] if j < NJ - 1 else [f"va{j}"] for j in range(NJ)], [])
          + [f"x{k}" for k in range(KT)] + [f"f{o}" for o in range(KT)])
PRE_ROW = ["brow", "deg"] + [f"h{t}" for t in range(NT)] + [f"o{t}" for t in range(NT)]
MID_ROW = [f"z{t}" for t in range(NT)] + sum([[f"r{t}", f"a{t}"] for t in range(NT)], [])
BLOCK_ROW = [f"wo{t}" for t in range(NT)] + [f"m2_{t}" for t in range(NT)]
L3_ROW = [f"H{t}" for t in range(NT)] + [f"P{j}" for j in range(NJ)] + [f"y{t}" for t in range(NT)]

NBIG, NROW = 3, 2
BIG0 = {n: i for i, n in enumerate(PRE_BIG + MID_BIG)}
BIGB = len(BIG0)
BIGBLK = {n: BIGB + i for i, n in enumerate(BLOCK_BIG)}
BIG3 = {n: BIGB + BLOCKS * len(BLOCK_BIG) + i for i, n in enumerate(L3_BIG)}
ROW0 = {n: i for i, n in enumerate(PRE_ROW + MID_ROW)}
ROWB = len(ROW0)
ROWBLK = {n: ROWB + i for i, n in enumerate(BLOCK_ROW)}
ROW3 = {n: ROWB + BLOCKS * len(BLOCK_ROW) + i for i, n in enumerate(L3_ROW)}
assert len(BLOCK_BIG) % NBIG == 0 and len(BLOCK_ROW) % NROW == 0

Q_CONV, Q_LIN, Q_L, Q_R = 0, 1, 2, 2 + KT
RING_BLK = 2 + 2 * KT
PERBLK = 6 * KT
VECS = 3 * BLOCKS * KT + 4 * KT + 1
RING_L3 = RING_BLK + BLOCKS * PERBLK
S_COND = RING_BLK
S_BLK = S_COND + 4
S_PERBLK = PERBLK + 4
S_L3 = S_BLK + BLOCKS * S_PERBLK
assert PERBLK % RING == 0 and S_PERBLK % STAGE == 0
WQ, WK, WV, WO, W1, W2 = (KT * i for i in range(6))
LN_L1, LN_IN, LN_BLK = NT, 2 * NT, 3 * NT
LN_L3 = LN_BLK + NT + BLOCKS * 2 * NT
XN_L3 = LN_BLK + BLOCKS * 2 * NT


def wide(ap640):
    return ap640.rearrange("p (h n) -> p h n", h=2)


def build(nc, a, out):
    ctx = ExitStack()
    with ctx:
        def sb(name, shape, dt):
            return ctx.enter_context(nc.sbuf_tensor(name, shape, dt))

        def sem(name):
            return ctx.enter_context(nc.semaphore(name))

        x = sb("x", [P, NT, D], F32)
        z = sb("z", [P, NT, D], F32)
        arena1 = sb("arena1", [P, 2 * 2 * HEADS * NP], F32R)
        arena2 = sb("arena2", [P, 2 * NT * D], F32R)
        arena3 = sb("arena3", [P, 2 * NT * NP], F32R)
        acc = sb("acc", [P, NT * 2 * ACCW + 40], F32)
        mask = sb("mask", [P, NT, NP], F32)
        ringw = sb("ringw", [P, RING, 2, D], F32R)
        raw = sb("raw", [P, STAGE, D], F32)
        condw = sb("condw", [P, 4, D], F32R)
        condT = sb("condT", [P, NP], F32R)
        bias = sb("bias", [P, 3, D], F32)
        xn = sb("xn", [P, 2, D], F32)
        ident = sb("ident", [P, P], F32)
        ones = sb("ones", [P, P], F32)
        iota16 = sb("iota16", [P, NP], F16)
        src_col = sb("src_col", [P, CH, NG], F32)
        dst_rel = sb("dst_rel", [P, CH, NG], F32)
        w_col = sb("w_col", [P, CH, NG], F32)
        w_part = sb("w_part", [P, 3, CH, NG], BF16)
        hot_dst = sb("hot_dst", [P, 2, CH, 4 * WIN], BF16)
        base_f = sb("base_f", [P, NG], F32)
        base_i = sb("base_i", [1, NG], I32)
        span = sb("span", [P, 2], F32)
        span_i = sb("span_i", [P, 2], I32)
        mnmx = sb("mnmx", [P, 4], F32)
        stats = sb("stats", [P, 2 * NT, 6], F32)
        mv = sb("mv", [P, 2 * NT, 2], F32)
        veps = sb("veps", [P, 2 * NT], F32)
        rstd = sb("rstd", [P, 2 * NT], F32)
        half = sb("half", [P, NT], F32)
        degs = sb("degs", [P, 4, NT], F32)
        rcnt = sb("rcnt", [P, 2, NT], F32)
        flag = sb("flag", [P, 4, NT], F32)
        smax = sb("smax", [P, HEADS * NT], F32)
        nsmax = sb("nsmax", [P, HEADS * NT], F32)
        den = sb("den", [P, HEADS * NT], F32)
        rden = sb("rden", [P, HEADS * NT], F32)
        vec = sb("vec", [VECS, P], F32)
        cols = sb("cols", [P, VECS], F32)
        fcol = sb("fcol", [P, 4], F32)
        f_w1 = sb("f_w1", [2 * NF, C16], F32)
        f_w2 = sb("f_w2", [C16, P], F32)
        l3s = sb("l3s", [P, 5, NT, NJ], F32)
        l3v = sb("l3v", [P, NT, 2 * NJ], F32)
        l3d = sb("l3d", [P, 2, NT], F32)
        bn3 = sb("bn3", [P, KT, 2, 6], F32)
        mv3 = sb("mv3", [P, KT, 2], F32)
        bnc = sb("bnc", [P, 4, KT], F32)

        bqk = cols[:, 0:3 * BLOCKS * KT].rearrange("p (i n) -> p i n", i=3)
        l3col = cols[:, 3 * BLOCKS * KT:VECS - 1].rearrange("p (i n) -> p i n", i=4)
        bconv = cols[:, VECS - 1:VECS]
        freq_i = fcol[0:2 * NF, 0:1].bitcast(I32)
        edge = z
        yT = arena3[:, 0:2 * KT * NP].rearrange("p (s k n) -> p s k n", s=2, k=KT)
        pT = arena3[:, :].rearrange("p (s k n) -> p s k n", s=2, k=NT)
        qT = arena1[:, 0:2 * HEADS * NP].rearrange("p (s k n) -> p s k n", s=2, k=HEADS)
        kT = arena1[:, 2 * HEADS * NP:4 * HEADS * NP].rearrange("p (s k n) -> p s k n", s=2, k=HEADS)
        adj = arena1[:, 0:2 * NT * NP].rearrange("p (s k n) -> p s k n", s=2, k=NT)
        vrow = arena2[:, :].rearrange("p (s k n) -> p s k n", s=2, k=NT)
        h0 = arena2[:, 0:2 * NT * P].rearrange("p (s k n) -> p s k n", s=2, k=NT)
        aT = arena2[:, 2 * NT * P:2 * NT * P + 2 * NP].rearrange("p (s n) -> p s n", s=2)
        bc_hl = arena2[:, 2 * NT * P + 2 * NP:2 * NT * P + 2 * NP + 2 * P].rearrange("p (s n) -> p s n", s=2)
        adjacc = acc[:, 0:NT * 2 * ACCW].rearrange("p (t c n) -> p t c n", t=NT, c=2)
        cnt_acc = adjacc[:, :, 0, 0:NP]
        w_acc = adjacc[:, :, 1, 0:NP]
        hot_src = mask[:, :, :].rearrange("p t n -> p (t n)").bitcast(BF16)[:, 0:2 * CH * NP].rearrange(
            "p (b j n) -> p b j n", b=2, j=CH)
        tmp64 = [mask[0:2 * NF, i, :] for i in range(NT)]
        pbuf = acc[:, 0:4 * NP].rearrange("p (b n) -> p b n", b=4)
        rbuf = acc[:, 4 * NP:6 * NP].rearrange("p (b n) -> p b n", b=2)
        ybuf = acc[:, 6 * NP:6 * NP + 2 * D].rearrange("p (b n) -> p b n", b=2)
        vbuf = acc[:, 6 * NP + 2 * D:6 * NP + 4 * D].rearrange("p (b n) -> p b n", b=2)
        t1 = acc[:, 0:2 * D].rearrange("p (b n) -> p b n", b=2)
        t2 = acc[:, 2 * D:4 * D].rearrange("p (b n) -> p b n", b=2)
        sg = acc[:, 4 * D:6 * D].rearrange("p (b n) -> p b n", b=2)
        maskT = acc[:, 0:NT * NP].rearrange("p (t n) -> p t n", t=NT)
        ebuf = [acc[:, (NT + i) * NP:(NT + i + 1) * NP] for i in range(2)] + [
            xn[:, :, :].rearrange("p b n -> p (b n)")[:, 0:NP]]
        vbrow = [bias[:, :, :].rearrange("p b n -> p (b n)")[:, i * NP:(i + 1) * NP] for i in range(2)]
        l3rows = hot_dst[0:2 * NJ, :, :, :].rearrange("p b j n -> p (b j n)").bitcast(F32)[:, 0:NP]
        Hx = acc[:, NT * NP + 2 * NP:NT * NP + 2 * NP + NT * NJ * (L3C + 1)].rearrange(
            "p (t j c) -> p t j c", t=NT, j=NJ)
        comb = z
        fT = z[:, :, :].rearrange("p t n -> p (t n)").rearrange("p (k n) -> p k n", k=KT)
        combT = yT

        big = [ctx.enter_context(nc.psum_tensor(f"big{i}", [P, 2, D], F32)) for i in range(NBIG)]
        row = [ctx.enter_context(nc.psum_tensor(f"row{i}", [P, D], F32)) for i in range(NROW)]

        def bwide(u):
            return big[u % NBIG][:, :, 0:HALF]

        def bflat(u):
            return big[u % NBIG][:, :, :].rearrange("p h n -> p (h n)")[:, 0:NP]

        def brow(u):
            return row[u % NROW][:, :]

        big_full = sem("big_full")
        big_read = sem("big_read")
        row_full = sem("row_full")
        row_read = sem("row_read")
        raw_ld = [sem(f"raw_ld{i}") for i in range(STAGE)]
        split_done = sem("split_done")
        x_clear = sem("x_clear")
        x_ld = sem("x_ld")
        e_clear = sem("e_clear")
        e_ld = sem("e_ld")
        f_ld = sem("f_ld")
        cb_one = sem("cb_one")
        col_ld = sem("col_ld")
        vec_ld = sem("vec_ld")
        bias_ld = sem("bias_ld")
        const0 = sem("const0")
        const1 = sem("const1")
        dstep = sem("dstep")
        gstep = sem("gstep")
        diag_up = sem("diag_up")
        emb_up = sem("emb_up")
        sin_done = sem("sin_done")
        sig_done = sem("sig_done")
        silu_up = sem("silu_up")
        condT_up = sem("condT_up")
        hot_src_up = sem("hot_src_up")
        hot_dst_up = sem("hot_dst_up")
        hot_w_up = sem("hot_w_up")
        scat_full = sem("scat_full")
        scat_read = sem("scat_read")
        w_ready = sem("w_ready")
        w_up = sem("w_up")
        whi_up = sem("whi_up")
        wlo_up = sem("wlo_up")
        chi_up = sem("chi_up")
        clo_up = sem("clo_up")
        dpow_up = sem("dpow_up")
        dinv_up = sem("dinv_up")
        bconv_up = sem("bconv_up")
        st_up = sem("st_up")
        aggr_up = sem("aggr_up")
        eps_up = sem("eps_up")
        rstd_up = sem("rstd_up")
        xn_up = sem("xn_up")
        z_up = sem("z_up")
        y1_up = sem("y1_up")
        yhi_up = sem("yhi_up")
        h0hi_up = sem("h0hi_up")
        ahi_up = sem("ahi_up")
        zhi_up = sem("zhi_up")
        xb_up = sem("xb_up")
        gate_up = sem("gate_up")
        l1p_up = sem("l1p_up")
        x_up = sem("x_up")
        ln_up = sem("ln_up")
        clamp_up = sem("clamp_up")
        pen_up = sem("pen_up")
        mask_up = sem("mask_up")
        qkhi_up = sem("qkhi_up")
        vhi_up = sem("vhi_up")
        vlo_up = sem("vlo_up")
        nb_up = sem("nb_up")
        exp_up = sem("exp_up")
        rden_up = sem("rden_up")
        pn_up = sem("pn_up")
        phi_up = sem("phi_up")
        ohi_up = sem("ohi_up")
        hhi_up = sem("hhi_up")
        hlo_up = sem("hlo_up")
        shi_up = sem("shi_up")
        clo1_up = sem("clo1_up")
        pass_up = sem("pass_up")
        m3_up = sem("m3_up")
        one_up = sem("one_up")
        hx_up = sem("hx_up")
        prod_up = sem("prod_up")
        att_up = sem("att_up")
        as_up = sem("as_up")
        am_up = sem("am_up")
        v_up = sem("v_up")
        e_up = sem("e_up")
        em_up = sem("em_up")
        p_up = sem("p_up")
        p_used = sem("p_used")
        l3d_up = sem("l3d_up")
        comb_hi_up = sem("comb_hi_up")
        bn_up = sem("bn_up")
        bn_eps_up = sem("bn_eps_up")
        bn_rstd_up = sem("bn_rstd_up")
        sh_up = sem("sh_up")
        fn_up = sem("fn_up")
        stored = sem("stored")

        def ld_count(n):
            dmas = {S_COND + i: 5 for i in range(4)}
            for b in range(BLOCKS):
                dmas |= {S_BLK + b * S_PERBLK + PERBLK + i: 5 for i in range(4)}
            return sum(16 * dmas.get(i, 1) for i in range(n % STAGE, n + 1, STAGE))

        LD_PERBLK = ld_count(S_BLK + S_PERBLK) - ld_count(S_BLK)

        def ringpart(m):
            return ringw[:, m % RING, 0, :], ringw[:, m % RING, 1, :]

        def wait_apart(eng, semaphore, value):
            eng.wait_ge(semaphore, value)
            if not isinstance(value, int):
                eng.nop(nofuse=True)

        block = ctx.enter_context(nc.Block())

        def item_used(eng, n):
            j, st = divmod(n, NT)
            if st < NT - 1:
                eng.wait_ge(p_used, j * (NT - 1) + st + 1)
            else:
                eng.wait_ge(row_full, ROW3[f"P{j}"] + 1)

        def pool_l3(g, rstd_of, split):
            def item(i):
                split(S_L3 + i, ringpart(RING_L3 + i))

            g.wait_ge(row_full, ROWB + BLOCKS * len(BLOCK_ROW))
            item(2)
            for t in range(NT):
                rstd_of(LN_L3 + t, t)
            item(3)
            g.memset(Hx[:, :, :, L3C:L3C + 1], 1.0).then_inc(one_up, 1)
            item(KT)
            item(KT + 1)
            g.wait_ge(row_full, ROW3["H4"] + 1)
            item(KT + 2)
            item(KT + 3)
            for n in range(NJ * NT):
                j, st = divmod(n, NT)
                if st < NT - 1:
                    g.wait_ge(e_up, j * (NT - 1) + st + 1)
                else:
                    g.wait_ge(big_read, BIG3[f"va{j}"] + 1)
                m = mask[:, st, :] if j < L3H else maskT[:, st, :]
                g.tensor_tensor(ebuf[n % 3], ebuf[n % 3], m, ALU.add).then_inc(em_up, 1)
            for o in range(KT):
                g.wait_ge(bn_up, 3 * o + 3)
                g.tensor_scalar(bnc[:, 0, o:o + 1], mv3[:, o, 1:2], EPS, 1.0, ALU.add, ALU.mult).then_inc(bn_eps_up, 1)
                g.wait_ge(bn_eps_up, o + 1)
                g.tensor_tensor(bnc[:, 1, o:o + 1], bnc[:, 0, o:o + 1], half[:, 0:1], ALU.pow).then_inc(bn_rstd_up, 1)

        def act_l3(act, turned_relu):
            act.wait_ge(row_read, ROWB + BLOCKS * len(BLOCK_ROW))
            for i, n in enumerate(("L3_gnn_att_src_", "L3_gnn_att_dst_")):
                for d in range(2):
                    act.dma_start(bias[:, i, d * L3H * L3C:(d + 1) * L3H * L3C],
                                  a[n + "fb"[d]].rearrange("h c -> (h c)").partition_broadcast(P)).then_inc(bias_ld, 16)
            for t in range(NT):
                turned_relu(BIG3[f"l3_{t}"], 0, t)
            for t in range(NT):
                act.wait_ge(row_full, ROW3[f"H{t}"] + 1)
                act.activation(Hx[:, t, :, 0:L3C], brow(ROW3[f"H{t}"]).rearrange("p (j c) -> p j c", j=NJ), ACT.Copy).then_inc(hx_up, 1)
            act.wait_ge(as_up, 2)
            for n in range(NJ * NT):
                j, st = divmod(n, NT)
                act.wait_ge(em_up, n + 1)
                act.activation(ebuf[n % 3], ebuf[n % 3], ACT.Exp, bias=l3s[:, 4, st, j:j + 1]).then_inc(p_up, 1)
            for k in range(KT):
                act.wait_ge(big_full, BIG3[f"x{k}"] + 1)
                act.activation(combT[:, 0, k, :], bflat(BIG3[f"x{k}"]), ACT.Identity, bias=l3col[:, 0, k:k + 1]).then_inc(comb_hi_up, 1)
            for o in range(KT):
                act.wait_ge(sh_up, 3 * o + 3)
                act.activation(fT[:, o, :], fT[:, o, :], ACT.Relu, bias=bnc[:, 3, o:o + 1], scale=bnc[:, 2, o:o + 1]).then_inc(fn_up, 1)

        def pe_l3(pe, turn_norm):
            for t in range(NT):
                turn_norm(BIG3[f"l3_{t}"], XN_L3 + t, t)
            pe.wait_ge(m3_up, NT)
            for t in range(NT):
                u = BIG3[f"mt{t}"]
                free_big(pe, u)
                for st in range(NT):
                    ins = pe.transpose(bflat(u)[:, st * P:(st + 1) * P], mask[:, st, t * P:(t + 1) * P], ident[:, :])
                ins.then_inc(big_full, 1)
            pe.wait_ge(split_done, S_L3 + KT)
            for t in range(NT):
                u = ROW3[f"H{t}"]
                free_row(pe, u)
                pe.wait_ge(big_read, BIG3[f"l3_{t}"] + 1)
                w = L3H * L3C
                for d in range(2):
                    def weight(k):
                        return [r[:, (k % 2) * w:(k % 2 + 1) * w] for r in ringpart(RING_L3 + 2 * d + k // 2)]
                    ins = row_mm(pe, brow(u)[:, d * w:(d + 1) * w], sum([parts(tile_of(yT, k, t), weight(k)) for k in range(KT)], []))
                ins.then_inc(row_full, 1)
            u = BIG3["as"]
            free_big(pe, u)
            pe.wait_ge(att_up, 2 * NT)
            for t in range(NT):
                ins = pe.transpose(bflat(u)[0:NJ, t * P:(t + 1) * P], l3s[:, 0, t, :], ident[:, :])
            ins.then_inc(big_full, 1)
            pe.wait_ge(big_read, u + 1)

            def spread(u, i, n):
                free_big(pe, u)
                wide_mm(pe, u, [(ident[0:n, i:i + 1].broadcast_to([n, P]), l3rows[0:n, :])]).then_inc(big_full, 1)

            for j in range(NJ):
                spread(BIG3[f"am{j}"], j, NJ)
            u = BIG3["vt"]
            free_big(pe, u)
            pe.wait_ge(v_up, 2)
            for t in range(NT):
                ins = pe.transpose(bflat(u)[0:2 * NJ, t * P:(t + 1) * P], l3v[:, t, :], ident[:, :])
            ins.then_inc(big_full, 1)
            pe.wait_ge(big_read, u + 1)
            pe.wait_ge(one_up, 1)
            spread(BIG3["vb0"], NJ, 2 * NJ)
            spread(BIG3["vb1"], NJ + 1, 2 * NJ)
            spread(BIG3["va0"], 0, 2 * NJ)
            for n in range(NJ * NT):
                j, st = divmod(n, NT)
                u = ROW3[f"P{j}"]
                if st == 0:
                    free_row(pe, u)
                pe.wait_ge(p_up, n + 1)
                for dt in range(NT):
                    ins = pe.matmul(brow(u)[:, dt * (L3C + 1):(dt + 1) * (L3C + 1)], ebuf[n % 3][:, dt * P:(dt + 1) * P],
                                    Hx[:, st, j, :], start=(st == 0 and dt == 0), stop=(st == NT - 1), skip_group_check=True)
                ins.then_inc(*((p_used, 1) if st < NT - 1 else (row_full, 1)))
                if st == 1 and j + 2 < NJ:
                    spread(BIG3[f"vb{j + 2}"], NJ + j + 2, 2 * NJ)
                elif st == 2 and j + 1 < NJ:
                    spread(BIG3[f"va{j + 1}"], j + 1, 2 * NJ)
            for k in range(KT):
                u = BIG3[f"x{k}"]
                free_big(pe, u)
                pe.wait_ge(row_read, ROW3[f"P{NJ - 1}"] + 1)
                for t in range(NT):
                    ins = pe.transpose(bflat(u)[:, t * P:(t + 1) * P], comb[:, t, k * P:(k + 1) * P], ident[:, :])
                ins.then_inc(big_full, 1)
            for o in range(KT):
                u = BIG3[f"f{o}"]
                free_big(pe, u)
                pe.wait_ge(big_read, BIG3[f"x{KT - 1}"] + 1)
                pe.wait_ge(split_done, S_L3 + KT + o + 1)
                wide_mm(pe, u, sum([parts(wcol(RING_L3 + KT + o, k), both(combT, k)) for k in range(KT)], [])).then_inc(big_full, 1)
            pe.wait_ge(fn_up, KT)
            for t in range(NT):
                u = ROW3[f"y{t}"]
                free_row(pe, u)
                for o in range(KT):
                    ins = pe.transpose(brow(u)[:, o * P:(o + 1) * P], fT[:, o, t * P:(t + 1) * P], ident[:, :])
                ins.then_inc(row_full, 1)

        def dve_l3(dve, tile_stats, relu_norm, step):
            f32 = lambda ap: ap.bitcast(F32)
            for t in range(NT):
                dve.wait_ge(x_up, NT + t + 1)
                tile_stats(LN_L3 + t, t, x[:, t, :])
            for t in range(NT):
                dve.tensor_scalar(mask[:, t, :], mask[:, t, :], DH ** -0.5, flag[:, 3, t:t + 1], ALU.mult, ALU.add).then_inc(m3_up, 1)
            relu_norm(LN_L3, 0, [BIG3[f"l3_{t}"] for t in range(NT)], 2 * NT + BLOCKS * 2 * NT)
            for t in range(NT):
                u = BIG3[f"mt{t}"]
                dve.wait_ge(big_full, u + 1)
                dve.tensor_copy(maskT[:, t, :], bflat(u)).then_inc(big_read, 1)
            dve.wait_ge(bias_ld, 48 * BLOCKS + 64)
            for t in range(NT):
                u = ROW3[f"H{t}"]
                dve.wait_ge(hx_up, t + 1)
                if t:
                    dve.wait_ge(att_up, 2 * t)
                for i in range(2):
                    dve.tensor_tensor(ebuf[i][:, 0:D], brow(u), bias[:, i, :], ALU.mult).then_inc(*((row_read, 1) if i else (prod_up, 1)))
                dve.wait_ge(prod_up, t + 1)
                dve.wait_ge(row_read, u + 1)
                for i in range(2):
                    dve.tensor_reduce(l3s[:, i, t, :], ebuf[i][:, 0:D].rearrange("p (j c) -> p j c", j=NJ), AX.X, ALU.add).then_inc(att_up, 1)
            dve.wait_ge(att_up, 2 * NT)
            dve.tensor_scalar(l3s[:, 3, :, :], l3s[:, 0, :, :], 0.8, None, ALU.mult).then_inc(as_up, 1)
            dve.tensor_scalar(l3s[:, 4, :, :], l3s[:, 0, :, :], 0.2, None, ALU.mult).then_inc(as_up, 1)
            u = BIG3["as"]
            dve.wait_ge(big_full, u + 1)
            dve.tensor_copy(l3rows[0:NJ, :], bflat(u)[0:NJ, :]).then_inc(big_read, 1)
            for j in range(NJ):
                u = BIG3[f"am{j}"]
                dve.wait_ge(big_full, u + 1)
                if j:
                    dve.wait_ge(big_read, u)
                for t in range(NT):
                    if t >= 3:
                        dve.wait_ge(am_up, j * (NT - 1) + t - 2)
                    m = maskT[:, t, :] if j < L3H else mask[:, t, :]
                    ins = dve.tensor_tensor_reduce(wide(ebuf[t % 3]), bwide(u), wide(m), 1.0, -3e38, ALU.add, ALU.max, l3s[:, 2, t, j:j + 1])
                    ins.then_inc(*((am_up, 1) if t < NT - 1 else (big_read, 1)))
            dve.wait_ge(big_read, BIG3[f"am{NJ - 1}"] + 1)
            step(dve.tensor_tensor(l3s[:, 2, :, :], l3s[:, 2, :, :], l3s[:, 1, :, :], ALU.add))
            step(dve.scalar_tensor_tensor(l3s[:, 2, :, :], l3s[:, 2, :, :], 0.2, l3s[:, 2, :, :], ALU.mult, ALU.max))
            dve.tensor_tensor(l3v[:, :, 0:NJ], l3s[:, 1, :, :], l3s[:, 2, :, :], ALU.subtract).then_inc(v_up, 1)
            dve.scalar_tensor_tensor(l3v[:, :, NJ:2 * NJ], l3s[:, 1, :, :], 0.2, l3s[:, 2, :, :], ALU.mult, ALU.subtract).then_inc(v_up, 1)
            u = BIG3["vt"]
            dve.wait_ge(big_full, u + 1)
            dve.tensor_copy(l3rows[:, :], bflat(u)[0:2 * NJ, :]).then_inc(big_read, 1)

            def combine(j):
                u = ROW3[f"P{j}"]
                dve.wait_ge(row_full, u + 1)
                s = brow(u)[:, 0:NT * (L3C + 1)].rearrange("p (t c) -> p t c", t=NT)
                dve.tensor_scalar(l3d[:, 0, :], s[:, :, L3C], 1e-16, None, ALU.add).then_inc(l3d_up, 1)
                dve.wait_ge(l3d_up, 2 * j + 1)
                dve.reciprocal(l3d[:, 1, :], l3d[:, 0, :]).then_inc(l3d_up, 1)
                dve.wait_ge(l3d_up, 2 * j + 2)
                dve.tensor_tensor(comb[:, :, j * L3C:(j + 1) * L3C], s[:, :, 0:L3C],
                                  l3d[:, 1, :].unsqueeze(2).broadcast_to([P, NT, L3C]), ALU.mult).then_inc(row_read, 1)

            def second_branch(j):
                u = BIG3[f"vb{j}"]
                dve.wait_ge(big_full, u + 1)
                if j >= 2:
                    dve.wait_ge(big_read, BIG3[f"va{j - 2}"] + 1)
                dve.tensor_copy(wide(vbrow[j % 2]), bwide(u)).then_inc(big_read, 1)

            second_branch(0)
            for n in range(NJ * NT):
                j, st = divmod(n, NT)
                u = BIG3[f"va{j}"]
                if st == 0:
                    if j < NJ - 1:
                        second_branch(j + 1)
                    dve.wait_ge(big_full, u + 1)
                    dve.wait_ge(big_read, BIG3[f"vb{j}"] + 1)
                if n >= 3:
                    item_used(dve, n - 3)
                ins = dve.scalar_tensor_tensor(wide(ebuf[n % 3]), bwide(u), l3s[:, 3, st, j:j + 1], wide(vbrow[j % 2]), ALU.add, ALU.max)
                ins.then_inc(*((e_up, 1) if st < NT - 1 else (big_read, 1)))
                if j and st == 3:
                    combine(j - 1)
            combine(NJ - 1)
            for k in range(KT):
                dve.wait_ge(comb_hi_up, k + 1)
                dve.scalar_tensor_tensor(combT[:, 1, k, :], bflat(BIG3[f"x{k}"]), l3col[:, 0, k:k + 1], f32(combT[:, 0, k, :]),
                                         ALU.add, ALU.subtract).then_inc(big_read, 1)
            for o in range(KT):
                u = BIG3[f"f{o}"]
                dve.wait_ge(big_full, u + 1)
                dve.tensor_scalar(wide(fT[:, o, :]), bwide(u), l3col[:, 1, o:o + 1], None, ALU.add).then_inc(big_read, 1)
                dve.wait_ge(big_read, u + 1)
                for i, (lo, hi) in enumerate(((0, HALF), (HALF, N))):
                    dve.bn_stats(bn3[:, o, i, :], fT[:, o, lo:hi]).then_inc(bn_up, 1)
                dve.wait_ge(bn_up, 3 * o + 2)
                dve.bn_aggr(mv3[:, o, :], bn3[:, o, :, :]).then_inc(bn_up, 1)
                dve.wait_ge(bn_up, 3 * o + 3)
                dve.wait_ge(bn_rstd_up, o + 1)
                dve.tensor_tensor(bnc[:, 2, o:o + 1], bnc[:, 1, o:o + 1], l3col[:, 2, o:o + 1], ALU.mult).then_inc(sh_up, 1)
                dve.wait_ge(sh_up, 3 * o + 1)
                dve.tensor_tensor(bnc[:, 3, o:o + 1], mv3[:, o, 0:1], bnc[:, 2, o:o + 1], ALU.mult).then_inc(sh_up, 1)
                dve.wait_ge(sh_up, 3 * o + 2)
                dve.tensor_tensor(bnc[:, 3, o:o + 1], l3col[:, 3, o:o + 1], bnc[:, 3, o:o + 1], ALU.subtract).then_inc(sh_up, 1)
            for t in range(NT):
                u = ROW3[f"y{t}"]
                dve.wait_ge(row_full, u + 1)
                dve.tensor_tensor(x[:, t, :], x[:, t, :], brow(u), ALU.add).then_inc(row_read, 1)

        def finish(sp):
            for t in range(NT):
                sp.wait_ge(row_read, ROW3[f"y{t}"] + 1)
                rows = TAIL if t == NT - 1 else P
                sp.dma_start(out[t * P:t * P + rows, :], x[0:rows, t, :]).then_inc(stored, 16)
            sp.wait_ge(stored, 16 * NT)

        @block.sync
        def _(sp):
            sp.wait_ge(e_clear, 2)
            full = (NG - 1) * GROUP
            for i, lst in enumerate((a["src"], a["dst"], a["edge_weight"])):
                to = edge[:, i, :] if i == 2 else edge[:, i, :].bitcast(I32)
                sp.dma_start(to[0:NG - 1, :], lst[0:full].rearrange("(g e) -> g e", e=GROUP)).then_inc(e_ld, 16)
                sp.dma_start(to[NG - 1:NG, 0:ELAST], lst[full:E].rearrange("(o e) -> o e", o=1)).then_inc(e_ld, 16)
                if i == 1:
                    sp.dma_start(to[NG - 1:NG, ELAST:GROUP],
                                 lst[E - (GROUP - ELAST):E].rearrange("(o e) -> o e", o=1)).then_inc(e_ld, 16)
            sp.wait_ge(x_clear, 1)
            sp.dma_start(x[:, 0:NT - 1, :], a["x"][0:(NT - 1) * P, :].rearrange("(t p) d -> p t d", p=P)).then_inc(x_ld, 16)
            sp.dma_start(x[0:TAIL, NT - 1, :], a["x"][(NT - 1) * P:N, :]).then_inc(x_ld, 16)

            def stage(n, src, it=0):
                if n >= STAGE:
                    sp.wait_ge(split_done, n - STAGE + 1 + it * S_PERBLK)
                to = raw[:, n % STAGE, :]
                if len(src.shape) == 3:
                    to = to.rearrange("p (k c) -> p k c", k=src.shape[1])
                sp.dma_start(to, src).then_inc(raw_ld[n % STAGE], 16)

            def stage_cond(n, w, b, it=0):
                sp.wait_ge(split_done, n - STAGE + 1 + it * S_PERBLK)
                for i in range(4):
                    sp.dma_start(raw[32 * i:32 * i + C16, n % STAGE, :], w).then_inc(raw_ld[n % STAGE], 16)
                sp.dma_start(raw[C16:P:32, n % STAGE, :], b.unsqueeze(0).broadcast_to([4, D])).then_inc(raw_ld[n % STAGE], 16)

            def columns(w, h):
                return w[:, h * P:(h + 1) * P].rearrange("(k p) c -> p k c", p=P)

            conds = [(a["L2_gnn_s1_w"], a["L2_gnn_s1_b"]), (a["L2_gnn_b1_w"], a["L2_gnn_b1_b"]),
                     (a["L2_gnn_s2_w"], a["L2_gnn_s2_b"]), (a["L2_gnn_b2_w"], a["L2_gnn_b2_b"])]
            by_col = {WQ: a["L2_gnn_wq"], WK: a["L2_gnn_wk"], W1: a["L2_gnn_m_w1"]}
            by_row = {WV: a["L2_gnn_wv"], WO: a["L2_gnn_wo"], W2: a["L2_gnn_m_w2"]}

            stage(Q_CONV, columns(a["L0_gnn_W_conv"], 0))
            stage(Q_LIN, a["L0_gnn_W_lin"])
            for k in range(KT):
                stage(Q_L + k, a["L1_gnn_W_l"][k * P:(k + 1) * P, :])
            for k in range(KT):
                stage(Q_R + k, a["L1_gnn_W_r"][k * P:(k + 1) * P, :])
            with sp.Fori(0, BLOCKS) as it:
                for i, (w, b) in enumerate(conds):
                    stage_cond(S_COND + i, w[it], b[it], it)
                for q in (WQ, WK, WV, WO, W1, W2):
                    for i in range(KT):
                        src = columns(by_col[q][it], i) if q in by_col else by_row[q][it][i * P:(i + 1) * P, :]
                        stage(S_BLK + q + i, src, it)
            for i, (w, b) in enumerate(conds):
                stage_cond(S_L3 - 4 + i, w[BLOCKS - 1], b[BLOCKS - 1])
            for i, w in enumerate((a["L3_gnn_W_f"], a["L3_gnn_W_b"])):
                for j in range(2):
                    stage(S_L3 + 2 * i + j, w[2 * j * P:2 * (j + 1) * P].rearrange("(k p) h c -> p k (h c)", p=P))
            for i in range(KT):
                stage(S_L3 + KT + i, columns(a["L3_gnn_W_fuse"], i))
            finish(sp)

        def pool_l2(g, rstd_of, split, split_cond):
            for i in range(4):
                split_cond(S_COND + i, i, i)
            for t in range(NT):
                rstd_of(LN_IN + t, t)
            for i in range(2):
                g.wait_ge(row_full, ROW0["z4"] + 1)
                split(S_BLK + i, ringpart(RING_BLK + i))
            for t in range(NT):
                rstd_of(LN_BLK + t, NT + t)
            with g.Fori(0, BLOCKS) as it:
                nb, nr = it * len(BLOCK_BIG), it * len(BLOCK_ROW)

                def quarters(q, first, last, used, v):
                    g.wait_ge(used, v)
                    for i in range(first, last):
                        split(S_BLK + q + i, ringpart(RING_BLK + q + i), it)

                quarters(WQ, 2, KT, row_full, ROWB + nr)
                quarters(WK, 0, 2, row_full, ROWB + nr)
                g.wait_ge(bias_ld, 48 * it + 48)
                for t in range(NT):
                    g.wait_ge(xn_up, LN_BLK + it * 2 * NT + t + 1)
                    g.tensor_tensor(z[:, t, :], z[:, t, :], bias[:, 1, :], ALU.add).then_inc(xb_up, 1)
                quarters(WK, 2, 3, big_full, BIGBLK["q0"] + nb + 1)
                quarters(WK, 3, 4, big_full, BIGBLK["q1"] + nb + 1)
                quarters(WV, 0, 1, big_full, BIGBLK["q2"] + nb + 1)
                quarters(WV, 1, 2, big_full, BIGBLK["q3"] + nb + 1)
                quarters(WV, 2, 3, big_full, BIGBLK["k0"] + nb + 1)
                quarters(WV, 3, 4, big_full, BIGBLK["k1"] + nb + 1)
                quarters(WO, 0, 1, big_full, BIGBLK["k2"] + nb + 1)
                quarters(WO, 1, 2, big_full, BIGBLK["k3"] + nb + 1)
                for t in range(NT):
                    g.wait_ge(vhi_up, it * NT + t + 1)
                    g.tensor_tensor(vrow[:, 1, t, :], vbuf[:, t % 2, :], vrow[:, 0, t, :].bitcast(F32), ALU.subtract).then_inc(vlo_up, 1)
                for k in range(HEADS * NT):
                    wait_apart(g, rden_up, it * HEADS * NT + k + 1)
                    g.tensor_scalar(pbuf[:, k % 4, :], pbuf[:, k % 4, :], rden[:, k:k + 1], flag[:, 1, k % NT:k % NT + 1],
                                    ALU.mult, ALU.mult).then_inc(pn_up, 1)
                    if k in (4, 6, 8, 10):
                        i = (k - 4) // 2
                        quarters(WO if i < 2 else W1, (i + 2) % KT, (i + 2) % KT + 1, big_full, BIGBLK["v4"] + nb + 1)
                for t in range(NT):
                    rstd_of(LN_BLK + it * 2 * NT + NT + t, t)
                quarters(W1, 2, 4, row_full, ROWBLK["wo4"] + nr + 1)
                for t in range(NT):
                    g.wait_ge(xn_up, LN_BLK + it * 2 * NT + NT + t + 1)
                    g.tensor_tensor(z[:, t, :], z[:, t, :], bias[:, 2, :], ALU.add).then_inc(xb_up, 1)
                quarters(W2, 0, 2, row_full, ROWBLK["wo4"] + nr + 1)
                for o in range(KT):
                    g.wait_ge(hhi_up, it * KT + o + 1)
                    g.tensor_tensor(kT[:, 1, o, :], rbuf[:, o % 2, :], kT[:, 0, o, :].bitcast(F32), ALU.subtract).then_inc(hlo_up, 1)
                    if o < 2:
                        quarters(W2, 2 + o, 3 + o, big_full, BIGBLK[f"m{o}"] + nb + 1)
                for i in range(4):
                    split_cond(S_BLK + PERBLK + i, i, 4 + i, it)
                    rstd_of(LN_BLK + (it + 1) * 2 * NT + i, NT + i)
                for i in range(2):
                    g.wait_ge(big_full, BIGBLK["m3"] + nb + 1)
                    split(S_BLK + S_PERBLK + i, ringpart(RING_BLK + i), it)
                rstd_of(LN_BLK + (it + 1) * 2 * NT + NT - 1, 2 * NT - 1)

        @block.gpsimd
        def _(g):
            own = [0]

            def step(ins):
                own[0] += 1
                ins.then_inc(gstep, 1)
                g.wait_ge(gstep, own[0])

            step(g.memset(ident[:, :], 0.0))
            g.affine_select(out=ident[:, :], in_=ident[:, :], compare_op=ALU.not_equal, fill=1.0, base=0,
                            pattern=[[-1, P]], channel_multiplier=1).then_inc(const0, 1)
            g.memset(ones[:, :], 1.0).then_inc(const0, 1)
            step(g.memset(half[:, :], -0.5))
            g.iota(iota16[:, :], [[1, NP]], base=0, channel_multiplier=0,
                   allow_small_or_imprecise_dtypes=True).then_inc(const0, 1)
            step(g.memset(fcol[:, :], 0.0))
            g.iota(fcol[0:NF, 0:1].bitcast(I32), [[1, 1]], base=1, channel_multiplier=1).then_inc(const1, 1)
            g.wait_ge(const1, 1)
            g.iota(fcol[NF:2 * NF, 0:1].bitcast(I32), [[1, 1]], base=1, channel_multiplier=1).then_inc(const1, 1)
            g.wait_ge(const1, 2)
            g.memset(tmp64[0][:, N:NP], 0.0).then_inc(const1, 1)
            g.wait_ge(const1, 3)
            step(g.memset(f_w2[:, :], 0.0))
            v0 = 0
            for b in ("bq", "bk", "m_b1"):
                g.dma_start(vec[v0:v0 + BLOCKS * KT, :], a["L2_gnn_" + b].rearrange("b (k p) -> (b k) p", p=P)).then_inc(vec_ld, 16)
                v0 += BLOCKS * KT
            for b in ("L3_gnn_bias_f", "L3_gnn_bias_b", "L3_gnn_b_fuse", "L3_gnn_bn_gamma", "L3_gnn_bn_beta", "L0_gnn_b_conv"):
                v = a[b].rearrange("(k p) -> k p", p=P)
                g.dma_start(vec[v0:v0 + v.shape[0], :], v).then_inc(vec_ld, 16)
                v0 += v.shape[0]
            assert v0 == VECS
            g.dma_start(tmp64[0][:, 0:N], a["node_vec1"].rearrange("n o -> o n").broadcast_to([2 * NF, N])).then_inc(f_ld, 16)
            g.dma_start(f_w1[:, :], a["L2_gnn_f_w1"]).then_inc(f_ld, 16)
            g.dma_start(fcol[0:C16, 3:4], a["L2_gnn_f_b1"].unsqueeze(1)).then_inc(f_ld, 16)
            for i in range(4):
                g.dma_start(f_w2[:, 32 * i:32 * i + C16], a["L2_gnn_f_w2"]).then_inc(f_ld, 16)
                g.dma_start(fcol[32 * i:32 * i + C16, 2:3], a["L2_gnn_f_b2"].unsqueeze(1)).then_inc(f_ld, 16)
            F_LOADS = 3 + 8
            g.wait_ge(f_ld, 16 * F_LOADS)
            for i in range(4):
                if i:
                    g.wait_ge(cb_one, i)
                g.affine_select(out=fcol[:, 2:3], in_=fcol[:, 2:3], compare_op=ALU.not_equal, fill=1.0,
                                base=-(32 * i + C16), pattern=[[0, 1]], channel_multiplier=1).then_inc(cb_one, 1)
            g.dma_start(bias[:, 0, :], a["L0_gnn_b_lin"].partition_broadcast(P)).then_inc(col_ld, 16)
            g.dma_start(bias[:, 1, :], a["L1_gnn_b"].partition_broadcast(P)).then_inc(col_ld, 16)

            def rstd_of(i, slot):
                wait_apart(g, aggr_up, i + 1)
                g.tensor_scalar(veps[:, slot:slot + 1], mv[:, slot, 1:2], EPS, 1.0, ALU.add, ALU.mult).then_inc(eps_up, 1)
                g.wait_ge(eps_up, i + 1)
                g.tensor_tensor(rstd[:, slot:slot + 1], veps[:, slot:slot + 1], half[:, 0:1], ALU.pow).then_inc(rstd_up, 1)

            def split(n, to, it=0):
                r = raw[:, n % STAGE, :]
                wait_apart(g, raw_ld[n % STAGE], ld_count(n) + it * LD_PERBLK)
                g.tensor_copy(to[0], r).then_inc(shi_up, 1)
                g.wait_ge(shi_up, n + 1 + it * S_PERBLK)
                g.tensor_tensor(to[1], r, to[0].bitcast(F32), ALU.subtract).then_inc(split_done, 1)

            def split_cond(n, kind, nth, it=0):
                r = raw[:, n % STAGE, :]
                to = condw[:, kind, :]
                wait_apart(g, raw_ld[n % STAGE], ld_count(n) + it * LD_PERBLK)
                g.tensor_copy(to, r).then_inc(shi_up, 1)
                g.wait_ge(shi_up, n + 1 + it * S_PERBLK)
                for lo in (32, 96):
                    ins = g.tensor_tensor(to[lo:lo + 32, :], r[lo:lo + 32, :], to[lo:lo + 32, :].bitcast(F32), ALU.subtract)
                    if lo == 32:
                        ins.then_inc(clo1_up, 1)
                        g.wait_ge(clo1_up, nth + 1 + it * 4)
                ins.then_inc(split_done, 1)
                g.wait_ge(split_done, n + 1 + it * S_PERBLK)

            for t in range(NT):
                rstd_of(t, t)
            for m in range(RING):
                split(m, ringpart(m))
            g.wait_ge(w_ready, 2)
            passes = g.value_load(span_i[0:1, 1:2], min_val=0, max_val=NP // WIN)
            with g.Fori(0, passes + 1) as kp:
                with g.Fori(0, NG // 2) as gi:
                    for b in range(2):
                        gr = gi * 2 + b
                        c = kp * NG + gr + 1
                        hot = hot_dst[:, b, :, 0:WIN]
                        g.wait_ge(hot_dst_up, c)
                        for i in range(3):
                            ins = g.tensor_tensor(
                                hot_dst[:, b, :, (i + 1) * WIN:(i + 2) * WIN], hot,
                                w_part[:, i, :, bass.ds(gr, 1)].broadcast_to([P, CH, WIN]), ALU.mult)
                        ins.then_inc(hot_w_up, 1)
            g.wait_ge(w_up, 3)
            g.tensor_tensor(degs[:, 2, :], degs[:, 1, :], half[:, :], ALU.pow).then_inc(dpow_up, 1)
            for t in range(NT):
                g.wait_ge(xn_up, t + 1)
                g.wait_ge(row_read, ROW0["brow"] + 1)
                g.tensor_tensor(x[:, t, :], x[:, t, :], bias[:, 0, :], ALU.add).then_inc(xb_up, 1)
            for t in range(NT):
                rstd_of(LN_L1 + t, NT + t)
            for m, used, v in ((6, row_full, ROW0["h4"]), (7, row_full, ROW0["o4"]), (8, row_full, ROW0["z4"]), (9, row_full, ROW0["z4"])):
                g.wait_ge(used, v + 1)
                split(m, ringpart(m))
            pool_l2(g, rstd_of, split, split_cond)
            pool_l3(g, rstd_of, split)

        def act_l2(act):
            with act.Fori(0, BLOCKS) as it:
                nb, nr = it * len(BLOCK_BIG), it * len(BLOCK_ROW)
                act.wait_ge(row_read, ROWB + nr)
                for i, b in enumerate(("bv", "bo", "m_b2")):
                    act.dma_start(bias[:, i, :], a["L2_gnn_" + b][it].partition_broadcast(P)).then_inc(bias_ld, 16)

                def turned(ln):
                    for t in range(NT):
                        u = BIGBLK[f"t{ln}_{t}"]
                        act.wait_ge(big_full, u + nb + 1)
                        act.activation(yT[:, 0, :, t * P:(t + 1) * P], bflat(u)[:, 0:D].rearrange("p (k n) -> p k n", k=KT),
                                       ACT.Copy).then_inc(yhi_up, 1)

                turned(0)
                for i, to in enumerate((qT, kT)):
                    for h in range(HEADS):
                        u = BIGBLK["qk"[i] + str(h)]
                        act.wait_ge(big_full, u + nb + 1)
                        act.activation(wide(to[:, 0, h, :]), bwide(u), ACT.Identity,
                                       bias=bqk[:, i, bass.ds(it * KT + h, 1)]).then_inc(qkhi_up, 1)
                for t in range(NT):
                    act.wait_ge(big_read, BIGBLK[f"v{t}"] + nb + 1)
                    act.activation(vrow[:, 0, t, :], vbuf[:, t % 2, :], ACT.Copy).then_inc(vhi_up, 1)
                for what, k in ATT:
                    if what == "S":
                        act.wait_ge(nb_up, it * HEADS * NT + k + 1)
                        act.activation(pbuf[:, k % 4, :], pbuf[:, k % 4, :], ACT.Exp, bias=nsmax[:, k:k + 1],
                                       scale=DH ** -0.5, accum_out=den[:, k:k + 1]).then_inc(exp_up, 1)
                    elif what == "T":
                        u = BIGBLK[f"T{k}"]
                        act.wait_ge(big_full, u + nb + 1)
                        act.activation(pT[:, 0, :, (k % NT) * P:(k % NT + 1) * P], bflat(u).rearrange("p (k n) -> p k n", k=NT),
                                       ACT.Copy).then_inc(phi_up, 1)
                    else:
                        u = BIGBLK[f"PV{k}"]
                        act.wait_ge(big_full, u + nb + 1)
                        act.activation(wide(qT[:, 0, k, :]), bwide(u), ACT.Copy).then_inc(ohi_up, 1)
                turned(1)
                for o in range(KT):
                    act.wait_ge(big_read, BIGBLK[f"m{o}"] + nb + 1)
                    act.activation(kT[:, 0, o, :], rbuf[:, o % 2, :], ACT.Copy).then_inc(hhi_up, 1)

        @block.scalar
        def _(act):
            act.wait_ge(emb_up, 1)
            act.activation(tmp64[4], tmp64[3], ACT.Sin).then_inc(sin_done, 1)
            act.wait_ge(big_read, BIG0["z1"] + 1)
            act.activation(mask[0:C16, 2, :], mask[0:C16, 1, :], ACT.Sigmoid).then_inc(sig_done, 1)

            def turned_relu(u, i, t):
                act.wait_ge(big_full, u + 1)
                act.activation(yT[:, 0, :, t * P:(t + 1) * P], bflat(u)[:, 0:D].rearrange("p (k n) -> p k n", k=KT),
                               ACT.Relu).then_inc(yhi_up, 1)

            for t in range(NT):
                turned_relu(BIG0[f"l0_{t}"], t, t)
            act.wait_ge(diag_up, NT)
            for t in range(NT):
                act.activation(adj[:, 0, t, :], w_acc[:, t, :], ACT.Copy).then_inc(whi_up, 1)
            act.wait_ge(dinv_up, 1)
            for t in range(NT):
                act.wait_ge(row_full, ROW0[f"h{t}"] + 1)
                act.activation(h0[:, 0, t, :], brow(ROW0[f"h{t}"])[:, 0:P], ACT.Copy, scale=degs[:, 3, t:t + 1]).then_inc(h0hi_up, 1)
            act.wait_ge(big_full, BIG0["agg"] + 1)
            act.activation(wide(aT[:, 0, :]), bwide(BIG0["agg"]), ACT.Copy).then_inc(ahi_up, 1)
            for t in range(NT):
                act.activation(adj[:, 0, t, :], cnt_acc[:, t, :], ACT.Copy).then_inc(chi_up, 1)
            for t in range(NT):
                turned_relu(BIG0[f"l1_{t}"], NT + t, t)
            act.wait_ge(clamp_up, 1)
            act.activation(mask[:, :, :], mask[:, :, :], ACT.Ln).then_inc(ln_up, 1)
            for t in range(NT):
                act.wait_ge(row_full, ROW0[f"z{t}"] + 1)
                act.activation(vrow[:, 0, t, :], brow(ROW0[f"z{t}"]), ACT.Copy).then_inc(zhi_up, 1)
            for t in range(NT):
                act.wait_ge(row_read, ROW0[f"a{t}"] + 1)
                if t >= 2:
                    act.wait_ge(l1p_up, t - 1)
                act.activation(sg[:, t % 2, :], t2[:, t % 2, :], ACT.Sigmoid).then_inc(gate_up, 1)
            act_l2(act)
            act_l3(act, turned_relu)

        def wide_mm(pe, u, terms):
            for i, (l, r) in enumerate(terms):
                for h in range(2):
                    ins = pe.matmul(big[u % NBIG][:, h, 0:HALF], l, r[:, h * HALF:(h + 1) * HALF],
                                    start=(i == 0), stop=(i == len(terms) - 1))
            return ins

        def row_mm(pe, to, terms):
            for i, (l, r) in enumerate(terms):
                ins = pe.matmul(to, l, r, start=(i == 0), stop=(i == len(terms) - 1))
            return ins

        def parts(l, r):
            return [(l[0], r[0]), (l[0], r[1]), (l[1], r[0])]

        def free_big(pe, u, it=0):
            if u >= NBIG:
                pe.wait_ge(big_read, u - NBIG + 1 + it)

        def free_row(pe, u, it=0):
            if u >= NROW:
                pe.wait_ge(row_read, u - NROW + 1 + it)

        def turn(pe, u, src, n):
            for k in range(n):
                ins = pe.transpose(bflat(u)[:, k * P:(k + 1) * P], src[:, k * P:(k + 1) * P], ident[:, :])
            return ins

        def wcol(m, k):
            return [w[:, k * P:(k + 1) * P] for w in ringpart(m)]

        def tile_of(t2, k, t):
            return [t2[:, s, k, t * P:(t + 1) * P] for s in range(2)]

        def both(t2, k):
            return [t2[:, s, k, :] for s in range(2)]

        def pe_l2(pe):
            pe.wait_ge(condT_up, 2)
            with pe.Fori(0, BLOCKS) as it:
                nb, nr, ns = it * len(BLOCK_BIG), it * len(BLOCK_ROW), it * S_PERBLK

                def cond(ln, t):
                    u = BIGBLK[f"c{ln}_{t}"]
                    free_big(pe, u, nb)
                    if t == 0:
                        pe.wait_ge(split_done, S_COND + 2 * ln + 2 + ns)
                    for i in range(2):
                        ins = pe.matmul(big[u % NBIG][:, i, :], condT[:, t * P:(t + 1) * P], condw[:, 2 * ln + i, :], start=True, stop=True)
                    ins.then_inc(big_full, 1)

                def turn_y(ln, t):
                    u = BIGBLK[f"t{ln}_{t}"]
                    free_big(pe, u, nb)
                    pe.wait_ge(big_read, BIGBLK[f"c{ln}_{t}"] + nb + 1)
                    turn(pe, u, ybuf[:, t % 2, :], KT).then_inc(big_full, 1)

                for n in norm_order(0):
                    (cond if n[0] == "c" else turn_y)(0, int(n[3]))
                pe.wait_ge(big_read, BIGBLK["t0_4"] + nb + 1)
                for i in range(2):
                    for h in range(HEADS):
                        u = BIGBLK["qk"[i] + str(h)]
                        free_big(pe, u, nb)
                        q = (WQ, WK)[i] + h
                        pe.wait_ge(split_done, S_BLK + q + 1 + ns)
                        wide_mm(pe, u, sum([parts(wcol(RING_BLK + q, k), both(yT, k)) for k in range(KT)], [])).then_inc(big_full, 1)
                pe.wait_ge(split_done, S_BLK + WV + KT + ns)
                for t in range(NT):
                    u = BIGBLK[f"v{t}"]
                    free_big(pe, u, nb)
                    row_mm(pe, big[u % NBIG][:, 0, :], sum([parts(tile_of(yT, k, t), ringpart(RING_BLK + WV + k)) for k in range(KT)], [])).then_inc(big_full, 1)
                for what, k in ATT:
                    u = BIGBLK[f"{what}{k}"]
                    free_big(pe, u, nb)
                    if what == "S":
                        h, t = k // NT, k % NT
                        pe.wait_ge(big_read, BIGBLK[f"k{h}"] + nb + 1)
                        wide_mm(pe, u, parts(tile_of(qT, h, t), both(kT, h))).then_inc(big_full, 1)
                    elif what == "T":
                        pe.wait_ge(pn_up, it * HEADS * NT + k + 1)
                        turn(pe, u, pbuf[:, k % 4, :], NT).then_inc(big_full, 1)
                    else:
                        pe.wait_ge(big_read, BIGBLK[f"T{k * NT + NT - 1}"] + nb + 1)
                        pe.wait_ge(vlo_up, (it + 1) * NT)
                        wide_mm(pe, u, sum([parts([vrow[:, s, st, k * DH:(k + 1) * DH] for s in range(2)], both(pT, st))
                                            for st in range(NT)], [])).then_inc(big_full, 1)
                pe.wait_ge(big_read, BIGBLK["PV3"] + nb + 1)
                pe.wait_ge(split_done, S_BLK + WO + KT + ns)

                def out_row(t):
                    u = ROWBLK[f"wo{t}"]
                    free_row(pe, u, nr)
                    row_mm(pe, brow(u)[:, :], sum([parts(tile_of(qT, h, t), ringpart(RING_BLK + WO + h)) for h in range(HEADS)], [])).then_inc(row_full, 1)

                rows = 0
                for n in norm_order(1):
                    if rows < NT and n[0] == "c":
                        out_row(rows)
                        rows += 1
                    (cond if n[0] == "c" else turn_y)(1, int(n[3]))
                pe.wait_ge(big_read, BIGBLK["t1_4"] + nb + 1)
                for o in range(KT):
                    u = BIGBLK[f"m{o}"]
                    free_big(pe, u, nb)
                    pe.wait_ge(split_done, S_BLK + W1 + o + 1 + ns)
                    wide_mm(pe, u, sum([parts(wcol(RING_BLK + W1 + o, k), both(yT, k)) for k in range(KT)], [])).then_inc(big_full, 1)
                pe.wait_ge(hlo_up, (it + 1) * KT)
                pe.wait_ge(split_done, S_BLK + W2 + KT + ns)
                for t in range(NT):
                    u = ROWBLK[f"m2_{t}"]
                    free_row(pe, u, nr)
                    row_mm(pe, brow(u)[:, :], sum([parts(tile_of(kT, k, t), ringpart(RING_BLK + W2 + k)) for k in range(KT)], [])).then_inc(row_full, 1)

        @block.tensor
        def _(pe):
            pe.wait_ge(const0, 3)
            pe.wait_ge(dstep, 5)
            for name, i in (("src", 3), ("w", 2)):
                u = BIG0[name]
                for j in range(CH):
                    ins = pe.transpose(bflat(u)[:, j * NG:(j + 1) * NG], edge[0:NG, i, j * P:(j + 1) * P], ident[0:NG, 0:NG])
                ins.then_inc(big_full, 1)
            pe.wait_ge(dstep, 7)
            pe.matmul(bflat(BIG0["base"])[:, 0:2 * NG], ones[0:NG, :], xn[0:NG, 0, 0:2 * NG],
                      start=True, stop=True).then_inc(big_full, 1)
            u = BIG0["dst"]
            free_big(pe, u)
            for j in range(CH):
                ins = pe.transpose(bflat(u)[:, j * NG:(j + 1) * NG], edge[0:NG, 4, j * P:(j + 1) * P], ident[0:NG, 0:NG])
            ins.then_inc(big_full, 1)
            u = BIG0["vec"]
            free_big(pe, u)
            pe.wait_ge(vec_ld, 16 * 9)
            pe.transpose(bflat(u)[:, 0:VECS], vec[:, :], ident[0:VECS, 0:VECS]).then_inc(big_full, 1)
            u = BIG0["z1"]
            free_big(pe, u)
            pe.wait_ge(sin_done, 1)
            pe.wait_ge(f_ld, 16 * 11)
            for h in range(2):
                ins = pe.matmul(big[u % NBIG][0:C16, h, 0:HALF], f_w1[:, :], tmp64[4][:, h * HALF:(h + 1) * HALF], start=True, stop=True)
            ins.then_inc(big_full, 1)
            u = BIG0["cond"]
            free_big(pe, u)
            pe.wait_ge(silu_up, 1)
            wide_mm(pe, u, [(f_w2[:, :], mask[0:C16, 3, :])]).then_inc(big_full, 1)

            def turn_norm(u, i, t):
                free_big(pe, u)
                pe.wait_ge(xn_up, i + 1)
                turn(pe, u, xn[:, t % 2, :], KT).then_inc(big_full, 1)

            for t in range(NT):
                turn_norm(BIG0[f"l0_{t}"], t, t)
            pe.wait_ge(big_read, len(PRE_BIG))
            pe.wait_ge(w_ready, 2)
            passes = pe.value_load(span_i[0:1, 1:2], min_val=0, max_val=NP // WIN)
            with pe.Fori(0, passes + 1) as kp:
                with pe.Fori(0, NG // 2) as gi:
                    for b in range(2):
                        c = kp * NG + gi * 2 + b + 1
                        to = bflat(b)
                        pe.wait_ge(hot_src_up, c)
                        pe.wait_ge(hot_w_up, c)
                        pe.wait_ge(scat_read, c)
                        for j in range(CH):
                            for t in range(NT):
                                s = hot_src[:, b, j, t * P:(t + 1) * P]
                                o = t * 2 * WIN
                                pe.matmul(to[:, o:o + 2 * WIN], s, hot_dst[:, b, j, 0:2 * WIN],
                                          start=(j == 0 and t in (0, 4)), stop=False, skip_group_check=True)
                                for i in (2, 3):
                                    ins = pe.matmul(to[:, o + WIN:o + 2 * WIN], s, hot_dst[:, b, j, i * WIN:(i + 1) * WIN],
                                                    start=False, stop=(j == CH - 1 and i == 3), skip_group_check=True)
                        ins.then_inc(scat_full, 1)
            pe.wait_ge(bconv_up, 1)
            pe.wait_ge(split_done, Q_LIN + 1)
            row_mm(pe, brow(ROW0["brow"])[:, :], parts([bc_hl[:, 0, :], bc_hl[:, 1, :]], ringpart(Q_LIN))).then_inc(row_full, 1)
            pe.wait_ge(diag_up, NT)
            to = brow(ROW0["deg"])
            for dt in range(NT):
                for i, m in ((0, w_acc), (1, cnt_acc)):
                    for st in range(NT):
                        ins = pe.matmul(to[:, i * NT + dt:i * NT + dt + 1], m[:, st, dt * P:(dt + 1) * P], ones[:, 0:1],
                                        start=(st == 0), stop=(st == NT - 1))
            ins.then_inc(row_full, 1)
            for t in range(NT):
                u = ROW0[f"h{t}"]
                free_row(pe, u)
                row_mm(pe, brow(u)[:, 0:P], sum([parts(tile_of(yT, k, t), wcol(Q_CONV, k)) for k in range(KT)], [])).then_inc(row_full, 1)
            u = BIG0["agg"]
            free_big(pe, u)
            pe.wait_ge(wlo_up, NT)
            pe.wait_ge(row_read, ROW0["h4"] + 1)
            wide_mm(pe, u, sum([parts(both(h0, st), both(adj, st)) for st in range(NT)], [])).then_inc(big_full, 1)
            pe.wait_ge(big_read, u + 1)
            for t in range(NT):
                u = ROW0[f"o{t}"]
                free_row(pe, u)
                row_mm(pe, brow(u)[:, :], parts([aT[:, s, t * P:(t + 1) * P] for s in range(2)], ringpart(Q_LIN))).then_inc(row_full, 1)
            for t in range(NT):
                turn_norm(BIG0[f"l1_{t}"], LN_L1 + t, t)
            pe.wait_ge(split_done, Q_L + KT)
            for t in range(NT):
                u = ROW0[f"z{t}"]
                free_row(pe, u)
                pe.wait_ge(big_read, BIG0[f"l1_{t}"] + 1)
                row_mm(pe, brow(u)[:, :], sum([parts(tile_of(yT, k, t), ringpart(Q_L + k)) for k in range(KT)], [])).then_inc(row_full, 1)
            pe.wait_ge(split_done, Q_R + KT)
            pe.wait_ge(clo_up, NT)
            for t in range(NT):
                u = ROW0[f"r{t}"]
                free_row(pe, u)
                row_mm(pe, brow(u)[:, :], sum([parts(tile_of(yT, k, t), ringpart(Q_R + k)) for k in range(KT)], [])).then_inc(row_full, 1)
                u = ROW0[f"a{t}"]
                pe.wait_ge(row_read, ROW0["z4"] + 1)
                free_row(pe, u)
                row_mm(pe, brow(u)[:, :], sum([parts(tile_of(adj, st, t), both(vrow, st)) for st in range(NT)], [])).then_inc(row_full, 1)
            pe_l2(pe)
            pe_l3(pe, turn_norm)

        def dve_l2(dve, tile_stats, normalise, f32):
            for t in range(NT):
                if t >= 2:
                    dve.wait_ge(z_up, t - 1)
                normalise(LN_IN + t, LN_IN + t, t, x[:, t, :], t)
                dve.wait_ge(xn_up, LN_IN + t + 1)
                dve.tensor_scalar(z[:, t, :], xn[:, t % 2, :], 0.0, None, ALU.max).then_inc(z_up, 1)
                dve.wait_ge(z_up, t + 1)
                tile_stats(LN_BLK + t, NT + t, z[:, t, :])
            with dve.Fori(0, BLOCKS) as it:
                nb, nr = it * len(BLOCK_BIG), it * len(BLOCK_ROW)

                def scaled(ln, t):
                    i = LN_BLK + it * 2 * NT + ln * NT + t
                    normalise(i, i, (NT + ln * NT + t) % (2 * NT), z[:, t, :], t)
                    u = BIGBLK[f"c{ln}_{t}"]
                    dve.wait_ge(big_full, u + nb + 1)
                    dve.wait_ge(xn_up, i + 1)
                    if t >= 2:
                        dve.wait_ge(big_full, BIGBLK[f"t{ln}_{t - 2}"] + nb + 1)
                    dve.scalar_tensor_tensor(ybuf[:, t % 2, :], big[u % NBIG][:, 0, :], 1.0, xn[:, t % 2, :],
                                             ALU.add, ALU.mult).then_inc(y1_up, 1)
                    dve.wait_ge(y1_up, it * 2 * NT + ln * NT + t + 1)
                    dve.tensor_tensor(ybuf[:, t % 2, :], big[u % NBIG][:, 1, :], ybuf[:, t % 2, :], ALU.add).then_inc(big_read, 1)

                def turned_rest(ln, t):
                    u = BIGBLK[f"t{ln}_{t}"]
                    dve.wait_ge(yhi_up, 2 * NT + it * 2 * NT + ln * NT + t + 1)
                    dve.tensor_tensor(yT[:, 1, :, t * P:(t + 1) * P], bflat(u)[:, 0:D].rearrange("p (k n) -> p k n", k=KT),
                                      f32(yT[:, 0, :, t * P:(t + 1) * P]), ALU.subtract).then_inc(big_read, 1)

                def residual(name, t, xb, i, slot):
                    u = ROWBLK[f"{name}{t}"]
                    dve.wait_ge(row_full, u + nr + 1)
                    dve.wait_ge(xb_up, xb)
                    dve.tensor_tensor(z[:, t, :], brow(u)[:, :], z[:, t, :], ALU.add).then_inc(row_read, 1)
                    dve.wait_ge(row_read, u + nr + 1)
                    tile_stats(i, slot, z[:, t, :])

                for n in norm_order(0):
                    (scaled if n[0] == "c" else turned_rest)(0, int(n[3]))
                for i, to in enumerate((qT, kT)):
                    for h in range(HEADS):
                        u = BIGBLK["qk"[i] + str(h)]
                        dve.wait_ge(qkhi_up, it * 2 * HEADS + i * HEADS + h + 1)
                        dve.scalar_tensor_tensor(wide(to[:, 1, h, :]), bwide(u), bqk[:, i, bass.ds(it * KT + h, 1)],
                                                 wide(f32(to[:, 0, h, :])), ALU.add, ALU.subtract).then_inc(big_read, 1)
                for t in range(NT):
                    u = BIGBLK[f"v{t}"]
                    dve.wait_ge(bias_ld, 48 * it + 48)
                    dve.wait_ge(big_full, u + nb + 1)
                    if t >= 2:
                        dve.wait_ge(vlo_up, it * NT + t - 1)
                    dve.tensor_tensor(vbuf[:, t % 2, :], big[u % NBIG][:, 0, :], bias[:, 0, :], ALU.add).then_inc(big_read, 1)
                heads = it * HEADS * NT
                for what, k in ATT + [("last", 0)]:
                    if what == "S":
                        u = BIGBLK[f"S{k}"]
                        t = k % NT
                        if k >= 4:
                            dve.wait_ge(big_full, BIGBLK[f"T{k - 4}"] + nb + 1)
                        wait_apart(dve, big_full, u + nb + 1)
                        dve.tensor_tensor_reduce(wide(pbuf[:, k % 4, :]), bwide(u), wide(mask[:, t, :]), 1.0, -3e38,
                                                 ALU.add, ALU.max, smax[:, k:k + 1]).then_inc(big_read, 1)
                        dve.wait_ge(big_read, u + nb + 1)
                        dve.tensor_scalar(nsmax[:, k:k + 1], smax[:, k:k + 1], -DH ** -0.5, None, ALU.mult).then_inc(nb_up, 1)
                    if what == "S" and k >= 1 or (what, k) == ("T", HEADS * NT - LAG):
                        j = k - 1 if what == "S" else HEADS * NT - 1
                        dve.wait_ge(exp_up, heads + j + 1)
                        dve.reciprocal(rden[:, j:j + 1], den[:, j:j + 1]).then_inc(rden_up, 1)
                    if what == "T":
                        u, t = BIGBLK[f"T{k}"], k % NT
                        dve.wait_ge(phi_up, heads + k + 1)
                        dve.tensor_tensor(pT[:, 1, :, t * P:(t + 1) * P], bflat(u).rearrange("p (k n) -> p k n", k=NT),
                                          f32(pT[:, 0, :, t * P:(t + 1) * P]), ALU.subtract).then_inc(big_read, 1)
                    elif what == "PV":
                        u = BIGBLK[f"PV{k}"]
                        dve.wait_ge(ohi_up, it * HEADS + k + 1)
                        dve.tensor_tensor(wide(qT[:, 1, k, :]), bwide(u), wide(f32(qT[:, 0, k, :])), ALU.subtract).then_inc(big_read, 1)
                xb = NT + it * 2 * NT + 1
                done = 0
                for n in norm_order(1):
                    while done < NT and n[0] == "c" and done < int(n[3]) + 2:
                        residual("wo", done, xb + done, LN_BLK + it * 2 * NT + NT + done, done)
                        done += 1
                    (scaled if n[0] == "c" else turned_rest)(1, int(n[3]))
                for o in range(KT):
                    u = BIGBLK[f"m{o}"]
                    dve.wait_ge(big_full, u + nb + 1)
                    if o >= 2:
                        dve.wait_ge(hlo_up, it * KT + o - 1)
                    dve.tensor_scalar(wide(rbuf[:, o % 2, :]), bwide(u), bqk[:, 2, bass.ds(it * KT + o, 1)], 0.0,
                                      ALU.add, ALU.max).then_inc(big_read, 1)
                for t in range(NT):
                    residual("m2_", t, xb + NT + t, LN_BLK + (it + 1) * 2 * NT + t, NT + t)
            for t in range(NT):
                dve.tensor_tensor(x[:, t, :], x[:, t, :], z[:, t, :], ALU.add).then_inc(x_up, 1)
        @block.vector
        def _(dve):
            own = [0]

            def step(ins):
                own[0] += 1
                ins.then_inc(dstep, 1)
                dve.wait_ge(dstep, own[0])

            def f32(ap):
                return ap.bitcast(F32)

            dve.memset(edge[0:NG, 0, :].bitcast(I32), 9999).then_inc(e_clear, 1)
            dve.memset(edge[0:NG, 2, :], 0.0).then_inc(e_clear, 1)
            dve.memset(x[:, NT - 1, :], 0.0).then_inc(x_clear, 1)
            dve.memset(acc[:, 0:NT * ACCW], 0.0).then_inc(scat_read, 2)
            dve.memset(acc[:, NT * ACCW:2 * NT * ACCW], 0.0).then_inc(scat_full, 2)
            dve.wait_ge(e_ld, 16 * 7)
            step(dve.tensor_copy(edge[0:NG, 3, :], edge[0:NG, 0, :].bitcast(I32)))
            step(dve.tensor_copy(edge[0:NG, 4, :], edge[0:NG, 1, :].bitcast(I32)))
            step(dve.tensor_reduce(mnmx[0:NG, 0:1], edge[0:NG, 4, :], AX.X, ALU.min))
            step(dve.tensor_reduce(mnmx[0:NG, 1:2], edge[0:NG, 4, :], AX.X, ALU.max))
            step(dve.tensor_tensor(mnmx[0:NG, 2:3], mnmx[0:NG, 1:2], mnmx[0:NG, 0:1], ALU.subtract))
            dve.wait_ge(const0, 3)
            step(dve.tensor_scalar(xn[0:NG, 0, 0:NG], ident[0:NG, 0:NG], mnmx[0:NG, 0:1], None, ALU.mult))
            step(dve.tensor_scalar(xn[0:NG, 0, NG:2 * NG], ident[0:NG, 0:NG], mnmx[0:NG, 2:3], None, ALU.mult))
            for name, to in (("src", src_col), ("w", w_col)):
                dve.wait_ge(big_full, BIG0[name] + 1)
                dve.tensor_copy(to[:, :, :], bflat(BIG0[name])[:, 0:CH * NG].rearrange("p (j g) -> p j g", j=CH)).then_inc(big_read, 1)
            u = BIG0["base"]
            dve.wait_ge(big_full, u + 1)
            step(dve.tensor_copy(base_f[:, :], bflat(u)[:, 0:NG]))
            dve.tensor_reduce(span[:, 0:1], bflat(u)[:, NG:2 * NG], AX.X, ALU.max).then_inc(big_read, 1)
            u = BIG0["dst"]
            dve.wait_ge(big_full, u + 1)
            dve.tensor_tensor(dst_rel[:, :, :], bflat(u)[:, 0:CH * NG].rearrange("p (j g) -> p j g", j=CH),
                              base_f[:, :].unsqueeze(1).broadcast_to([P, CH, NG]), ALU.subtract).then_inc(big_read, 1)
            step(dve.tensor_copy(base_i[:, :], base_f[0:1, :]))
            dve.wait_ge(big_read, u + 1)
            step(dve.tensor_copy(span_i[:, 0:1], span[:, 0:1]))
            dve.tensor_scalar(span_i[:, 1:2], span_i[:, 0:1], WIN.bit_length() - 1, None, ALU.arith_shift_right).then_inc(w_ready, 1)
            step(dve.tensor_copy(w_part[:, 0, :, :], w_col[:, :, :]))
            for i in (1, 2):
                step(dve.tensor_tensor(w_col[:, :, :], w_col[:, :, :], w_part[:, i - 1, :, :], ALU.subtract))
                ins = dve.tensor_copy(w_part[:, i, :, :], w_col[:, :, :])
                if i == 1:
                    step(ins)
            ins.then_inc(w_ready, 1)
            u = BIG0["vec"]
            dve.wait_ge(big_full, u + 1)
            dve.tensor_copy(cols[:, :], bflat(u)[:, 0:VECS]).then_inc(big_read, 1)
            dve.wait_ge(const1, 3)
            dve.wait_ge(f_ld, 16 * 11)
            step(dve.tensor_scalar(fcol[0:2 * NF, 1:2], freq_i, float(np.float32(2.0 * np.pi / 16)), None, ALU.mult))
            noise, ph, kf, r = tmp64[0:4]
            step(dve.tensor_scalar(ph, noise, fcol[0:2 * NF, 1:2], None, ALU.mult))
            MAGIC = 1.5 * 2.0 ** 23
            step(dve.tensor_scalar(kf, ph, float(1 / (2 * np.pi)), MAGIC, ALU.mult, ALU.add))
            step(dve.tensor_scalar(kf, kf, MAGIC, None, ALU.subtract))
            TURN_HI = 6.28125
            step(dve.scalar_tensor_tensor(r, kf, -TURN_HI, ph, ALU.mult, ALU.add))
            step(dve.scalar_tensor_tensor(r, kf, -float(2 * np.pi - TURN_HI), r, ALU.mult, ALU.add))
            step(dve.tensor_scalar(r, r, 3.1415925, -3.1415925, ALU.min, ALU.max))
            c = r[NF:2 * NF]
            step(dve.scalar_tensor_tensor(c, c, -1.0, c, ALU.mult, ALU.max))
            dve.tensor_scalar(c, c, -1.0, float(np.pi / 2), ALU.mult, ALU.add).then_inc(emb_up, 1)
            u = BIG0["z1"]
            dve.wait_ge(big_full, u + 1)
            z1 = mask[0:C16, 1, :]
            dve.tensor_scalar(wide(z1), big[u % NBIG][0:C16, :, 0:HALF], fcol[0:C16, 3:4], None, ALU.add).then_inc(big_read, 1)
            dve.wait_ge(sig_done, 1)
            dve.tensor_tensor(mask[0:C16, 3, :], z1, mask[0:C16, 2, :], ALU.mult).then_inc(silu_up, 1)
            u = BIG0["cond"]
            dve.wait_ge(cb_one, 4)
            dve.wait_ge(big_full, u + 1)
            ct = mask[:, 4, :]
            dve.tensor_scalar(wide(ct), bwide(u), fcol[:, 2:3], None, ALU.add).then_inc(big_read, 1)
            dve.wait_ge(big_read, u + 1)
            dve.tensor_copy(condT[0:64, :], ct[0:64]).then_inc(condT_up, 1)
            step(dve.tensor_copy(condT[64:P, :], ct[64:P]))
            dve.tensor_tensor(condT[64:P, :], ct[64:P], f32(condT[64:P, :]), ALU.subtract).then_inc(condT_up, 1)

            def tile_stats(i, slot, src):
                dve.bn_stats(stats[:, slot, :], src).then_inc(st_up, 1)
                wait_apart(dve, st_up, i + 1)
                dve.bn_aggr(mv[:, slot, :], stats[:, slot, :]).then_inc(aggr_up, 1)

            def normalise(i, ixn, slot, src, t):
                dve.wait_ge(rstd_up, i + 1)
                dve.tensor_scalar(xn[:, t % 2, :], src, mv[:, slot, 0:1], rstd[:, slot:slot + 1],
                                  ALU.subtract, ALU.mult).then_inc(xn_up, 1)

            def turned_rest(u, i, t):
                dve.wait_ge(yhi_up, i + 1)
                dve.scalar_tensor_tensor(yT[:, 1, :, t * P:(t + 1) * P], bflat(u)[:, 0:D].rearrange("p (k n) -> p k n", k=KT),
                                         0.0, f32(yT[:, 0, :, t * P:(t + 1) * P]), ALU.max, ALU.subtract).then_inc(big_read, 1)

            def relu_norm(first, slot0, names, yfirst):
                for t in range(NT + 1):
                    if t < NT:
                        if t >= 2:
                            dve.wait_ge(big_full, names[t - 2] + 1)
                        normalise(first + t, first + t, slot0 + t, x[:, t, :], t)
                    if t >= 1:
                        turned_rest(names[t - 1], yfirst + t - 1, t - 1)

            dve.wait_ge(x_ld, 32)
            for t in range(NT):
                tile_stats(t, t, x[:, t, :])
            relu_norm(0, 0, [BIG0[f"l0_{t}"] for t in range(NT)], 0)

            dve.wait_ge(w_ready, 2)
            passes = dve.value_load(span_i[0:1, 1:2], min_val=0, max_val=NP // WIN)
            with dve.Fori(0, passes + 1) as kp:
                def hot(g, b):
                    dve.wait_ge(scat_full, kp * NG + g + 1)
                    for j in range(CH):
                        ins = dve.tensor_scalar(hot_src[:, b, j, :], iota16[:, :], src_col[:, j, bass.ds(g, 1)], None, ALU.is_equal)
                    ins.then_inc(hot_src_up, 1)
                    dve.tensor_tensor(hot_dst[:, b, :, 0:WIN], iota16[:, 0:WIN].unsqueeze(1).broadcast_to([P, CH, WIN]),
                                      dst_rel[:, :, bass.ds(g, 1)].broadcast_to([P, CH, WIN]), ALU.is_equal).then_inc(hot_dst_up, 1)

                def add(g, b):
                    w0 = dve.value_load(base_i[0:1, bass.ds(g, 1)], min_val=0, max_val=NP)
                    dve.wait_ge(scat_full, kp * NG + g + 3)
                    dve.wait_ge(scat_read, kp * NG + g + 2)
                    win = adjacc[:, :, :, bass.ds(w0, WIN)]
                    dve.tensor_tensor(win, bflat(b).rearrange("p (t c n) -> p t c n", t=NT, c=2), win, ALU.add).then_inc(scat_read, 1)

                hot(0, 0)
                with dve.Fori(0, NG // 2 - 1) as gi:
                    hot(gi * 2 + 1, 1)
                    add(gi * 2, 0)
                    hot(gi * 2 + 2, 0)
                    add(gi * 2 + 1, 1)
                hot(NG - 1, 1)
                add(NG - 2, 0)
                add(NG - 1, 1)
                dve.tensor_scalar(dst_rel[:, :, :], dst_rel[:, :, :], float(WIN), None, ALU.subtract).then_inc(pass_up, 1)
                dve.tensor_scalar(base_f[0:1, :], base_f[0:1, :], float(WIN), float(NP), ALU.add, ALU.min).then_inc(pass_up, 1)
                dve.wait_ge(pass_up, kp * 3 + 2)
                dve.tensor_copy(base_i[:, :], base_f[0:1, :]).then_inc(pass_up, 1)
                dve.wait_ge(pass_up, kp * 3 + 3)
            dve.wait_ge(scat_read, (passes + 1) * NG + 2)

            for t in range(NT):
                d = w_acc[:, t, t * P:(t + 1) * P]
                dve.tensor_tensor(d, d, ident[:, :], ALU.add).then_inc(diag_up, 1)
            dve.wait_ge(col_ld, 16 * 2)
            step(dve.tensor_scalar(bc_hl[:, 0, :], ones[:, :], bconv[:, 0:1], None, ALU.mult))
            dve.scalar_tensor_tensor(bc_hl[:, 1, :], ones[:, :], bconv[:, 0:1], f32(bc_hl[:, 0, :]), ALU.mult, ALU.subtract).then_inc(bconv_up, 1)
            u = ROW0["brow"]
            dve.wait_ge(row_full, u + 1)
            dve.tensor_tensor(bias[:, 0, :], brow(u)[:, :], bias[:, 0, :], ALU.add).then_inc(row_read, 1)
            u = ROW0["deg"]
            dve.wait_ge(row_full, u + 1)
            dve.tensor_copy(degs[:, 0, :], brow(u)[:, 0:NT]).then_inc(w_up, 1)
            dve.tensor_scalar(degs[:, 1, :], brow(u)[:, 0:NT], 1e-30, None, ALU.max).then_inc(w_up, 1)
            dve.tensor_scalar(rcnt[:, 0, :], brow(u)[:, NT:2 * NT], 1.0, None, ALU.max).then_inc(row_read, 1)
            dve.wait_ge(row_read, u + 1)
            dve.reciprocal(rcnt[:, 1, :], rcnt[:, 0, :]).then_inc(w_up, 1)
            for t in range(NT):
                dve.wait_ge(whi_up, t + 1)
                dve.tensor_tensor(adj[:, 1, t, :], w_acc[:, t, :], f32(adj[:, 0, t, :]), ALU.subtract).then_inc(wlo_up, 1)
            dve.wait_ge(dpow_up, 1)
            dve.scalar_tensor_tensor(degs[:, 3, :], degs[:, 0, :], 0.0, degs[:, 2, :], ALU.is_gt, ALU.mult).then_inc(dinv_up, 1)
            dve.wait_ge(dinv_up, 1)
            for t in range(NT):
                u = ROW0[f"h{t}"]
                dve.wait_ge(h0hi_up, t + 1)
                dve.scalar_tensor_tensor(h0[:, 1, t, :], brow(u)[:, 0:P], degs[:, 3, t:t + 1], f32(h0[:, 0, t, :]),
                                         ALU.mult, ALU.subtract).then_inc(row_read, 1)
            u = BIG0["agg"]
            dve.wait_ge(ahi_up, 1)
            dve.tensor_tensor(wide(aT[:, 1, :]), bwide(u), wide(f32(aT[:, 0, :])), ALU.subtract).then_inc(big_read, 1)
            for t in range(NT):
                u = ROW0[f"o{t}"]
                dve.wait_ge(row_full, u + 1)
                dve.wait_ge(xb_up, t + 1)
                dve.scalar_tensor_tensor(x[:, t, :], brow(u)[:, :], degs[:, 3, t:t + 1], x[:, t, :], ALU.mult, ALU.add).then_inc(row_read, 1)
                dve.wait_ge(row_read, u + 1)
                tile_stats(LN_L1 + t, NT + t, x[:, t, :])
            for t in range(NT):
                dve.wait_ge(chi_up, t + 1)
                dve.tensor_tensor(adj[:, 1, t, :], cnt_acc[:, t, :], f32(adj[:, 0, t, :]), ALU.subtract).then_inc(clo_up, 1)
            relu_norm(LN_L1, NT, [BIG0[f"l1_{t}"] for t in range(NT)], NT)
            step(dve.tensor_reduce(flag[:, 0, :], cnt_acc, AX.X, ALU.max))
            step(dve.tensor_scalar(flag[:, 1, :], flag[:, 0, :], 0.5, None, ALU.is_gt))
            step(dve.tensor_scalar(flag[:, 2, :], flag[:, 1, :], NOEDGE, None, ALU.mult))
            step(dve.tensor_scalar(flag[:, 3, :], flag[:, 2, :], -1.0, NOEDGE, ALU.mult, ALU.add))
            dve.tensor_scalar(mask[:, :, :], cnt_acc, 1.0, None, ALU.max).then_inc(clamp_up, 1)
            for t in range(NT):
                u = ROW0[f"z{t}"]
                dve.wait_ge(zhi_up, t + 1)
                dve.tensor_tensor(vrow[:, 1, t, :], brow(u)[:, :], f32(vrow[:, 0, t, :]), ALU.subtract).then_inc(row_read, 1)
            pen = cnt_acc
            for t in range(NT):
                dve.tensor_scalar(pen[:, t, :], pen[:, t, :], 0.5, flag[:, 2, t:t + 1], ALU.is_lt, ALU.mult).then_inc(pen_up, 1)
            dve.wait_ge(pen_up, NT)
            dve.wait_ge(ln_up, 1)
            dve.scalar_tensor_tensor(mask[:, :, :], mask[:, :, :], DH ** 0.5, pen, ALU.mult, ALU.add).then_inc(mask_up, 1)
            dve.wait_ge(mask_up, 1)
            for t in range(NT):
                u = ROW0[f"r{t}"]
                dve.wait_ge(row_full, u + 1)
                dve.tensor_tensor(t1[:, t % 2, :], brow(u)[:, :], bias[:, 1, :], ALU.add).then_inc(row_read, 1)
                dve.wait_ge(row_read, u + 1)
                u = ROW0[f"a{t}"]
                dve.wait_ge(row_full, u + 1)
                if t >= 2:
                    dve.wait_ge(l1p_up, t - 1)
                dve.scalar_tensor_tensor(t2[:, t % 2, :], brow(u)[:, :], rcnt[:, 1, t:t + 1], t1[:, t % 2, :],
                                         ALU.mult, ALU.add).then_inc(row_read, 1)
                dve.wait_ge(gate_up, t + 1)
                dve.tensor_tensor(t1[:, t % 2, :], t2[:, t % 2, :], sg[:, t % 2, :], ALU.mult).then_inc(l1p_up, 1)
                dve.wait_ge(l1p_up, t + 1)
                dve.tensor_tensor(x[:, t, :], x[:, t, :], t1[:, t % 2, :], ALU.add).then_inc(x_up, 1)
                dve.wait_ge(x_up, t + 1)
                tile_stats(LN_IN + t, t, x[:, t, :])
            dve_l2(dve, tile_stats, normalise, f32)
            dve_l3(dve, tile_stats, relu_norm, step)



NAMES = (
    ["x", "src", "dst", "edge_weight", "node_vec1"]
    + ["L0_gnn_" + n for n in ("W_conv", "b_conv", "W_lin", "b_lin")]
    + ["L1_gnn_" + n for n in ("W_l", "W_r", "b")]
    + ["L2_gnn_" + n for n in ("f_w1", "f_b1", "f_w2", "f_b2", "s1_w", "s1_b", "b1_w", "b1_b", "wq", "bq", "wk", "bk",
                               "wv", "bv", "wo", "bo", "s2_w", "s2_b", "b2_w", "b2_b", "m_w1", "m_b1", "m_w2", "m_b2")]
    + ["L3_gnn_" + n for n in ("W_f", "att_src_f", "att_dst_f", "bias_f", "W_b", "att_src_b", "att_dst_b", "bias_b",
                               "W_fuse", "b_fuse", "bn_gamma", "bn_beta")]
)


def kernel(**inputs):
    import numpy as np
    import concourse.bacc as bacc
    from concourse import mybir
    from concourse.bass_utils import run_bass_kernel_spmd as run

    nc = bacc.Bacc("TRN2", target_bir_lowering=False, num_devices=1)
    arrays, aps = {}, {}
    for name in NAMES:
        v = np.ascontiguousarray(inputs[name])
        arrays["in_" + name] = v
        aps[name] = nc.dram_tensor("in_" + name, v.shape, mybir.dt.from_np(v.dtype), kind="ExternalInput").ap()
    out = nc.dram_tensor("out_x", (N, D), F32, kind="ExternalOutput").ap()
    build(nc, aps, out)
    r = run(nc, [arrays], core_ids=[0])
    return r.results[0]["out_x"]
```

```python
from contextlib import ExitStack

import numpy as np

import concourse.bass as bass
from concourse import mybir

F32 = mybir.dt.float32
F32R = mybir.dt.float32r
BF16 = mybir.dt.bfloat16
F16 = mybir.dt.float16
I32 = mybir.dt.int32
ALU = mybir.AluOpType
ACT = mybir.ActivationFunctionType
AX = mybir.AxisListType

P = 128
N = 625
NT = (N + P - 1) // P
NP = NT * P
TAIL = N - (NT - 1) * P
HALF = NP // 2
D = 512
KT = D // P
E = 20000
GROUP = 512
CH = GROUP // P
NG = (E + GROUP - 1) // GROUP
ELAST = E - (NG - 1) * GROUP
WIN = 40
PASS_MUL = 2 ** 16 // WIN + 1
assert all((i * PASS_MUL) >> 16 == i // WIN for i in range(NP + 1))
HOT = 4
assert NG % HOT == 0 and NT * 2 * WIN <= 512
ACCW = NP + WIN
BLOCKS = 4
HEADS = 4
DH = D // HEADS
L3H = 4
L3C = D // (2 * L3H)
NJ = 2 * L3H
NF = 32
C16 = 16
EPS = 1e-5
NOEDGE = -1e30
RING = 6
STAGE = 2
LAG = 3

PRE_BIG = ["src", "w", "base", "dst"] + [f"l0_{t}" for t in range(NT)] + ["z1", "cond", "hall"]
MID_BIG = ["degw", "degc", "agg"] + [f"l1_{t}" for t in range(NT)]


def norm_order(ln):
    return [f"c{ln}_0", f"c{ln}_1", f"t{ln}_0", f"c{ln}_2", f"t{ln}_1", f"c{ln}_3", f"t{ln}_2",
            f"c{ln}_4", f"t{ln}_3", f"t{ln}_4"]


def attention_order(scores_first):
    steps = []
    for k in range(HEADS * NT + LAG):
        scores = [("S", k)] if k < HEADS * NT else []
        kk = k - LAG
        turned = [("PV", kk // NT - 1)] if kk >= NT and kk % NT == 0 else []
        turned += [("T", kk)] if kk >= 0 else []
        steps += scores + turned if scores_first else turned + scores
    return steps + [("PV", HEADS - 1)]


ATT = attention_order(True)
ATT_ACT = attention_order(False)
IN_HEADS = (4, 6, 8, 10)
BLOCK_BIG = (norm_order(0) + [f"q{h}" for h in range(HEADS)] + [f"k{h}" for h in range(HEADS)]
             + [f"v{t}" for t in range(NT)] + [f"{a}{b}" for a, b in ATT] + norm_order(1)
             + [f"m{o}" for o in range(KT)])
L3_BIG = ([f"l3_{t}" for t in range(NT)] + [f"mt{t}" for t in range(NT)] + ["as"]
          + [f"am{j}" for j in range(NJ)] + ["vt"]
          + ["vb0"] + sum([[f"vb{j + 1}", f"va{j}"] if j < NJ - 1 else [f"va{j}"] for j in range(NJ)], [])
          + ["rec"] + [f"rb{k}" for k in range(KT)] + [f"f{o}" for o in range(KT)])
PRE_ROW = ["vec", "brow"] + [f"o{t}" for t in range(NT)]
MID_ROW = [f"z{t}" for t in range(NT)] + sum([[f"r{t}", f"a{t}"] for t in range(NT)], [])
BLOCK_ROW = [f"wo{t}" for t in range(NT)] + [f"m2_{t}" for t in range(NT)]
L3_ROW = [f"H{t}" for t in range(NT)] + sum([[f"P{j}a", f"P{j}b"] for j in range(NJ)], []) + [f"y{t}" for t in range(NT)]

NBIG, NROW = 3, 2
ROW_SPLIT = (3 * P, NP - 3 * P)
NE = 4
assert PRE_BIG.index("hall") == len(PRE_BIG) - 1 and PRE_BIG.index("hall") % NBIG == 2
BIG0 = {n: i for i, n in enumerate(PRE_BIG + MID_BIG)}
BIGB = len(BIG0)
BIGBLK = {n: BIGB + i for i, n in enumerate(BLOCK_BIG)}
BIG3 = {n: BIGB + BLOCKS * len(BLOCK_BIG) + i for i, n in enumerate(L3_BIG)}
ROW0 = {n: i for i, n in enumerate(PRE_ROW + MID_ROW)}
ROWB = len(ROW0)
ROWBLK = {n: ROWB + i for i, n in enumerate(BLOCK_ROW)}
ROW3 = {n: ROWB + BLOCKS * len(BLOCK_ROW) + i for i, n in enumerate(L3_ROW)}
assert len(BLOCK_BIG) % NBIG == 0 and len(BLOCK_ROW) % NROW == 0

Q_CONV, Q_LIN, Q_L, Q_R = 0, 1, 2, 2 + KT
RING_BLK = 2 + 2 * KT
PERBLK = 6 * KT
F_LOADS = 3 + 2 * 4
VECS = 3 * BLOCKS * KT + 4 * KT + 1
RING_L3 = RING_BLK + BLOCKS * PERBLK
S_COND = RING_BLK
S_BLK = S_COND + 4
S_PERBLK = PERBLK + 4
S_L3 = S_BLK + BLOCKS * S_PERBLK
assert PERBLK % RING == 0 and S_PERBLK % STAGE == 0
WQ, WK, WV, WO, W1, W2 = (KT * i for i in range(6))
LN_L1, LN_IN, LN_BLK = NT, 2 * NT, 3 * NT
LN_L3 = LN_BLK + NT + BLOCKS * 2 * NT
XN_L3 = LN_BLK + BLOCKS * 2 * NT


def wide(ap640):
    return ap640.rearrange("p (h n) -> p h n", h=2)


def build(nc, a, out):
    ctx = ExitStack()
    with ctx:
        def sb(name, shape, dt):
            return ctx.enter_context(nc.sbuf_tensor(name, shape, dt))

        def sem(name):
            return ctx.enter_context(nc.semaphore(name))

        x = sb("x", [P, NT, D], F32)
        z = sb("z", [P, NT, D], F32)
        arena1 = sb("arena1", [P, 2 * 2 * HEADS * NP], F32R)
        arena2 = sb("arena2", [P, 2 * NT * D], F32R)
        arena3 = sb("arena3", [P, 2 * NT * NP], F32R)
        acc = sb("acc", [P, NT * NP + NT * NJ // 2 * 3 * L3C], F32)
        mask = sb("mask", [P, NT, NP], F32)
        ringw = sb("ringw", [P, RING, 2, D], F32R)
        raw = sb("raw", [P, STAGE, D], F32)
        condw = sb("condw", [P, 4, D], F32R)
        condT = sb("condT", [P, NP], F32R)
        bias = sb("bias", [P, 3, D], F32)
        xn = sb("xn", [P, 2, D], F32)
        ident = sb("ident", [P, P], F32)
        ones = sb("ones", [P, P], F32)
        iota16 = sb("iota16", [P, NP], F16)
        edge_col = sb("edge_col", [P, 3 * CH * NG], F32)
        w_part = sb("w_part", [P, 3, CH, NG], BF16)
        hot_dst = sb("hot_dst", [P, HOT, CH, 4 * WIN], BF16)
        base_f = sb("base_f", [P, NG], F32)
        base_i = sb("base_i", [1, NG], I32)
        span = sb("span", [P, 2], F32)
        span_i = sb("span_i", [P, 2], I32)
        mnmx = sb("mnmx", [P, 4], F32)
        stats = sb("stats", [P, 2 * NT, 6], F32)
        mv = sb("mv", [P, 2 * NT, 2], F32)
        veps = sb("veps", [P, 2 * NT], F32)
        rstd = sb("rstd", [P, 2 * NT], F32)
        half = sb("half", [P, NT], F32)
        degs = sb("degs", [P, 4, NT], F32)
        rcnt = sb("rcnt", [P, 2, NT], F32)
        flag = sb("flag", [P, 4, NT], F32)
        nsmax = sb("nsmax", [P, HEADS * NT], F32)
        den = sb("den", [P, HEADS * NT], F32)
        rden = sb("rden", [P, HEADS * NT], F32)
        vec = sb("vec", [VECS, P], F32)
        cols = sb("cols", [P, VECS], F32)
        fcol = sb("fcol", [P, 4], F32)
        f_w1 = sb("f_w1", [2 * NF, C16], F32)
        f_w2 = sb("f_w2", [C16, P], F32)
        bn3 = sb("bn3", [P, KT, 2, 6], F32)
        mv3 = sb("mv3", [P, KT, 2], F32)
        bnc = sb("bnc", [P, 4, KT], F32)

        src_col, dst_rel, w_col = [edge_col[:, i * CH * NG:(i + 1) * CH * NG].rearrange("p (j g) -> p j g", j=CH) for i in range(3)]
        l3s = edge_col[:, 0:5 * NT * NJ].rearrange(
            "p (i t j) -> p i t j", i=5, t=NT)
        l3v = edge_col[:, 5 * NT * NJ:7 * NT * NJ].rearrange(
            "p (t j) -> p t j", t=NT)
        bqk = cols[:, 0:3 * BLOCKS * KT].rearrange("p (i n) -> p i n", i=3)
        l3col = cols[:, 3 * BLOCKS * KT:VECS - 1].rearrange("p (i n) -> p i n", i=4)
        bconv = cols[:, VECS - 1:VECS]
        freq_i = fcol[0:2 * NF, 0:1].bitcast(I32)
        edge = z
        yT = arena3[:, 0:2 * KT * NP].rearrange("p (s k n) -> p s k n", s=2, k=KT)
        pT = arena3[:, :].rearrange("p (s k n) -> p s k n", s=2, k=NT)
        qT = arena1[:, 0:2 * HEADS * NP].rearrange("p (s k n) -> p s k n", s=2, k=HEADS)
        kT = arena1[:, 2 * HEADS * NP:4 * HEADS * NP].rearrange("p (s k n) -> p s k n", s=2, k=HEADS)
        adj = arena1[:, 0:2 * NT * NP].rearrange("p (s k n) -> p s k n", s=2, k=NT)
        vrow = arena2[:, :].rearrange("p (s k n) -> p s k n", s=2, k=NT)
        h0 = arena2[:, 0:2 * NT * P].rearrange("p (s k n) -> p s k n", s=2, k=NT)
        aT = arena2[:, 2 * NT * P:2 * NT * P + 2 * NP].rearrange("p (s n) -> p s n", s=2)
        bc_hl = arena2[:, 2 * NT * P + 2 * NP:2 * NT * P + 2 * NP + 2 * P].rearrange("p (s n) -> p s n", s=2)
        adjacc = acc[:, 0:NT * 2 * ACCW].rearrange("p (t c n) -> p t c n", t=NT, c=2)
        cnt_acc = adjacc[:, :, 0, 0:NP]
        w_acc = adjacc[:, :, 1, 0:NP]
        hot_src = [m[:, :, :].rearrange("p t n -> p (t n)").bitcast(BF16)[:, b * CH * NP:(b + 1) * CH * NP].rearrange(
            "p (j n) -> p j n", j=CH) for m in (mask, z) for b in range(2)]
        hot_abs = [mask[:, NT - 1, :].bitcast(BF16)[:, b * NP:(b + 1) * NP] for b in range(2)]
        tmp64 = [mask[0:2 * NF, i, :] for i in range(NT)]
        pbuf = acc[:, 0:4 * NP].rearrange("p (b n) -> p b n", b=4)
        rbuf = acc[:, 4 * NP:6 * NP].rearrange("p (b n) -> p b n", b=2)
        ybuf = acc[:, 6 * NP:6 * NP + 2 * D].rearrange("p (b n) -> p b n", b=2)
        vbuf = acc[:, 6 * NP + 2 * D:6 * NP + 4 * D].rearrange("p (b n) -> p b n", b=2)
        t1 = w_acc[:, 0:2, 0:D]
        t2 = w_acc[:, 2:4, 0:D]
        sg = z[:, 0:2, :]
        maskT = acc[:, 0:NT * NP].rearrange("p (t n) -> p t n", t=NT)
        ebuf = [xn[:, :, :].rearrange("p b n -> p (b n)")[:, 0:NP]] + [
            hot_dst[:, :, :, :].rearrange("p b j n -> p (b j n)").bitcast(F32)[:, i * NP:(i + 1) * NP] for i in range(2)] + [
            raw[:, :, :].rearrange("p b n -> p (b n)")[:, 0:NP]]
        vbrow = [bias[:, :, :].rearrange("p b n -> p (b n)")[:, i * NP:(i + 1) * NP] for i in range(2)]
        den_row = [b[:, :, :].rearrange("p b n -> p (b n)")[:, NP:NP + n] for b, n in zip((raw, xn), ROW_SPLIT)]
        l3rows = arena1[0:2 * NJ, 0:2 * NP].rearrange("p (s n) -> p s n", s=2)
        l3pick = arena1[0:2 * NJ, 2 * NP:2 * NP + 2 * NJ]
        l3pair = arena1[0:NJ, 2 * NP + 2 * NJ:2 * NP + 2 * NJ + NJ * L3C]
        Hx = acc[:, NT * NP:NT * NP + NT * NJ // 2 * 3 * L3C].rearrange("p (t k c) -> p t k c", t=NT, k=NJ // 2)
        fT = z[:, :, :].rearrange("p t n -> p (t n)").rearrange("p (k n) -> p k n", k=KT)
        comb = fT
        combT = yT

        psum = ctx.enter_context(nc.psum_tensor("psum", [P, 2 * NBIG + NROW, D], F32))
        big = [psum[:, 2 * i:2 * i + 2, :] for i in range(NBIG)]
        row = [psum[:, 2 * NBIG + i, :] for i in range(NROW)]
        den_col = psum[:, 2 * NBIG + 1, D - NT * NJ:D]

        def bwide(u):
            return big[u % NBIG][:, :, 0:HALF]

        def bflat(u):
            return big[u % NBIG][:, :, :].rearrange("p h n -> p (h n)")[:, 0:NP]

        def scat(b):
            return big[b // 2][:, b % 2, 0:NT * 2 * WIN]

        def brow(u):
            return row[u % NROW][:, :]

        big_full = sem("big_full")
        big_read = sem("big_read")
        row_full = sem("row_full")
        row_read = sem("row_read")
        raw_ld = [sem(f"raw_ld{i}") for i in range(STAGE)]
        split_done = sem("split_done")
        x_clear = sem("x_clear")
        x_ld = sem("x_ld")
        e_clear = sem("e_clear")
        e_ld = sem("e_ld")
        f_ld = sem("f_ld")
        cb_one = sem("cb_one")
        col_ld = sem("col_ld")
        vec_ld = sem("vec_ld")
        bias_ld = sem("bias_ld")
        const0 = sem("const0")
        const1 = sem("const1")
        dstep = sem("dstep")
        gstep = sem("gstep")
        diag_up = sem("diag_up")
        emb_up = sem("emb_up")
        sin_done = sem("sin_done")
        sig_done = sem("sig_done")
        silu_up = sem("silu_up")
        condT_up = sem("condT_up")
        hot_src_up = sem("hot_src_up")
        hot_abs_up = sem("hot_abs_up")
        hot_act_up = sem("hot_act_up")
        hot_dst_up = sem("hot_dst_up")
        hot_w_up = sem("hot_w_up")
        scat_full = sem("scat_full")
        scat_read = sem("scat_read")
        w_ready = sem("w_ready")
        w_up = sem("w_up")
        whi_up = sem("whi_up")
        wlo_up = sem("wlo_up")
        chi_up = sem("chi_up")
        clo_up = sem("clo_up")
        dpow_up = sem("dpow_up")
        dinv_up = sem("dinv_up")
        bconv_up = sem("bconv_up")
        st_up = sem("st_up")
        aggr_up = sem("aggr_up")
        eps_up = sem("eps_up")
        rstd_up = sem("rstd_up")
        xn_up = sem("xn_up")
        z_up = sem("z_up")
        y1_up = sem("y1_up")
        yhi_up = sem("yhi_up")
        h0hi_up = sem("h0hi_up")
        ahi_up = sem("ahi_up")
        zhi_up = sem("zhi_up")
        xb_up = sem("xb_up")
        gate_up = sem("gate_up")
        l1p_up = sem("l1p_up")
        x_up = sem("x_up")
        ln_up = sem("ln_up")
        clamp_up = sem("clamp_up")
        pen_up = sem("pen_up")
        mask_up = sem("mask_up")
        qkhi_up = sem("qkhi_up")
        vhi_up = sem("vhi_up")
        vlo_up = sem("vlo_up")
        exp_up = sem("exp_up")
        rden_up = sem("rden_up")
        pn_up = sem("pn_up")
        phi_up = sem("phi_up")
        ohi_up = sem("ohi_up")
        hhi_up = sem("hhi_up")
        hlo_up = sem("hlo_up")
        shi_up = sem("shi_up")
        clo1_up = sem("clo1_up")
        pass_up = sem("pass_up")
        m3_up = sem("m3_up")
        one_up = sem("one_up")
        l3hi_up = sem("l3hi_up")
        hx_up = sem("hx_up")
        prod_up = sem("prod_up")
        att_up = sem("att_up")
        as_up = sem("as_up")
        am_up = sem("am_up")
        v_up = sem("v_up")
        e_up = sem("e_up")
        em_up = sem("em_up")
        p_up = sem("p_up")
        p_used = sem("p_used")
        den_up = sem("den_up")
        den_full = sem("den_full")
        rec_up = sem("rec_up")
        comb_lo_up = sem("comb_lo_up")
        comb_hi_up = sem("comb_hi_up")
        bn_up = sem("bn_up")
        bn_eps_up = sem("bn_eps_up")
        bn_rstd_up = sem("bn_rstd_up")
        sh_up = sem("sh_up")
        fn_up = sem("fn_up")
        stored = sem("stored")

        def ld_count(n):
            dmas = {S_COND + i: 5 for i in range(4)}
            for b in range(BLOCKS):
                dmas |= {S_BLK + b * S_PERBLK + PERBLK + i: 5 for i in range(4)}
            return sum(16 * dmas.get(i, 1) for i in range(n % STAGE, n + 1, STAGE))

        LD_PERBLK = ld_count(S_BLK + S_PERBLK) - ld_count(S_BLK)

        def ringpart(m):
            return ringw[:, m % RING, 0, :], ringw[:, m % RING, 1, :]

        def wait_apart(eng, semaphore, value):
            eng.wait_ge(semaphore, value)
            if not isinstance(value, int):
                eng.nop(nofuse=True)

        block = ctx.enter_context(nc.Block())

        def item_used(eng, n):
            j, st = divmod(n, NT)
            if st < NT - 1:
                eng.wait_ge(p_used, j * (NT - 1) + st + 1)
            else:
                eng.wait_ge(row_full, ROW3[f"P{j}b"] + 1)

        def pool_l3(g, rstd_of, rest):
            def item(i):
                rest(S_L3 + i, ringpart(RING_L3 + i))

            item(2)
            for t in range(NT):
                rstd_of(LN_L3 + t, t)
            item(3)
            g.wait_ge(row_full, ROWB + BLOCKS * len(BLOCK_ROW))
            for t in range(NT):
                g.tensor_scalar(mask[:, t, :], mask[:, t, :], DH ** -0.5, flag[:, 3, t:t + 1], ALU.mult, ALU.add).then_inc(m3_up, 1)
            g.memset(Hx[:, :, :, L3C:2 * L3C], 1.0).then_inc(one_up, 1)
            for i in range(KT):
                item(KT + i)
            for n in range(NJ * NT):
                j, st = divmod(n, NT)
                if st < NT - 1:
                    g.wait_ge(e_up, j * (NT - 1) + st + 1)
                else:
                    g.wait_ge(big_read, BIG3[f"va{j}"] + 1)
                m = mask[:, st, :] if j < L3H else maskT[:, st, :]
                g.tensor_tensor(ebuf[n % NE], ebuf[n % NE], m, ALU.add).then_inc(em_up, 1)
            for o in range(KT):
                g.wait_ge(bn_up, 3 * o + 3)
                g.tensor_scalar(bnc[:, 0, o:o + 1], mv3[:, o, 1:2], EPS, 1.0, ALU.add, ALU.mult).then_inc(bn_eps_up, 1)
                g.wait_ge(bn_eps_up, o + 1)
                g.tensor_tensor(bnc[:, 1, o:o + 1], bnc[:, 0, o:o + 1], half[:, 0:1], ALU.pow).then_inc(bn_rstd_up, 1)

        def act_l3(act, high, turned_relu):
            def item(i):
                high(S_L3 + i, ringpart(RING_L3 + i)[0])

            act.wait_ge(row_read, ROWB + BLOCKS * len(BLOCK_ROW))
            for i, n in enumerate(("L3_gnn_att_src_", "L3_gnn_att_dst_")):
                for d in range(2):
                    act.dma_start(bias[:, i, d * L3H * L3C:(d + 1) * L3H * L3C],
                                  a[n + "fb"[d]].rearrange("h c -> (h c)").partition_broadcast(P)).then_inc(bias_ld, 16)
            act.activation(l3pick, ident[0:2 * NJ, 0:2 * NJ], ACT.Copy).then_inc(l3hi_up, 1)
            act.activation(l3pair.rearrange("p (j c) -> p j c", j=NJ), ident[0:NJ, 0:NJ].unsqueeze(2).broadcast_to([NJ, NJ, L3C]),
                           ACT.Copy).then_inc(l3hi_up, 1)
            for t in range(NT):
                if t < 4:
                    item(2 + t)
                turned_relu(BIG3[f"l3_{t}"], 0, t)
            for t in range(NT):
                act.wait_ge(row_full, ROW3[f"H{t}"] + 1)
                act.activation(Hx[:, t, :, :].rearrange("p k (s c) -> p k s c", s=3)[:, :, 0:3:2, :],
                               brow(ROW3[f"H{t}"]).rearrange("p (k s c) -> p k s c", k=NJ // 2, s=2), ACT.Copy).then_inc(hx_up, 1)
            act.wait_ge(big_read, BIG3["mt0"])
            for t in range(NT):
                act.wait_ge(big_full, BIG3[f"mt{t}"] + 1)
                act.activation(maskT[:, t, :], bflat(BIG3[f"mt{t}"]), ACT.Copy).then_inc(big_read, 1)
            item(6)
            item(7)

            def rows_high(name, rows):
                act.wait_ge(big_full, BIG3[name] + 1)
                act.activation(l3rows[0:rows, 0, :], bflat(BIG3[name])[0:rows, :], ACT.Copy).then_inc(l3hi_up, 1)

            def sums(j):
                mine, other = (j % 2) * L3C, (1 - j % 2) * L3C
                act.wait_ge(row_full, ROW3[f"P{j}b"] + 1)
                if j >= 2:
                    act.wait_ge(den_full, j - 1)
                for h in range(2):
                    act.activation(den_row[h][other:other + 1], brow(ROW3[f"P{j}{'ab'[h]}"])[other:other + 1, 0:ROW_SPLIT[h]], ACT.Copy).then_inc(den_up, 1)
                for h in range(2):
                    act.activation(comb[mine:mine + L3C, j // 2, h * ROW_SPLIT[0]:h * ROW_SPLIT[0] + ROW_SPLIT[h]],
                                   brow(ROW3[f"P{j}{'ab'[h]}"])[mine:mine + L3C, 0:ROW_SPLIT[h]], ACT.Copy).then_inc(row_read, 1)

            rows_high("as", NJ)
            rows_high("vt", 2 * NJ)
            act.wait_ge(as_up, 2)

            def comb_high(k):
                act.wait_ge(big_read, BIG3[f"rb{k}"] + 1)
                act.activation(combT[:, 0, k, :], comb[:, k, :], ACT.Identity, bias=l3col[:, 0, k:k + 1]).then_inc(comb_hi_up, 1)

            for n in range(NJ * NT):
                j, st = divmod(n, NT)
                act.wait_ge(em_up, n + 1)
                act.activation(ebuf[n % NE], ebuf[n % NE], ACT.Exp, bias=l3s[:, 4, st, j:j + 1]).then_inc(p_up, 1)
                if st == 0 and j:
                    sums(j - 1)
            sums(NJ - 1)
            rows_high("rec", NJ)
            for k in range(KT):
                comb_high(k)
            for o in range(KT):
                act.wait_ge(sh_up, 3 * o + 3)
                act.activation(fT[:, o, :], fT[:, o, :], ACT.Relu, bias=bnc[:, 3, o:o + 1], scale=bnc[:, 2, o:o + 1]).then_inc(fn_up, 1)

        def pe_l3(pe, turn_norm):
            for t in range(NT):
                turn_norm(BIG3[f"l3_{t}"], XN_L3 + t, t)
            pe.wait_ge(split_done, S_L3 + KT)
            for t in range(NT):
                u = ROW3[f"H{t}"]
                free_row(pe, u)
                pe.wait_ge(big_read, BIG3[f"l3_{t}"] + 1)
                w = L3H * L3C
                for d in range(2):
                    def weight(k):
                        return [r[:, (k % 2) * w:(k % 2 + 1) * w] for r in ringpart(RING_L3 + 2 * d + k // 2)]
                    ins = row_mm(pe, brow(u)[:, d * w:(d + 1) * w], sum([parts(tile_of(yT, k, t), weight(k)) for k in range(KT)], []))
                ins.then_inc(row_full, 1)
            pe.wait_ge(m3_up, NT)
            for t in range(NT):
                u = BIG3[f"mt{t}"]
                free_big(pe, u)
                for st in range(NT):
                    ins = pe.transpose(bflat(u)[:, st * P:(st + 1) * P], mask[:, st, t * P:(t + 1) * P], ident[:, :])
                ins.then_inc(big_full, 1)
            u = BIG3["as"]
            free_big(pe, u)
            pe.wait_ge(att_up, 2 * NT)
            for t in range(NT):
                ins = pe.transpose(bflat(u)[0:NJ, t * P:(t + 1) * P], l3s[:, 0, t, :], ident[:, :])
            ins.then_inc(big_full, 1)
            pe.wait_ge(big_read, u + 1)

            def spread(u, i, n):
                free_big(pe, u)
                pick = l3pick[0:n, i:i + 1].broadcast_to([n, P])
                wide_mm(pe, u, [(pick, l3rows[0:n, part, :]) for part in range(2)]).then_inc(big_full, 1)

            for j in range(NJ):
                spread(BIG3[f"am{j}"], j, NJ)
            u = BIG3["vt"]
            free_big(pe, u)
            pe.wait_ge(v_up, 2)
            for t in range(NT):
                ins = pe.transpose(bflat(u)[0:2 * NJ, t * P:(t + 1) * P], l3v[:, t, :], ident[:, :])
            ins.then_inc(big_full, 1)
            pe.wait_ge(big_read, u + 1)
            pe.wait_ge(one_up, 1)

            def den_turn(j):
                at = (1 - j % 2) * L3C
                pe.wait_ge(den_up, 2 * j + 2)
                pe.wait_ge(row_read, ROW3[f"P{j}b"] + 1)
                for t in range(NT):
                    h, c = (0, t * P) if t < 3 else (1, t * P - ROW_SPLIT[0])
                    ins = pe.matmul(den_col[:, t * NJ + j:t * NJ + j + 1], den_row[h][at:at + 1, c:c + P], ident[at:at + 1, at:at + 1],
                                    start=True, stop=True, skip_group_check=True)
                ins.then_inc(den_full, 1)

            spread(BIG3["vb0"], NJ, 2 * NJ)
            spread(BIG3["vb1"], NJ + 1, 2 * NJ)
            spread(BIG3["va0"], 0, 2 * NJ)
            for n in range(NJ * NT):
                j, st = divmod(n, NT)
                if st == 0:
                    if j + 2 < NJ:
                        spread(BIG3[f"vb{j + 2}"], NJ + j + 2, 2 * NJ)
                    if j + 1 < NJ:
                        spread(BIG3[f"va{j + 1}"], j + 1, 2 * NJ)
                    free_row(pe, ROW3[f"P{j}b"])
                    if j:
                        den_turn(j - 1)
                pe.wait_ge(p_up, n + 1)
                lhs = Hx[:, st, j // 2, (j % 2) * L3C:(j % 2 + 2) * L3C]
                for h in range(2):
                    lo = h * ROW_SPLIT[0]
                    ins = pe.matmul(brow(ROW3[f"P{j}{'ab'[h]}"])[:, 0:ROW_SPLIT[h]], lhs, ebuf[n % NE][:, lo:lo + ROW_SPLIT[h]],
                                    start=(st == 0), stop=(st == NT - 1))
                ins.then_inc(*((p_used, 1) if st < NT - 1 else (row_full, 2)))
            den_turn(NJ - 1)
            u = BIG3["rec"]
            free_big(pe, u)
            pe.wait_ge(rec_up, 2)
            for t in range(NT):
                ins = pe.transpose(bflat(u)[0:NJ, t * P:(t + 1) * P], l3s[:, 2, t, :], ident[:, :])
            ins.then_inc(big_full, 1)
            pe.wait_ge(big_read, u + 1)
            for k in range(KT):
                u = BIG3[f"rb{k}"]
                free_big(pe, u)
                wide_mm(pe, u, [(l3pair[:, k * P:(k + 1) * P], l3rows[0:NJ, part, :]) for part in range(2)]).then_inc(big_full, 1)
            for o in range(KT):
                u = BIG3[f"f{o}"]
                free_big(pe, u)
                pe.wait_ge(comb_lo_up, KT)
                pe.wait_ge(split_done, S_L3 + KT + o + 1)
                wide_mm(pe, u, sum([parts(wcol(RING_L3 + KT + o, k), both(combT, k)) for k in range(KT)], [])).then_inc(big_full, 1)
            pe.wait_ge(fn_up, KT)
            for t in range(NT):
                u = ROW3[f"y{t}"]
                free_row(pe, u)
                for o in range(KT):
                    ins = pe.transpose(brow(u)[:, o * P:(o + 1) * P], fT[:, o, t * P:(t + 1) * P], ident[:, :])
                ins.then_inc(row_full, 1)

        def dve_l3(dve, tile_stats, relu_norm, step):
            f32 = lambda ap: ap.bitcast(F32)
            for t in range(NT):
                dve.wait_ge(x_up, NT + t + 1)
                tile_stats(LN_L3 + t, t, x[:, t, :])
            relu_norm(LN_L3, 0, [BIG3[f"l3_{t}"] for t in range(NT)], 2 * NT + BLOCKS * 2 * NT)
            dve.wait_ge(bias_ld, 48 * BLOCKS + 64)
            for t in range(NT):
                u = ROW3[f"H{t}"]
                dve.wait_ge(hx_up, t + 1)
                if t:
                    dve.wait_ge(att_up, 2 * t)
                for i in range(2):
                    dve.tensor_tensor(ebuf[i][:, 0:D], brow(u), bias[:, i, :], ALU.mult).then_inc(*((row_read, 1) if i else (prod_up, 1)))
                dve.wait_ge(prod_up, t + 1)
                dve.wait_ge(row_read, u + 1)
                for i in range(2):
                    dve.tensor_reduce(l3s[:, i, t, :], ebuf[i][:, 0:D].rearrange("p (j c) -> p j c", j=NJ), AX.X, ALU.add).then_inc(att_up, 1)
            dve.wait_ge(att_up, 2 * NT)
            dve.tensor_scalar(l3s[:, 3, :, :], l3s[:, 0, :, :], 0.8, None, ALU.mult).then_inc(as_up, 1)
            dve.tensor_scalar(l3s[:, 4, :, :], l3s[:, 0, :, :], 0.2, None, ALU.mult).then_inc(as_up, 1)

            def rows_rest(name, rows, nth):
                u = BIG3[name]
                dve.wait_ge(big_read, u)
                dve.wait_ge(l3hi_up, nth)
                dve.tensor_tensor(l3rows[0:rows, 1, :], bflat(u)[0:rows, :], f32(l3rows[0:rows, 0, :]), ALU.subtract).then_inc(big_read, 1)

            rows_rest("as", NJ, 3)
            dve.wait_ge(m3_up, NT)
            for j in range(NJ):
                u = BIG3[f"am{j}"]
                dve.wait_ge(big_full, u + 1)
                if j:
                    dve.wait_ge(big_read, u)
                for t in range(NT):
                    if t >= 3:
                        dve.wait_ge(am_up, j * (NT - 1) + t - 2)
                    m = maskT[:, t, :] if j < L3H else mask[:, t, :]
                    ins = dve.tensor_tensor_reduce(wide(ebuf[t % 3]), bwide(u), wide(m), 1.0, -3e38, ALU.add, ALU.max, l3s[:, 2, t, j:j + 1])
                    ins.then_inc(*((am_up, 1) if t < NT - 1 else (big_read, 1)))
            dve.wait_ge(big_read, BIG3[f"am{NJ - 1}"] + 1)
            step(dve.tensor_tensor(l3s[:, 2, :, :], l3s[:, 2, :, :], l3s[:, 1, :, :], ALU.add))
            step(dve.scalar_tensor_tensor(l3s[:, 2, :, :], l3s[:, 2, :, :], 0.2, l3s[:, 2, :, :], ALU.mult, ALU.max))
            dve.tensor_tensor(l3v[:, :, 0:NJ], l3s[:, 1, :, :], l3s[:, 2, :, :], ALU.subtract).then_inc(v_up, 1)
            dve.scalar_tensor_tensor(l3v[:, :, NJ:2 * NJ], l3s[:, 1, :, :], 0.2, l3s[:, 2, :, :], ALU.mult, ALU.subtract).then_inc(v_up, 1)
            rows_rest("vt", 2 * NJ, 4)
            dve.wait_ge(split_done, S_L3 + 2 * KT)

            def comb_rest(k):
                dve.wait_ge(comb_hi_up, k + 1)
                dve.scalar_tensor_tensor(combT[:, 1, k, :], comb[:, k, :], l3col[:, 0, k:k + 1], f32(combT[:, 0, k, :]),
                                         ALU.add, ALU.subtract).then_inc(comb_lo_up, 1)

            def second_branch(j):
                u = BIG3[f"vb{j}"]
                dve.wait_ge(big_full, u + 1)
                if j >= 2:
                    dve.wait_ge(big_read, BIG3[f"va{j - 2}"] + 1)
                dve.tensor_copy(wide(vbrow[j % 2]), bwide(u)).then_inc(big_read, 1)

            second_branch(0)
            for n in range(NJ * NT):
                j, st = divmod(n, NT)
                u = BIG3[f"va{j}"]
                if st == 0:
                    if j < NJ - 1:
                        second_branch(j + 1)
                    dve.wait_ge(big_full, u + 1)
                    dve.wait_ge(big_read, BIG3[f"vb{j}"] + 1)
                if n >= NE:
                    item_used(dve, n - NE)
                ins = dve.scalar_tensor_tensor(wide(ebuf[n % NE]), bwide(u), l3s[:, 3, st, j:j + 1], wide(vbrow[j % 2]), ALU.add, ALU.max)
                ins.then_inc(*((e_up, 1) if st < NT - 1 else (big_read, 1)))
            dve.wait_ge(den_full, NJ)
            sums = l3s[:, 2, :, :].rearrange("p t j -> p (t j)")
            dve.tensor_scalar(sums, den_col, 1e-16, None, ALU.add).then_inc(rec_up, 1)
            dve.wait_ge(rec_up, 1)
            dve.reciprocal(sums, sums).then_inc(rec_up, 1)
            rows_rest("rec", NJ, 5)
            for k in range(KT + 1):
                if k < KT:
                    u = BIG3[f"rb{k}"]
                    dve.wait_ge(big_full, u + 1)
                    dve.wait_ge(row_read, ROW3[f"P{2 * k + 1}b"] + 1)
                    dve.tensor_tensor(wide(comb[:, k, :]), bwide(u), wide(comb[:, k, :]), ALU.mult).then_inc(big_read, 1)
                if k:
                    comb_rest(k - 1)
            for o in range(KT):
                u = BIG3[f"f{o}"]
                dve.wait_ge(big_full, u + 1)
                dve.tensor_scalar(wide(fT[:, o, :]), bwide(u), l3col[:, 1, o:o + 1], None, ALU.add).then_inc(big_read, 1)
                dve.wait_ge(big_read, u + 1)
                for i, (lo, hi) in enumerate(((0, HALF), (HALF, N))):
                    dve.bn_stats(bn3[:, o, i, :], fT[:, o, lo:hi]).then_inc(bn_up, 1)
                dve.wait_ge(bn_up, 3 * o + 2)
                dve.bn_aggr(mv3[:, o, :], bn3[:, o, :, :]).then_inc(bn_up, 1)
                dve.wait_ge(bn_up, 3 * o + 3)
                dve.wait_ge(bn_rstd_up, o + 1)
                dve.tensor_tensor(bnc[:, 2, o:o + 1], bnc[:, 1, o:o + 1], l3col[:, 2, o:o + 1], ALU.mult).then_inc(sh_up, 1)
                dve.wait_ge(sh_up, 3 * o + 1)
                dve.tensor_tensor(bnc[:, 3, o:o + 1], mv3[:, o, 0:1], bnc[:, 2, o:o + 1], ALU.mult).then_inc(sh_up, 1)
                dve.wait_ge(sh_up, 3 * o + 2)
                dve.tensor_tensor(bnc[:, 3, o:o + 1], l3col[:, 3, o:o + 1], bnc[:, 3, o:o + 1], ALU.subtract).then_inc(sh_up, 1)
            for t in range(NT):
                u = ROW3[f"y{t}"]
                dve.wait_ge(row_full, u + 1)
                dve.tensor_tensor(x[:, t, :], x[:, t, :], brow(u), ALU.add).then_inc(row_read, 1)

        def finish(sp):
            for t in range(NT):
                sp.wait_ge(row_read, ROW3[f"y{t}"] + 1)
                rows = TAIL if t == NT - 1 else P
                sp.dma_start(out[t * P:t * P + rows, :], x[0:rows, t, :]).then_inc(stored, 16)
            sp.wait_ge(stored, 16 * NT)

        @block.sync
        def _(sp):
            full = (NG - 1) * GROUP
            dst_to = edge[:, 1, :].bitcast(I32)
            sp.dma_start(dst_to[NG - 1:NG, ELAST:GROUP], a["dst"][E - (GROUP - ELAST):E].rearrange("(o e) -> o e", o=1)).then_inc(e_ld, 16)
            for i, lst in ((1, a["dst"]), (0, a["src"]), (2, a["edge_weight"])):
                if i == 0:
                    sp.wait_ge(e_clear, 2)
                to = edge[:, i, :] if i == 2 else edge[:, i, :].bitcast(I32)
                sp.dma_start(to[0:NG - 1, :], lst[0:full].rearrange("(g e) -> g e", e=GROUP)).then_inc(e_ld, 16)
                sp.dma_start(to[NG - 1:NG, 0:ELAST], lst[full:E].rearrange("(o e) -> o e", o=1)).then_inc(e_ld, 16)
            sp.wait_ge(x_clear, 1)
            sp.dma_start(x[:, 0:NT - 1, :], a["x"][0:(NT - 1) * P, :].rearrange("(t p) d -> p t d", p=P)).then_inc(x_ld, 16)
            sp.dma_start(x[0:TAIL, NT - 1, :], a["x"][(NT - 1) * P:N, :]).then_inc(x_ld, 16)

            def stage(n, src, it=0):
                if n >= STAGE:
                    sp.wait_ge(split_done, n - STAGE + 1 + it * S_PERBLK)
                to = raw[:, n % STAGE, :]
                if len(src.shape) == 3:
                    to = to.rearrange("p (k c) -> p k c", k=src.shape[1])
                sp.dma_start(to, src).then_inc(raw_ld[n % STAGE], 16)

            def stage_cond(n, w, b, it=0):
                sp.wait_ge(split_done, n - STAGE + 1 + it * S_PERBLK)
                for i in range(4):
                    sp.dma_start(raw[32 * i:32 * i + C16, n % STAGE, :], w).then_inc(raw_ld[n % STAGE], 16)
                sp.dma_start(raw[C16:P:32, n % STAGE, :], b.unsqueeze(0).broadcast_to([4, D])).then_inc(raw_ld[n % STAGE], 16)

            def columns(w, h):
                return w[:, h * P:(h + 1) * P].rearrange("(k p) c -> p k c", p=P)

            conds = [(a["L2_gnn_s1_w"], a["L2_gnn_s1_b"]), (a["L2_gnn_b1_w"], a["L2_gnn_b1_b"]),
                     (a["L2_gnn_s2_w"], a["L2_gnn_s2_b"]), (a["L2_gnn_b2_w"], a["L2_gnn_b2_b"])]
            by_col = {WQ: a["L2_gnn_wq"], WK: a["L2_gnn_wk"], W1: a["L2_gnn_m_w1"]}
            by_row = {WV: a["L2_gnn_wv"], WO: a["L2_gnn_wo"], W2: a["L2_gnn_m_w2"]}

            stage(Q_CONV, columns(a["L0_gnn_W_conv"], 0))
            stage(Q_LIN, a["L0_gnn_W_lin"])
            v0 = 0
            for b in ("bq", "bk", "m_b1"):
                sp.dma_start(vec[v0:v0 + BLOCKS * KT, :], a["L2_gnn_" + b].rearrange("b (k p) -> (b k) p", p=P)).then_inc(vec_ld, 16)
                v0 += BLOCKS * KT
            for b in ("L3_gnn_bias_f", "L3_gnn_bias_b", "L3_gnn_b_fuse", "L3_gnn_bn_gamma", "L3_gnn_bn_beta", "L0_gnn_b_conv"):
                v = a[b].rearrange("(k p) -> k p", p=P)
                sp.dma_start(vec[v0:v0 + v.shape[0], :], v).then_inc(vec_ld, 16)
                v0 += v.shape[0]
            assert v0 == VECS
            sp.dma_start(bias[:, 0, :], a["L0_gnn_b_lin"].partition_broadcast(P)).then_inc(col_ld, 16)
            sp.dma_start(bias[:, 1, :], a["L1_gnn_b"].partition_broadcast(P)).then_inc(col_ld, 16)
            for k in range(KT):
                stage(Q_L + k, a["L1_gnn_W_l"][k * P:(k + 1) * P, :])
            for k in range(KT):
                stage(Q_R + k, a["L1_gnn_W_r"][k * P:(k + 1) * P, :])
            with sp.Fori(0, BLOCKS) as it:
                for i, (w, b) in enumerate(conds):
                    stage_cond(S_COND + i, w[it], b[it], it)
                for q in (WQ, WK, WV, WO, W1, W2):
                    for i in range(KT):
                        src = columns(by_col[q][it], i) if q in by_col else by_row[q][it][i * P:(i + 1) * P, :]
                        stage(S_BLK + q + i, src, it)
            for i, (w, b) in enumerate(conds):
                stage_cond(S_L3 - 4 + i, w[BLOCKS - 1], b[BLOCKS - 1])
            for i, w in enumerate((a["L3_gnn_W_f"], a["L3_gnn_W_b"])):
                for j in range(2):
                    stage(S_L3 + 2 * i + j, w[2 * j * P:2 * (j + 1) * P].rearrange("(k p) h c -> p k (h c)", p=P))
            for i in range(KT):
                stage(S_L3 + KT + i, columns(a["L3_gnn_W_fuse"], i))
            finish(sp)

        def pool_l2(g, rstd_of, rest, rest_cond):
            for i in range(4):
                rest_cond(S_COND + i, i, i, behind=LN_IN + i - 1 if i else None)
                rstd_of(LN_IN + i, i)
            rstd_of(LN_IN + NT - 1, NT - 1)
            for i in range(2):
                rest(S_BLK + i, ringpart(RING_BLK + i))
            for t in range(NT):
                rstd_of(LN_BLK + t, NT + t)
            with g.Fori(0, BLOCKS) as it:
                def rests(q, first, last):
                    for i in range(first, last):
                        rest(S_BLK + q + i, ringpart(RING_BLK + q + i), it)

                def add_bias(ln, t, b):
                    g.wait_ge(xn_up, LN_BLK + it * 2 * NT + ln * NT + t + 1)
                    g.tensor_tensor(z[:, t, :], z[:, t, :], bias[:, b, :], ALU.add).then_inc(xb_up, 1)

                rests(WQ, 2, KT)
                rests(WK, 0, 2)
                g.wait_ge(bias_ld, 48 * it + 48)
                for t in range(NT):
                    add_bias(0, t, 1)
                rests(WK, 2, KT)
                rests(WV, 0, KT)
                rests(WO, 0, 2)
                for t in range(NT):
                    g.wait_ge(vhi_up, it * NT + t + 1)
                    g.tensor_tensor(vrow[:, 1, t, :], vbuf[:, t % 2, :], vrow[:, 0, t, :].bitcast(F32), ALU.subtract).then_inc(vlo_up, 1)
                for k in range(HEADS * NT):
                    wait_apart(g, rden_up, it * HEADS * NT + k + 1)
                    g.tensor_scalar(pbuf[:, k % 4, :], pbuf[:, k % 4, :], rden[:, k:k + 1], flag[:, 1, k % NT:k % NT + 1],
                                    ALU.mult, ALU.mult).then_inc(pn_up, 1)
                    if k in IN_HEADS:
                        i = IN_HEADS.index(k)
                        rests(WO if i < 2 else W1, (i + 2) % KT, (i + 2) % KT + 1)
                for t in range(NT):
                    rstd_of(LN_BLK + it * 2 * NT + NT + t, t)
                rests(W1, 2, KT)
                for t in range(NT):
                    add_bias(1, t, 2)
                    if t in (1, 2):
                        rests(W2, t - 1, t)
                rests(W2, 2, KT)
                for i in range(4):
                    tile = LN_BLK + (it + 1) * 2 * NT + i
                    rest_cond(S_BLK + PERBLK + i, i, 4 + i, it, behind=tile - 2 if i >= 2 else None)
                    if i >= 1:
                        rstd_of(tile - 1, NT + i - 1)
                for i in range(2):
                    rest(S_BLK + S_PERBLK + i, ringpart(RING_BLK + i), it)
                    rstd_of(LN_BLK + (it + 1) * 2 * NT + 3 + i, NT + 3 + i)

        @block.gpsimd
        def _(g):
            own = [0]

            def step(ins):
                own[0] += 1
                ins.then_inc(gstep, 1)
                g.wait_ge(gstep, own[0])

            step(g.memset(ident[:, :], 0.0))
            g.affine_select(out=ident[:, :], in_=ident[:, :], compare_op=ALU.not_equal, fill=1.0, base=0,
                            pattern=[[-1, P]], channel_multiplier=1).then_inc(const0, 1)
            g.memset(ones[:, :], 1.0).then_inc(const0, 1)
            step(g.memset(half[:, :], -0.5))
            g.iota(iota16[:, :], [[1, NP]], base=0, channel_multiplier=0,
                   allow_small_or_imprecise_dtypes=True).then_inc(const0, 1)
            step(g.memset(fcol[:, :], 0.0))
            g.iota(fcol[0:NF, 0:1].bitcast(I32), [[1, 1]], base=1, channel_multiplier=1).then_inc(const1, 1)
            g.wait_ge(const1, 1)
            g.iota(fcol[NF:2 * NF, 0:1].bitcast(I32), [[1, 1]], base=1, channel_multiplier=1).then_inc(const1, 1)
            g.wait_ge(const1, 2)
            g.memset(tmp64[0][:, N:NP], 0.0).then_inc(const1, 1)
            g.wait_ge(const1, 3)
            g.memset(f_w2[:, :], 0.0).then_inc(const1, 1)
            g.memset(acc[:, 0:NT * ACCW], 0.0).then_inc(scat_read, HOT)
            g.memset(acc[:, NT * ACCW:2 * NT * ACCW], 0.0).then_inc(scat_full, HOT)
            g.wait_ge(f_ld, 16 * F_LOADS)
            for i in range(4):
                if i:
                    g.wait_ge(cb_one, i)
                g.affine_select(out=fcol[:, 2:3], in_=fcol[:, 2:3], compare_op=ALU.not_equal, fill=1.0,
                                base=-(32 * i + C16), pattern=[[0, 1]], channel_multiplier=1).then_inc(cb_one, 1)

            def rstd_of(i, slot):
                wait_apart(g, aggr_up, i + 1)
                g.tensor_scalar(veps[:, slot:slot + 1], mv[:, slot, 1:2], EPS, 1.0, ALU.add, ALU.mult).then_inc(eps_up, 1)
                g.wait_ge(eps_up, i + 1)
                g.tensor_tensor(rstd[:, slot:slot + 1], veps[:, slot:slot + 1], half[:, 0:1], ALU.pow).then_inc(rstd_up, 1)

            def rest(n, to, it=0):
                g.wait_ge(shi_up, n + 1 + it * S_PERBLK)
                g.tensor_tensor(to[1], raw[:, n % STAGE, :], to[0].bitcast(F32), ALU.subtract).then_inc(split_done, 1)

            def rest_cond(n, kind, nth, it=0, behind=None):
                if behind is None:
                    g.wait_ge(split_done, n + it * S_PERBLK)
                else:
                    g.wait_ge(rstd_up, behind + 1)
                r = raw[:, n % STAGE, :]
                to = condw[:, kind, :]
                g.wait_ge(shi_up, n + 1 + it * S_PERBLK)
                for lo in (32, 96):
                    ins = g.tensor_tensor(to[lo:lo + 32, :], r[lo:lo + 32, :], to[lo:lo + 32, :].bitcast(F32), ALU.subtract)
                    if lo == 32:
                        ins.then_inc(clo1_up, 1)
                        g.wait_ge(clo1_up, nth + 1 + it * 4)
                ins.then_inc(split_done, 1)
                g.wait_ge(split_done, n + 1 + it * S_PERBLK)

            for t in range(NT):
                rstd_of(t, t)
            for m in range(2):
                rest(m, ringpart(m))
            g.wait_ge(w_ready, 2)
            passes = g.value_load(span_i[0:1, 1:2], min_val=0, max_val=NP // WIN)
            with g.Fori(0, passes + 1) as kp:
                with g.Fori(0, NG // HOT) as gi:
                    for b in range(HOT):
                        gr = gi * HOT + b
                        c = kp * NG + gr + 1
                        hot = hot_dst[:, b, :, 0:WIN]
                        g.wait_ge(hot_dst_up, c)
                        for i in range(3):
                            ins = g.tensor_tensor(
                                hot_dst[:, b, :, (i + 1) * WIN:(i + 2) * WIN], hot,
                                w_part[:, i, :, bass.ds(gr, 1)].broadcast_to([P, CH, WIN]), ALU.mult)
                        ins.then_inc(hot_w_up, 1)
            g.wait_ge(w_up, 1)
            g.tensor_tensor(degs[:, 2, :], degs[:, 1, :], half[:, :], ALU.pow).then_inc(dpow_up, 1)
            for m in range(2, 4):
                rest(m, ringpart(m))
            for t in range(NT):
                g.wait_ge(xn_up, t + 1)
                g.wait_ge(row_read, ROW0["brow"] + 1)
                g.tensor_tensor(x[:, t, :], x[:, t, :], bias[:, 0, :], ALU.add).then_inc(xb_up, 1)
            for m in range(4, RING + 1):
                rest(m, ringpart(m))
            for t in range(NT):
                rstd_of(LN_L1 + t, NT + t)
            for m in range(RING + 1, RING_BLK):
                rest(m, ringpart(m))
            pool_l2(g, rstd_of, rest, rest_cond)
            pool_l3(g, rstd_of, rest)

        def act_l2(act, high):
            with act.Fori(0, BLOCKS) as it:
                nb, nr = it * len(BLOCK_BIG), it * len(BLOCK_ROW)

                def highs(q, first, last):
                    for i in range(first, last):
                        high(S_BLK + q + i, ringpart(RING_BLK + q + i)[0], it)

                def turned(ln, t):
                    u = BIGBLK[f"t{ln}_{t}"]
                    act.wait_ge(big_full, u + nb + 1)
                    act.activation(yT[:, 0, :, t * P:(t + 1) * P], bflat(u)[:, 0:D].rearrange("p (k n) -> p k n", k=KT),
                                   ACT.Copy).then_inc(yhi_up, 1)

                act.wait_ge(row_read, ROWB + nr)
                for i, b in enumerate(("bv", "bo", "m_b2")):
                    act.dma_start(bias[:, i, :], a["L2_gnn_" + b][it].partition_broadcast(P)).then_inc(bias_ld, 16)
                for t in range(NT):
                    if t < 4:
                        highs((WQ, WK)[t // 2], (t + 2) % KT, (t + 2) % KT + 1)
                    turned(0, t)
                for i, to in enumerate((qT, kT)):
                    for h in range(HEADS):
                        u = BIGBLK["qk"[i] + str(h)]
                        act.wait_ge(big_full, u + nb + 1)
                        act.activation(wide(to[:, 0, h, :]), bwide(u), ACT.Identity,
                                       bias=bqk[:, i, bass.ds(it * KT + h, 1)]).then_inc(qkhi_up, 1)
                        n = i * HEADS + h + 2
                        highs((WK, WV, WO)[n // KT], n % KT, n % KT + 1)
                for t in range(NT):
                    act.wait_ge(big_read, BIGBLK[f"v{t}"] + nb + 1)
                    act.activation(vrow[:, 0, t, :], vbuf[:, t % 2, :], ACT.Copy).then_inc(vhi_up, 1)
                for what, k in ATT_ACT:
                    if what == "S":
                        act.wait_ge(big_read, BIGBLK[f"S{k}"] + nb + 1)
                        act.activation(pbuf[:, k % 4, :], pbuf[:, k % 4, :], ACT.Exp, bias=nsmax[:, k:k + 1],
                                       scale=-1.0, accum_out=den[:, k:k + 1]).then_inc(exp_up, 1)
                        if k in IN_HEADS:
                            i = IN_HEADS.index(k)
                            highs(WO if i < 2 else W1, (i + 2) % KT, (i + 2) % KT + 1)
                    elif what == "T":
                        u = BIGBLK[f"T{k}"]
                        act.wait_ge(big_full, u + nb + 1)
                        act.activation(pT[:, 0, :, (k % NT) * P:(k % NT + 1) * P], bflat(u).rearrange("p (k n) -> p k n", k=NT),
                                       ACT.Copy).then_inc(phi_up, 1)
                    else:
                        u = BIGBLK[f"PV{k}"]
                        act.wait_ge(big_full, u + nb + 1)
                        act.activation(wide(qT[:, 0, k, :]), bwide(u), ACT.Copy).then_inc(ohi_up, 1)
                for t in range(NT):
                    turned(1, t)
                    if t == 2:
                        act.wait_ge(row_full, ROWBLK["wo4"] + nr + 1)
                    if t >= 2:
                        highs((W1, W1, W2)[t - 2], (2, 3, 0)[t - 2], (3, 4, 1)[t - 2])
                highs(W2, 1, 2)
                for o in range(KT):
                    act.wait_ge(big_read, BIGBLK[f"m{o}"] + nb + 1)
                    act.activation(kT[:, 0, o, :], rbuf[:, o % 2, :], ACT.Copy).then_inc(hhi_up, 1)
                    if o < 2:
                        highs(W2, 2 + o, 3 + o)
                    else:
                        for i in (2 * o - 4, 2 * o - 3):
                            high(S_BLK + PERBLK + i, condw[:, i, :], it)
                for i in range(2):
                    high(S_BLK + S_PERBLK + i, ringpart(RING_BLK + i)[0], it)

        @block.scalar
        def _(act):
            def high(n, to, it=0):
                act.wait_ge(raw_ld[n % STAGE], ld_count(n) + it * LD_PERBLK)
                act.activation(to, raw[:, n % STAGE, :], ACT.Copy).then_inc(shi_up, 1)

            act.wait_ge(const1, 4)
            act.dma_start(tmp64[0][:, 0:N], a["node_vec1"].rearrange("n o -> o n").broadcast_to([2 * NF, N])).then_inc(f_ld, 16)
            act.dma_start(f_w1[:, :], a["L2_gnn_f_w1"]).then_inc(f_ld, 16)
            act.dma_start(fcol[0:C16, 3:4], a["L2_gnn_f_b1"].unsqueeze(1)).then_inc(f_ld, 16)
            for i in range(4):
                act.dma_start(f_w2[:, 32 * i:32 * i + C16], a["L2_gnn_f_w2"]).then_inc(f_ld, 16)
                act.dma_start(fcol[32 * i:32 * i + C16, 2:3], a["L2_gnn_f_b2"].unsqueeze(1)).then_inc(f_ld, 16)
            for m in range(2):
                high(m, ringpart(m)[0])
            act.wait_ge(emb_up, 1)
            act.activation(tmp64[4], tmp64[3], ACT.Sin).then_inc(sin_done, 1)

            def turned_relu(u, i, t):
                act.wait_ge(big_full, u + 1)
                act.activation(yT[:, 0, :, t * P:(t + 1) * P], bflat(u)[:, 0:D].rearrange("p (k n) -> p k n", k=KT),
                               ACT.Relu).then_inc(yhi_up, 1)

            for t in range(NT):
                turned_relu(BIG0[f"l0_{t}"], t, t)
            act.wait_ge(big_read, BIG0["z1"] + 1)
            act.activation(mask[0:C16, 2, :], mask[0:C16, 1, :], ACT.Sigmoid).then_inc(sig_done, 1)
            act.wait_ge(big_full, BIG0["hall"] + 1)
            act.activation(h0[:, 0, :, :], bflat(BIG0["hall"]).rearrange("p (t n) -> p t n", t=NT), ACT.Copy).then_inc(h0hi_up, 1)
            for m in range(2, 4):
                high(m, ringpart(m)[0])
            act.wait_ge(condT_up, 2)
            act.wait_ge(w_ready, 2)
            passes = act.value_load(span_i[0:1, 1:2], min_val=0, max_val=NP // WIN)
            with act.Fori(0, passes + 1) as kp:
                with act.Fori(0, NG // HOT) as gi:
                    for b in range(HOT):
                        g = gi * HOT + b
                        act.wait_ge(scat_full, kp * NG + g + 1)
                        act.activation(hot_abs[b % 2], iota16[:, :], ACT.Abs, bias=src_col[:, CH - 1, bass.ds(g, 1)], scale=-1.0).then_inc(hot_abs_up, 1)
                        act.wait_ge(hot_abs_up, kp * NG + g + 1)
                        act.activation(hot_src[b][:, CH - 1, :], hot_abs[b % 2], ACT.Relu, bias=1.0, scale=-1.0).then_inc(hot_act_up, 1)
            act.wait_ge(dinv_up, 1)
            for t in range(NT):
                act.activation(adj[:, 0, t, :], w_acc[:, t, :], ACT.Copy, scale=degs[:, 3, t:t + 1]).then_inc(whi_up, 1)
            for m in range(4, RING):
                high(m, ringpart(m)[0])
            act.wait_ge(big_full, BIG0["agg"] + 1)
            act.activation(wide(aT[:, 0, :]), bwide(BIG0["agg"]), ACT.Copy).then_inc(ahi_up, 1)
            high(RING, ringpart(RING)[0])
            for t in range(NT):
                act.activation(adj[:, 0, t, :], cnt_acc[:, t, :], ACT.Copy,
                               accum_out=flag[:, 0, t:t + 1]).then_inc(chi_up, 1)
            act.wait_ge(row_full, ROW0["o4"] + 1)
            high(RING + 1, ringpart(RING + 1)[0])
            for t in range(NT):
                turned_relu(BIG0[f"l1_{t}"], NT + t, t)
            for t in range(NT):
                act.wait_ge(row_full, ROW0[f"z{t}"] + 1)
                act.activation(vrow[:, 0, t, :], brow(ROW0[f"z{t}"]), ACT.Copy).then_inc(zhi_up, 1)
                if t == NT - 1:
                    for m in range(RING + 2, RING_BLK):
                        high(m, ringpart(m)[0])
                act.wait_ge(clamp_up, t + 1)
                act.activation(mask[:, t, :], mask[:, t, :], ACT.Ln).then_inc(ln_up, 1)
            for t in range(NT):
                if t:
                    high(S_COND + t - 1, condw[:, t - 1, :])
                act.wait_ge(row_read, ROW0[f"a{t}"] + 1)
                if t >= 2:
                    act.wait_ge(l1p_up, t - 1)
                act.activation(sg[:, t % 2, :], t2[:, t % 2, :], ACT.Sigmoid).then_inc(gate_up, 1)
            for i in range(2):
                high(S_BLK + i, ringpart(RING_BLK + i)[0])
            act_l2(act, high)
            act_l3(act, high, turned_relu)

        def wide_mm(pe, u, terms):
            for i, (l, r) in enumerate(terms):
                for h in range(2):
                    ins = pe.matmul(big[u % NBIG][:, h, 0:HALF], l, r[:, h * HALF:(h + 1) * HALF],
                                    start=(i == 0), stop=(i == len(terms) - 1))
            return ins

        def row_mm(pe, to, terms):
            for i, (l, r) in enumerate(terms):
                ins = pe.matmul(to, l, r, start=(i == 0), stop=(i == len(terms) - 1))
            return ins

        def parts(l, r):
            return [(l[0], r[0]), (l[0], r[1]), (l[1], r[0])]

        def free_big(pe, u, it=0):
            if u >= NBIG:
                pe.wait_ge(big_read, u - NBIG + 1 + it)

        def free_row(pe, u, it=0):
            if u >= NROW:
                pe.wait_ge(row_read, u - NROW + 1 + it)

        def turn(pe, u, src, n):
            for k in range(n):
                ins = pe.transpose(bflat(u)[:, k * P:(k + 1) * P], src[:, k * P:(k + 1) * P], ident[:, :])
            return ins

        def wcol(m, k):
            return [w[:, k * P:(k + 1) * P] for w in ringpart(m)]

        def tile_of(t2, k, t):
            return [t2[:, s, k, t * P:(t + 1) * P] for s in range(2)]

        def both(t2, k):
            return [t2[:, s, k, :] for s in range(2)]

        def pe_l2(pe):
            pe.wait_ge(condT_up, 2)
            with pe.Fori(0, BLOCKS) as it:
                nb, nr, ns = it * len(BLOCK_BIG), it * len(BLOCK_ROW), it * S_PERBLK

                def cond(ln, t):
                    u = BIGBLK[f"c{ln}_{t}"]
                    free_big(pe, u, nb)
                    if t == 0:
                        pe.wait_ge(split_done, S_COND + 2 * ln + 2 + ns)
                    for i in range(2):
                        ins = pe.matmul(big[u % NBIG][:, i, :], condT[:, t * P:(t + 1) * P], condw[:, 2 * ln + i, :], start=True, stop=True)
                    ins.then_inc(big_full, 1)

                def turn_y(ln, t):
                    u = BIGBLK[f"t{ln}_{t}"]
                    free_big(pe, u, nb)
                    pe.wait_ge(big_read, BIGBLK[f"c{ln}_{t}"] + nb + 1)
                    turn(pe, u, ybuf[:, t % 2, :], KT).then_inc(big_full, 1)

                for n in norm_order(0):
                    (cond if n[0] == "c" else turn_y)(0, int(n[3]))
                pe.wait_ge(big_read, BIGBLK["t0_4"] + nb + 1)
                for i in range(2):
                    for h in range(HEADS):
                        u = BIGBLK["qk"[i] + str(h)]
                        free_big(pe, u, nb)
                        q = (WQ, WK)[i] + h
                        pe.wait_ge(split_done, S_BLK + q + 1 + ns)
                        wide_mm(pe, u, sum([parts(wcol(RING_BLK + q, k), both(yT, k)) for k in range(KT)], [])).then_inc(big_full, 1)
                pe.wait_ge(split_done, S_BLK + WV + KT + ns)
                for t in range(NT):
                    u = BIGBLK[f"v{t}"]
                    free_big(pe, u, nb)
                    row_mm(pe, big[u % NBIG][:, 0, :], sum([parts(tile_of(yT, k, t), ringpart(RING_BLK + WV + k)) for k in range(KT)], [])).then_inc(big_full, 1)
                for what, k in ATT:
                    u = BIGBLK[f"{what}{k}"]
                    free_big(pe, u, nb)
                    if what == "S":
                        h, t = k // NT, k % NT
                        pe.wait_ge(big_read, BIGBLK[f"k{h}"] + nb + 1)
                        wide_mm(pe, u, parts(tile_of(qT, h, t), both(kT, h))).then_inc(big_full, 1)
                    elif what == "T":
                        pe.wait_ge(pn_up, it * HEADS * NT + k + 1)
                        turn(pe, u, pbuf[:, k % 4, :], NT).then_inc(big_full, 1)
                    else:
                        pe.wait_ge(big_read, BIGBLK[f"T{k * NT + NT - 1}"] + nb + 1)
                        pe.wait_ge(vlo_up, (it + 1) * NT)
                        wide_mm(pe, u, sum([parts([vrow[:, s, st, k * DH:(k + 1) * DH] for s in range(2)], both(pT, st))
                                            for st in range(NT)], [])).then_inc(big_full, 1)
                pe.wait_ge(big_read, BIGBLK["PV3"] + nb + 1)
                pe.wait_ge(split_done, S_BLK + WO + KT + ns)

                def out_row(t):
                    u = ROWBLK[f"wo{t}"]
                    free_row(pe, u, nr)
                    row_mm(pe, brow(u)[:, :], sum([parts(tile_of(qT, h, t), ringpart(RING_BLK + WO + h)) for h in range(HEADS)], [])).then_inc(row_full, 1)

                out_row(0)
                rows = 1
                for n in norm_order(1):
                    if rows < NT and n[0] == "c":
                        out_row(rows)
                        rows += 1
                    (cond if n[0] == "c" else turn_y)(1, int(n[3]))
                pe.wait_ge(big_read, BIGBLK["t1_4"] + nb + 1)
                for o in range(KT):
                    u = BIGBLK[f"m{o}"]
                    free_big(pe, u, nb)
                    pe.wait_ge(split_done, S_BLK + W1 + o + 1 + ns)
                    wide_mm(pe, u, sum([parts(wcol(RING_BLK + W1 + o, k), both(yT, k)) for k in range(KT)], [])).then_inc(big_full, 1)
                pe.wait_ge(hlo_up, (it + 1) * KT)
                pe.wait_ge(split_done, S_BLK + W2 + KT + ns)
                for t in range(NT):
                    u = ROWBLK[f"m2_{t}"]
                    free_row(pe, u, nr)
                    row_mm(pe, brow(u)[:, :], sum([parts(tile_of(kT, k, t), ringpart(RING_BLK + W2 + k)) for k in range(KT)], [])).then_inc(row_full, 1)

        @block.tensor
        def _(pe):
            pe.wait_ge(const0, 3)
            pe.wait_ge(dstep, 5)
            for name, i in (("src", 3), ("w", 2)):
                u = BIG0[name]
                for j in range(CH):
                    ins = pe.transpose(bflat(u)[:, j * NG:(j + 1) * NG], edge[0:NG, i, j * P:(j + 1) * P], ident[0:NG, 0:NG])
                ins.then_inc(big_full, 1)
            pe.wait_ge(dstep, 7)
            pe.matmul(bflat(BIG0["base"])[:, 0:2 * NG], ones[0:NG, :], xn[0:NG, 0, 0:2 * NG],
                      start=True, stop=True).then_inc(big_full, 1)
            u = BIG0["dst"]
            free_big(pe, u)
            for j in range(CH):
                ins = pe.transpose(bflat(u)[:, j * NG:(j + 1) * NG], edge[0:NG, 4, j * P:(j + 1) * P], ident[0:NG, 0:NG])
            ins.then_inc(big_full, 1)
            def turn_norm(u, i, t):
                free_big(pe, u)
                pe.wait_ge(xn_up, i + 1)
                turn(pe, u, xn[:, t % 2, :], KT).then_inc(big_full, 1)

            for t in range(NT):
                turn_norm(BIG0[f"l0_{t}"], t, t)
            u = ROW0["vec"]
            pe.wait_ge(vec_ld, 16 * 9)
            pe.transpose(brow(u)[:, 0:VECS], vec[:, :], ident[0:VECS, 0:VECS]).then_inc(row_full, 1)
            u = BIG0["z1"]
            free_big(pe, u)
            pe.wait_ge(sin_done, 1)
            pe.wait_ge(f_ld, 16 * F_LOADS)
            for h in range(2):
                ins = pe.matmul(big[u % NBIG][0:C16, h, 0:HALF], f_w1[:, :], tmp64[4][:, h * HALF:(h + 1) * HALF], start=True, stop=True)
            ins.then_inc(big_full, 1)
            u = ROW0["brow"]
            free_row(pe, u)
            pe.wait_ge(bconv_up, 1)
            pe.wait_ge(split_done, Q_LIN + 1)
            row_mm(pe, brow(u)[:, :], parts([bc_hl[:, 0, :], bc_hl[:, 1, :]], ringpart(Q_LIN))).then_inc(row_full, 1)
            u = BIG0["cond"]
            free_big(pe, u)
            pe.wait_ge(silu_up, 1)
            wide_mm(pe, u, [(f_w2[:, :], mask[0:C16, 3, :])]).then_inc(big_full, 1)
            u = BIG0["hall"]
            free_big(pe, u)
            pe.wait_ge(split_done, Q_CONV + 1)
            pe.wait_ge(big_read, BIG0[f"l0_{NT - 1}"] + 1)
            for t in range(NT):
                ins = row_mm(pe, bflat(u)[:, t * P:(t + 1) * P], sum([parts(tile_of(yT, k, t), wcol(Q_CONV, k)) for k in range(KT)], []))
            ins.then_inc(big_full, 1)
            pe.wait_ge(big_read, BIG0["hall"])
            pe.wait_ge(w_ready, 2)
            passes = pe.value_load(span_i[0:1, 1:2], min_val=0, max_val=NP // WIN)
            with pe.Fori(0, passes + 1) as kp:
                with pe.Fori(0, NG // HOT) as gi:
                    for b in range(HOT):
                        c = kp * NG + gi * HOT + b + 1
                        to = scat(b)
                        pe.wait_ge(hot_src_up, c)
                        pe.wait_ge(hot_act_up, c)
                        pe.wait_ge(hot_w_up, c)
                        pe.wait_ge(scat_read, c)
                        for j in range(CH):
                            for t in range(NT):
                                s = hot_src[b][:, j, t * P:(t + 1) * P]
                                o = t * 2 * WIN
                                pe.matmul(to[:, o:o + 2 * WIN], s, hot_dst[:, b, j, 0:2 * WIN],
                                          start=(j == 0 and t == 0), stop=False, skip_group_check=True)
                                for i in (2, 3):
                                    ins = pe.matmul(to[:, o + WIN:o + 2 * WIN], s, hot_dst[:, b, j, i * WIN:(i + 1) * WIN],
                                                    start=False, stop=(j == CH - 1 and i == 3), skip_group_check=True)
                        ins.then_inc(scat_full, 1)
            pe.wait_ge(diag_up, NT)
            for name, m in (("degw", w_acc), ("degc", cnt_acc)):
                u = BIG0[name]
                free_big(pe, u)
                for cols640 in (slice(0, D), slice(D, NP)):
                    ins = row_mm(pe, bflat(u)[:, cols640], [(ones[:, :], m[:, st, cols640]) for st in range(NT)])
                ins.then_inc(big_full, 1)
            u = BIG0["agg"]
            free_big(pe, u)
            pe.wait_ge(wlo_up, NT)
            pe.wait_ge(big_read, BIG0["hall"] + 1)
            wide_mm(pe, u, sum([parts(both(h0, st), both(adj, st)) for st in range(NT)], [])).then_inc(big_full, 1)
            pe.wait_ge(big_read, u + 1)
            for t in range(NT):
                u = ROW0[f"o{t}"]
                free_row(pe, u)
                row_mm(pe, brow(u)[:, :], parts([aT[:, s, t * P:(t + 1) * P] for s in range(2)], ringpart(Q_LIN))).then_inc(row_full, 1)
            for t in range(NT):
                turn_norm(BIG0[f"l1_{t}"], LN_L1 + t, t)
            pe.wait_ge(split_done, Q_L + KT)
            for t in range(NT):
                u = ROW0[f"z{t}"]
                free_row(pe, u)
                pe.wait_ge(big_read, BIG0[f"l1_{t}"] + 1)
                row_mm(pe, brow(u)[:, :], sum([parts(tile_of(yT, k, t), ringpart(Q_L + k)) for k in range(KT)], [])).then_inc(row_full, 1)
            pe.wait_ge(split_done, Q_R + KT)
            pe.wait_ge(clo_up, NT)
            for t in range(NT):
                u = ROW0[f"r{t}"]
                free_row(pe, u)
                row_mm(pe, brow(u)[:, :], sum([parts(tile_of(yT, k, t), ringpart(Q_R + k)) for k in range(KT)], [])).then_inc(row_full, 1)
                u = ROW0[f"a{t}"]
                pe.wait_ge(row_read, ROW0["z4"] + 1)
                free_row(pe, u)
                row_mm(pe, brow(u)[:, :], sum([parts(tile_of(adj, st, t), both(vrow, st)) for st in range(NT)], [])).then_inc(row_full, 1)
            pe_l2(pe)
            pe_l3(pe, turn_norm)

        def dve_l2(dve, tile_stats, normalise, f32):
            dve.wait_ge(mask_up, NT)
            for t in range(NT):
                if t >= 2:
                    dve.wait_ge(z_up, t - 1)
                normalise(LN_IN + t, LN_IN + t, t, x[:, t, :], t)
                dve.wait_ge(xn_up, LN_IN + t + 1)
                dve.tensor_scalar(z[:, t, :], xn[:, t % 2, :], 0.0, None, ALU.max).then_inc(z_up, 1)
                dve.wait_ge(z_up, t + 1)
                tile_stats(LN_BLK + t, NT + t, z[:, t, :])
            with dve.Fori(0, BLOCKS) as it:
                nb, nr = it * len(BLOCK_BIG), it * len(BLOCK_ROW)

                def scaled(ln, t):
                    i = LN_BLK + it * 2 * NT + ln * NT + t
                    normalise(i, i, (NT + ln * NT + t) % (2 * NT), z[:, t, :], t)
                    u = BIGBLK[f"c{ln}_{t}"]
                    dve.wait_ge(big_full, u + nb + 1)
                    dve.wait_ge(xn_up, i + 1)
                    if t >= 2:
                        dve.wait_ge(big_full, BIGBLK[f"t{ln}_{t - 2}"] + nb + 1)
                    dve.scalar_tensor_tensor(ybuf[:, t % 2, :], big[u % NBIG][:, 0, :], 1.0, xn[:, t % 2, :],
                                             ALU.add, ALU.mult).then_inc(y1_up, 1)
                    dve.wait_ge(y1_up, it * 2 * NT + ln * NT + t + 1)
                    dve.tensor_tensor(ybuf[:, t % 2, :], big[u % NBIG][:, 1, :], ybuf[:, t % 2, :], ALU.add).then_inc(big_read, 1)

                def turned_rest(ln, t):
                    u = BIGBLK[f"t{ln}_{t}"]
                    dve.wait_ge(yhi_up, 2 * NT + it * 2 * NT + ln * NT + t + 1)
                    dve.tensor_tensor(yT[:, 1, :, t * P:(t + 1) * P], bflat(u)[:, 0:D].rearrange("p (k n) -> p k n", k=KT),
                                      f32(yT[:, 0, :, t * P:(t + 1) * P]), ALU.subtract).then_inc(big_read, 1)

                def residual(name, t, xb, i, slot):
                    u = ROWBLK[f"{name}{t}"]
                    dve.wait_ge(row_full, u + nr + 1)
                    dve.wait_ge(xb_up, xb)
                    dve.tensor_tensor(z[:, t, :], brow(u)[:, :], z[:, t, :], ALU.add).then_inc(row_read, 1)
                    dve.wait_ge(row_read, u + nr + 1)
                    tile_stats(i, slot, z[:, t, :])

                for n in norm_order(0):
                    (scaled if n[0] == "c" else turned_rest)(0, int(n[3]))
                for i, to in enumerate((qT, kT)):
                    for h in range(HEADS):
                        u = BIGBLK["qk"[i] + str(h)]
                        dve.wait_ge(qkhi_up, it * 2 * HEADS + i * HEADS + h + 1)
                        dve.scalar_tensor_tensor(wide(to[:, 1, h, :]), bwide(u), bqk[:, i, bass.ds(it * KT + h, 1)],
                                                 wide(f32(to[:, 0, h, :])), ALU.add, ALU.subtract).then_inc(big_read, 1)
                for t in range(NT):
                    u = BIGBLK[f"v{t}"]
                    dve.wait_ge(bias_ld, 48 * it + 48)
                    dve.wait_ge(big_full, u + nb + 1)
                    if t >= 2:
                        dve.wait_ge(vlo_up, it * NT + t - 1)
                    dve.tensor_tensor(vbuf[:, t % 2, :], big[u % NBIG][:, 0, :], bias[:, 0, :], ALU.add).then_inc(big_read, 1)
                heads = it * HEADS * NT
                for what, k in ATT + [("last", 0)]:
                    if what == "S":
                        u = BIGBLK[f"S{k}"]
                        t = k % NT
                        if k >= 4:
                            dve.wait_ge(big_full, BIGBLK[f"T{k - 4}"] + nb + 1)
                        wait_apart(dve, big_full, u + nb + 1)
                        dve.tensor_tensor_reduce(wide(pbuf[:, k % 4, :]), bwide(u), wide(mask[:, t, :]), -DH ** -0.5, 3e38,
                                                 ALU.add, ALU.min, nsmax[:, k:k + 1]).then_inc(big_read, 1)
                    if what == "S" and k >= 1 or (what, k) == ("T", HEADS * NT - LAG):
                        j = k - 1 if what == "S" else HEADS * NT - 1
                        dve.wait_ge(exp_up, heads + j + 1)
                        dve.reciprocal(rden[:, j:j + 1], den[:, j:j + 1]).then_inc(rden_up, 1)
                    if what == "T":
                        u, t = BIGBLK[f"T{k}"], k % NT
                        dve.wait_ge(phi_up, heads + k + 1)
                        dve.tensor_tensor(pT[:, 1, :, t * P:(t + 1) * P], bflat(u).rearrange("p (k n) -> p k n", k=NT),
                                          f32(pT[:, 0, :, t * P:(t + 1) * P]), ALU.subtract).then_inc(big_read, 1)
                    elif what == "PV":
                        u = BIGBLK[f"PV{k}"]
                        dve.wait_ge(ohi_up, it * HEADS + k + 1)
                        dve.tensor_tensor(wide(qT[:, 1, k, :]), bwide(u), wide(f32(qT[:, 0, k, :])), ALU.subtract).then_inc(big_read, 1)
                xb = NT + it * 2 * NT + 1
                done = 0
                for n in norm_order(1):
                    while done < NT and n[0] == "c" and done < int(n[3]) + 2:
                        residual("wo", done, xb + done, LN_BLK + it * 2 * NT + NT + done, done)
                        done += 1
                    (scaled if n[0] == "c" else turned_rest)(1, int(n[3]))
                for o in range(KT + 1):
                    if o < KT:
                        u = BIGBLK[f"m{o}"]
                        dve.wait_ge(big_full, u + nb + 1)
                        if o >= 2:
                            dve.wait_ge(hlo_up, it * KT + o - 1)
                        dve.tensor_scalar(wide(rbuf[:, o % 2, :]), bwide(u), bqk[:, 2, bass.ds(it * KT + o, 1)], 0.0,
                                          ALU.add, ALU.max).then_inc(big_read, 1)
                    if o >= 1:
                        dve.wait_ge(hhi_up, it * KT + o)
                        dve.tensor_tensor(kT[:, 1, o - 1, :], rbuf[:, (o - 1) % 2, :], f32(kT[:, 0, o - 1, :]), ALU.subtract).then_inc(hlo_up, 1)
                for t in range(NT):
                    residual("m2_", t, xb + NT + t, LN_BLK + (it + 1) * 2 * NT + t, NT + t)
            for t in range(NT):
                dve.tensor_tensor(x[:, t, :], x[:, t, :], z[:, t, :], ALU.add).then_inc(x_up, 1)
        @block.vector
        def _(dve):
            own = [0]

            def step(ins):
                own[0] += 1
                ins.then_inc(dstep, 1)
                dve.wait_ge(dstep, own[0])

            def f32(ap):
                return ap.bitcast(F32)

            dve.memset(edge[0:NG, 0, :].bitcast(I32), 9999).then_inc(e_clear, 1)
            dve.memset(edge[0:NG, 2, :], 0.0).then_inc(e_clear, 1)
            dve.memset(x[:, NT - 1, :], 0.0).then_inc(x_clear, 1)
            dve.wait_ge(e_ld, 16 * 7)
            step(dve.tensor_copy(edge[0:NG, 3, :], edge[0:NG, 0, :].bitcast(I32)))
            step(dve.tensor_copy(edge[0:NG, 4, :], edge[0:NG, 1, :].bitcast(I32)))
            step(dve.tensor_reduce(mnmx[0:NG, 0:1], edge[0:NG, 4, :], AX.X, ALU.min))
            step(dve.tensor_reduce(mnmx[0:NG, 1:2], edge[0:NG, 4, :], AX.X, ALU.max))
            step(dve.tensor_tensor(mnmx[0:NG, 2:3], mnmx[0:NG, 1:2], mnmx[0:NG, 0:1], ALU.subtract))
            dve.wait_ge(const0, 3)
            step(dve.tensor_scalar(xn[0:NG, 0, 0:NG], ident[0:NG, 0:NG], mnmx[0:NG, 0:1], None, ALU.mult))
            step(dve.tensor_scalar(xn[0:NG, 0, NG:2 * NG], ident[0:NG, 0:NG], mnmx[0:NG, 2:3], None, ALU.mult))
            for name, to in (("src", src_col), ("w", w_col)):
                dve.wait_ge(big_full, BIG0[name] + 1)
                dve.tensor_copy(to[:, :, :], bflat(BIG0[name])[:, 0:CH * NG].rearrange("p (j g) -> p j g", j=CH)).then_inc(big_read, 1)
            u = BIG0["base"]
            dve.wait_ge(big_full, u + 1)
            step(dve.tensor_copy(base_f[:, :], bflat(u)[:, 0:NG]))
            dve.tensor_reduce(span[:, 0:1], bflat(u)[:, NG:2 * NG], AX.X, ALU.max).then_inc(big_read, 1)
            u = BIG0["dst"]
            dve.wait_ge(big_full, u + 1)
            dve.tensor_tensor(dst_rel[:, :, :], bflat(u)[:, 0:CH * NG].rearrange("p (j g) -> p j g", j=CH),
                              base_f[:, :].unsqueeze(1).broadcast_to([P, CH, NG]), ALU.subtract).then_inc(big_read, 1)
            step(dve.tensor_copy(base_i[:, :], base_f[0:1, :]))
            dve.wait_ge(big_read, u + 1)
            step(dve.tensor_scalar(span[:, 1:2], span[:, 0:1], float(PASS_MUL), None, ALU.mult))
            step(dve.tensor_copy(span_i[:, 0:1], span[:, 1:2]))
            dve.tensor_scalar(span_i[:, 1:2], span_i[:, 0:1], 16, None, ALU.arith_shift_right).then_inc(w_ready, 1)
            step(dve.tensor_copy(w_part[:, 0, :, :], w_col[:, :, :]))
            for i in (1, 2):
                step(dve.tensor_tensor(w_col[:, :, :], w_col[:, :, :], w_part[:, i - 1, :, :], ALU.subtract))
                ins = dve.tensor_copy(w_part[:, i, :, :], w_col[:, :, :])
                if i == 1:
                    step(ins)
            ins.then_inc(w_ready, 1)
            def tile_stats(i, slot, src):
                dve.bn_stats(stats[:, slot, :], src).then_inc(st_up, 1)
                wait_apart(dve, st_up, i + 1)
                dve.bn_aggr(mv[:, slot, :], stats[:, slot, :]).then_inc(aggr_up, 1)

            def normalise(i, ixn, slot, src, t):
                dve.wait_ge(rstd_up, i + 1)
                dve.tensor_scalar(xn[:, t % 2, :], src, mv[:, slot, 0:1], rstd[:, slot:slot + 1],
                                  ALU.subtract, ALU.mult).then_inc(xn_up, 1)

            def turned_rest(u, i, t):
                dve.wait_ge(yhi_up, i + 1)
                dve.scalar_tensor_tensor(yT[:, 1, :, t * P:(t + 1) * P], bflat(u)[:, 0:D].rearrange("p (k n) -> p k n", k=KT),
                                         0.0, f32(yT[:, 0, :, t * P:(t + 1) * P]), ALU.max, ALU.subtract).then_inc(big_read, 1)

            def relu_norm(first, slot0, names, yfirst):
                for t in range(NT + 1):
                    if t < NT:
                        if t >= 2:
                            dve.wait_ge(big_full, names[t - 2] + 1)
                        normalise(first + t, first + t, slot0 + t, x[:, t, :], t)
                    if t >= 1:
                        turned_rest(names[t - 1], yfirst + t - 1, t - 1)

            dve.wait_ge(x_ld, 32)
            for t in range(NT):
                tile_stats(t, t, x[:, t, :])
            dve.wait_ge(const1, 3)
            dve.wait_ge(f_ld, 16 * F_LOADS)
            step(dve.tensor_scalar(fcol[0:2 * NF, 1:2], freq_i, float(np.float32(2.0 * np.pi / 16)), None, ALU.mult))
            noise, ph, kf, r = tmp64[0:4]
            step(dve.tensor_scalar(ph, noise, fcol[0:2 * NF, 1:2], None, ALU.mult))
            MAGIC = 1.5 * 2.0 ** 23
            step(dve.tensor_scalar(kf, ph, float(1 / (2 * np.pi)), MAGIC, ALU.mult, ALU.add))
            step(dve.tensor_scalar(kf, kf, MAGIC, None, ALU.subtract))
            TURN_HI = 6.28125
            step(dve.scalar_tensor_tensor(r, kf, -TURN_HI, ph, ALU.mult, ALU.add))
            step(dve.scalar_tensor_tensor(r, kf, -float(2 * np.pi - TURN_HI), r, ALU.mult, ALU.add))
            step(dve.tensor_scalar(r, r, 3.1415925, -3.1415925, ALU.min, ALU.max))
            c = r[NF:2 * NF]
            step(dve.scalar_tensor_tensor(c, c, -1.0, c, ALU.mult, ALU.max))
            dve.tensor_scalar(c, c, -1.0, float(np.pi / 2), ALU.mult, ALU.add).then_inc(emb_up, 1)
            relu_norm(0, 0, [BIG0[f"l0_{t}"] for t in range(NT)], 0)
            u = ROW0["vec"]
            dve.wait_ge(row_full, u + 1)
            dve.tensor_copy(cols[:, :], brow(u)[:, 0:VECS]).then_inc(row_read, 1)
            dve.wait_ge(row_read, u + 1)
            u = BIG0["z1"]
            dve.wait_ge(big_full, u + 1)
            z1 = mask[0:C16, 1, :]
            dve.tensor_scalar(wide(z1), big[u % NBIG][0:C16, :, 0:HALF], fcol[0:C16, 3:4], None, ALU.add).then_inc(big_read, 1)
            step(dve.tensor_scalar(bc_hl[:, 0, :], ones[:, :], bconv[:, 0:1], None, ALU.mult))
            dve.scalar_tensor_tensor(bc_hl[:, 1, :], ones[:, :], bconv[:, 0:1], f32(bc_hl[:, 0, :]), ALU.mult, ALU.subtract).then_inc(bconv_up, 1)
            dve.wait_ge(sig_done, 1)
            dve.tensor_tensor(mask[0:C16, 3, :], z1, mask[0:C16, 2, :], ALU.mult).then_inc(silu_up, 1)
            u = ROW0["brow"]
            dve.wait_ge(col_ld, 16 * 2)
            dve.wait_ge(row_full, u + 1)
            dve.tensor_tensor(bias[:, 0, :], brow(u)[:, :], bias[:, 0, :], ALU.add).then_inc(row_read, 1)
            u = BIG0["cond"]
            dve.wait_ge(cb_one, 4)
            dve.wait_ge(big_full, u + 1)
            ct = mask[:, 4, :]
            dve.tensor_scalar(wide(ct), bwide(u), fcol[:, 2:3], None, ALU.add).then_inc(big_read, 1)
            dve.wait_ge(big_read, u + 1)
            dve.tensor_copy(condT[0:64, :], ct[0:64]).then_inc(condT_up, 1)
            step(dve.tensor_copy(condT[64:P, :], ct[64:P]))
            dve.tensor_tensor(condT[64:P, :], ct[64:P], f32(condT[64:P, :]), ALU.subtract).then_inc(condT_up, 1)

            dve.wait_ge(w_ready, 2)
            passes = dve.value_load(span_i[0:1, 1:2], min_val=0, max_val=NP // WIN)
            with dve.Fori(0, passes + 1) as kp:
                def hot(g, b):
                    dve.wait_ge(scat_full, kp * NG + g + 1)
                    for j in range(CH - 1):
                        ins = dve.tensor_scalar(hot_src[b][:, j, :], iota16[:, :], src_col[:, j, bass.ds(g, 1)], None, ALU.is_equal)
                    ins.then_inc(hot_src_up, 1)
                    dve.tensor_tensor(hot_dst[:, b, :, 0:WIN], iota16[:, 0:WIN].unsqueeze(1).broadcast_to([P, CH, WIN]),
                                      dst_rel[:, :, bass.ds(g, 1)].broadcast_to([P, CH, WIN]), ALU.is_equal).then_inc(hot_dst_up, 1)

                def add(g, b):
                    w0 = dve.value_load(base_i[0:1, bass.ds(g, 1)], min_val=0, max_val=NP)
                    dve.wait_ge(scat_full, kp * NG + g + HOT + 1)
                    dve.wait_ge(scat_read, kp * NG + g + HOT)
                    win = adjacc[:, :, :, bass.ds(w0, WIN)]
                    dve.tensor_tensor(win, scat(b).rearrange("p (t c n) -> p t c n", t=NT, c=2), win, ALU.add).then_inc(scat_read, 1)

                for b in range(HOT - 1):
                    hot(b, b)
                with dve.Fori(0, NG // HOT - 1) as gi:
                    for b in range(HOT):
                        hot(gi * HOT + b + HOT - 1, (b + HOT - 1) % HOT)
                        add(gi * HOT + b, b)
                hot(NG - 1, HOT - 1)
                for b in range(HOT):
                    add(NG - HOT + b, b)
                dve.tensor_scalar(dst_rel[:, :, :], dst_rel[:, :, :], float(WIN), None, ALU.subtract).then_inc(pass_up, 1)
                dve.tensor_scalar(base_f[0:1, :], base_f[0:1, :], float(WIN), float(NP), ALU.add, ALU.min).then_inc(pass_up, 1)
                dve.wait_ge(pass_up, kp * 3 + 2)
                dve.tensor_copy(base_i[:, :], base_f[0:1, :]).then_inc(pass_up, 1)
                dve.wait_ge(pass_up, kp * 3 + 3)
            dve.wait_ge(scat_read, (passes + 1) * NG + HOT)

            for t in range(NT):
                d = w_acc[:, t, t * P:(t + 1) * P]
                dve.tensor_tensor(d, d, ident[:, :], ALU.add).then_inc(diag_up, 1)
            def own_sums(name, to):
                u = BIG0[name]
                dve.wait_ge(big_full, u + 1)
                for t in range(NT):
                    ins = dve.tensor_tensor_reduce(xn[:, t // KT, (t % KT) * P:(t % KT + 1) * P], bflat(u)[:, t * P:(t + 1) * P],
                                                   ident[:, :], 1.0, 0.0, ALU.mult, ALU.add, to[:, t:t + 1])
                ins.then_inc(big_read, 1)
                dve.wait_ge(big_read, u + 1)

            u = BIG0["hall"]
            dve.wait_ge(h0hi_up, 1)
            dve.tensor_tensor(h0[:, 1, :, :], bflat(u).rearrange("p (t n) -> p t n", t=NT), f32(h0[:, 0, :, :]), ALU.subtract).then_inc(big_read, 1)
            own_sums("degw", degs[:, 0, :])
            dve.tensor_scalar(degs[:, 1, :], degs[:, 0, :], 1e-30, None, ALU.max).then_inc(w_up, 1)
            dve.wait_ge(dpow_up, 1)
            dve.scalar_tensor_tensor(degs[:, 3, :], degs[:, 0, :], 0.0, degs[:, 2, :], ALU.is_gt, ALU.mult).then_inc(dinv_up, 1)
            dve.wait_ge(dinv_up, 1)
            for t in range(NT):
                dve.wait_ge(whi_up, t + 1)
                dve.scalar_tensor_tensor(adj[:, 1, t, :], w_acc[:, t, :], degs[:, 3, t:t + 1], f32(adj[:, 0, t, :]),
                                         ALU.mult, ALU.subtract).then_inc(wlo_up, 1)
            own_sums("degc", rcnt[:, 0, :])
            dve.tensor_scalar(rcnt[:, 0, :], rcnt[:, 0, :], 1.0, None, ALU.max).then_inc(w_up, 1)
            dve.wait_ge(w_up, 2)
            dve.reciprocal(rcnt[:, 1, :], rcnt[:, 0, :]).then_inc(w_up, 1)
            u = BIG0["agg"]
            dve.wait_ge(ahi_up, 1)
            dve.tensor_tensor(wide(aT[:, 1, :]), bwide(u), wide(f32(aT[:, 0, :])), ALU.subtract).then_inc(big_read, 1)
            for t in range(NT):
                u = ROW0[f"o{t}"]
                dve.wait_ge(row_full, u + 1)
                dve.wait_ge(xb_up, t + 1)
                dve.scalar_tensor_tensor(x[:, t, :], brow(u)[:, :], degs[:, 3, t:t + 1], x[:, t, :], ALU.mult, ALU.add).then_inc(row_read, 1)
                dve.wait_ge(row_read, u + 1)
                tile_stats(LN_L1 + t, NT + t, x[:, t, :])
            relu_norm(LN_L1, NT, [BIG0[f"l1_{t}"] for t in range(NT)], NT)
            for t in range(NT):
                u = ROW0[f"z{t}"]
                dve.wait_ge(zhi_up, t + 1)
                dve.tensor_tensor(vrow[:, 1, t, :], brow(u)[:, :], f32(vrow[:, 0, t, :]), ALU.subtract).then_inc(row_read, 1)
                dve.tensor_scalar(mask[:, t, :], cnt_acc[:, t, :], 1.0, None, ALU.max).then_inc(clamp_up, 1)
                dve.wait_ge(chi_up, t + 1)
                dve.tensor_tensor(adj[:, 1, t, :], cnt_acc[:, t, :], f32(adj[:, 0, t, :]), ALU.subtract).then_inc(clo_up, 1)
            step(dve.tensor_scalar(flag[:, 1, :], flag[:, 0, :], 0.5, None, ALU.is_gt))
            step(dve.tensor_scalar(flag[:, 2, :], flag[:, 1, :], NOEDGE, None, ALU.mult))
            step(dve.tensor_scalar(flag[:, 3, :], flag[:, 2, :], -1.0, NOEDGE, ALU.mult, ALU.add))
            for t in range(NT):
                u = ROW0[f"r{t}"]
                dve.wait_ge(row_full, u + 1)
                dve.tensor_tensor(t1[:, t % 2, :], brow(u)[:, :], bias[:, 1, :], ALU.add).then_inc(row_read, 1)
                dve.wait_ge(row_read, u + 1)
                dve.wait_ge(clo_up, NT)
                dve.tensor_scalar(cnt_acc[:, t, :], cnt_acc[:, t, :], 0.5, flag[:, 2, t:t + 1], ALU.is_lt, ALU.mult).then_inc(pen_up, 1)
                dve.wait_ge(pen_up, t + 1)
                dve.wait_ge(ln_up, t + 1)
                dve.scalar_tensor_tensor(mask[:, t, :], mask[:, t, :], DH ** 0.5, cnt_acc[:, t, :], ALU.mult, ALU.add).then_inc(mask_up, 1)
                u = ROW0[f"a{t}"]
                dve.wait_ge(row_full, u + 1)
                if t >= 2:
                    dve.wait_ge(l1p_up, t - 1)
                dve.scalar_tensor_tensor(t2[:, t % 2, :], brow(u)[:, :], rcnt[:, 1, t:t + 1], t1[:, t % 2, :],
                                         ALU.mult, ALU.add).then_inc(row_read, 1)
                dve.wait_ge(gate_up, t + 1)
                dve.tensor_tensor(t1[:, t % 2, :], t2[:, t % 2, :], sg[:, t % 2, :], ALU.mult).then_inc(l1p_up, 1)
                dve.wait_ge(l1p_up, t + 1)
                dve.tensor_tensor(x[:, t, :], x[:, t, :], t1[:, t % 2, :], ALU.add).then_inc(x_up, 1)
                dve.wait_ge(x_up, t + 1)
                tile_stats(LN_IN + t, t, x[:, t, :])
            dve_l2(dve, tile_stats, normalise, f32)
            dve_l3(dve, tile_stats, relu_norm, step)



NAMES = (
    ["x", "src", "dst", "edge_weight", "node_vec1"]
    + ["L0_gnn_" + n for n in ("W_conv", "b_conv", "W_lin", "b_lin")]
    + ["L1_gnn_" + n for n in ("W_l", "W_r", "b")]
    + ["L2_gnn_" + n for n in ("f_w1", "f_b1", "f_w2", "f_b2", "s1_w", "s1_b", "b1_w", "b1_b", "wq", "bq", "wk", "bk",
                               "wv", "bv", "wo", "bo", "s2_w", "s2_b", "b2_w", "b2_b", "m_w1", "m_b1", "m_w2", "m_b2")]
    + ["L3_gnn_" + n for n in ("W_f", "att_src_f", "att_dst_f", "bias_f", "W_b", "att_src_b", "att_dst_b", "bias_b",
                               "W_fuse", "b_fuse", "bn_gamma", "bn_beta")]
)


def kernel(**inputs):
    import numpy as np
    import concourse.bacc as bacc
    from concourse import mybir
    from concourse.bass_utils import run_bass_kernel_spmd as run

    nc = bacc.Bacc("TRN2", target_bir_lowering=False, num_devices=1)
    arrays, aps = {}, {}
    for name in NAMES:
        v = np.ascontiguousarray(inputs[name])
        arrays["in_" + name] = v
        aps[name] = nc.dram_tensor("in_" + name, v.shape, mybir.dt.from_np(v.dtype), kind="ExternalInput").ap()
    out = nc.dram_tensor("out_x", (N, D), F32, kind="ExternalOutput").ap()
    build(nc, aps, out)
    r = run(nc, [arrays], core_ids=[0])
    return r.results[0]["out_x"]
```

```python
from contextlib import ExitStack

import numpy as np

import concourse.bass as bass
from concourse import mybir

F32 = mybir.dt.float32
F32R = mybir.dt.float32r
BF16 = mybir.dt.bfloat16
F16 = mybir.dt.float16
I32 = mybir.dt.int32
ALU = mybir.AluOpType
ACT = mybir.ActivationFunctionType
AX = mybir.AxisListType

P = 128
N = 625
NT = (N + P - 1) // P
NP = NT * P
TAIL = N - (NT - 1) * P
HALF = NP // 2
D = 512
KT = D // P
E = 20000
GROUP = 512
CH = GROUP // P
NG = (E + GROUP - 1) // GROUP
ELAST = E - (NG - 1) * GROUP
WIN = 40
PASS_MUL = 2 ** 16 // WIN + 1
assert all((i * PASS_MUL) >> 16 == i // WIN for i in range(NP + 1))
HOT = 4
assert NG % HOT == 0 and NT * 2 * WIN <= 512
ACCW = NP + WIN
BLOCKS = 4
HEADS = 4
DH = D // HEADS
L3H = 4
L3C = D // (2 * L3H)
NJ = 2 * L3H
NF = 32
C16 = 16
EPS = 1e-5
NOEDGE = -1e30
RING = 6
STAGE = 4
OUTER = 2
PVA_AT, PVB_AT = 4, 6
LAG = 3

NBIG, NROW = 3, 2

PRE_BIG = ["src", "w", "base", "dst"] + [f"l0_{t}" for t in range(NT)] + ["z1", "cond", "hall"]
MID_BIG = ["degw", "degc", "agg"] + [f"l1_{t}" for t in range(NT)]


FIRST_NORM = ["c0_0", "c0_1", "t0_0", "t0_1", "c0_2", "c0_3", "t0_2", "c0_4", "t0_3", "t0_4"]
AHEAD = 4


def norm_order(ln):
    return [f"c{ln}_0", f"c{ln}_1", f"t{ln}_0", f"c{ln}_2", f"t{ln}_1", f"c{ln}_3", f"t{ln}_2",
            f"c{ln}_4", f"t{ln}_3", f"t{ln}_4"]


def attention_order(scores_first):
    steps = []
    for k in range(HEADS * NT + LAG):
        scores = [("S", k)] if k < HEADS * NT else []
        kk = k - LAG
        turned = [("T", kk)] if kk >= 0 else []
        for what, behind in (("PVa", PVA_AT), ("PVb", PVB_AT)):
            if kk >= behind and (kk - behind) % NT == 0:
                turned.insert(-1, (what, (kk - behind) // NT))
        steps += scores + turned if scores_first else turned + scores
    return steps + [("PVb", HEADS - 1)]


ATT = attention_order(True)
ATT_ACT = attention_order(False)
BLOCK_BIG = (FIRST_NORM + [f"q{h}" for h in range(HEADS)] + [f"k{h}" for h in range(HEADS)]
             + [f"{a}{b}" for a, b in ATT] + norm_order(1) + [f"m{o}" for o in range(KT)])
L3_BIG = ([f"l3_{t}" for t in range(NT)] + [f"mt{t}" for t in range(NT)] + ["as"]
          + [f"am{j}" for j in range(NJ)] + ["vt"]
          + ["vb0"] + sum([[f"vb{j + 1}", f"va{j}"] if j < NJ - 1 else [f"va{j}"] for j in range(NJ)], [])
          + ["rec"] + [f"rb{k}" for k in range(KT)] + [f"f{o}" for o in range(KT)])
PRE_ROW = ["vec", "brow"] + [f"o{t}" for t in range(NT)]
MID_ROW = [f"z{t}" for t in range(NT)] + sum([[f"r{t}", f"a{t}"] for t in range(NT)], [])
ROW_SPARE = -3 * NT % NROW
BLOCK_ROW = [f"v{t}" for t in range(NT)] + [f"spare{i}" for i in range(ROW_SPARE)] + [f"wo{t}" for t in range(NT)] + [f"m2_{t}" for t in range(NT)]
L3_ROW = [f"H{t}" for t in range(NT)] + sum([[f"P{j}a", f"P{j}b"] for j in range(NJ)], []) + [f"y{t}" for t in range(NT)]

ROW_SPLIT = (3 * P, NP - 3 * P)
NE = 4
assert PRE_BIG.index("hall") == len(PRE_BIG) - 1 and PRE_BIG.index("hall") % NBIG == 2
BIG_SPARE = -len(BLOCK_BIG) % NBIG
BLOCK_BIG += [f"spare{i}" for i in range(BIG_SPARE)]
assert len(BLOCK_BIG) % NBIG == 0 and len(BLOCK_ROW) % NROW == 0
BIG0 = {n: i for i, n in enumerate(PRE_BIG + MID_BIG)}
BIGB = len(BIG0)
BIGBLK = {n: BIGB + i for i, n in enumerate(BLOCK_BIG)}
BIG3 = {n: BIGB + BLOCKS * len(BLOCK_BIG) + AHEAD + i for i, n in enumerate(L3_BIG)}
ROW0 = {n: i for i, n in enumerate(PRE_ROW + MID_ROW)}
ROWB = len(ROW0)
ROWBLK = {n: ROWB + i for i, n in enumerate(BLOCK_ROW)}
ROW3 = {n: ROWB + BLOCKS * len(BLOCK_ROW) + i for i, n in enumerate(L3_ROW)}

Q_CONV, Q_LIN, Q_L, Q_R = 0, 1, 2, 2 + KT
RING_BLK = 2 + 2 * KT
PERBLK = 6 * KT
F_LOADS = 3 + 2 * 4
VECS = 3 * BLOCKS * KT + 4 * KT + 1
RING_L3 = RING_BLK + BLOCKS * PERBLK
S_COND = RING_BLK
S_BLK = S_COND + 4
S_PERBLK = PERBLK + 4
S_L3 = S_BLK + BLOCKS * S_PERBLK
assert PERBLK % RING == 0 and S_PERBLK % STAGE == 0 and S_COND % OUTER == 0 and S_L3 % OUTER == 0
WV, WQ, WK, WO, W1, W2 = (KT * i for i in range(6))
LN_L1, LN_IN, LN_BLK = NT, 2 * NT, 3 * NT
LN_L3 = LN_BLK + NT + BLOCKS * 2 * NT
XN_L3 = LN_BLK


def wide(ap640):
    return ap640.rearrange("p (h n) -> p h n", h=2)


def build(nc, a, out):
    ctx = ExitStack()
    with ctx:
        def sb(name, shape, dt):
            return ctx.enter_context(nc.sbuf_tensor(name, shape, dt))

        def sem(name):
            return ctx.enter_context(nc.semaphore(name))

        x = sb("x", [P, NT, D], F32)
        z = sb("z", [P, NT, D], F32)
        arena1 = sb("arena1", [P, 2 * 2 * HEADS * NP], F32R)
        arena2 = sb("arena2", [P, 2 * NT * D], F32R)
        arena3 = sb("arena3", [P, 2 * NT * NP], F32R)
        acc = sb("acc", [P, NT * NP + NT * NJ // 2 * 3 * L3C], F32)
        mask = sb("mask", [P, NT, NP], F32)
        ringw = sb("ringw", [P, RING, 2, D], F32R)
        raw = sb("raw", [P, OUTER, D], F32)
        condw = sb("condw", [P, 4, D], F32R)
        condT = sb("condT", [P, NP], F32R)
        bias = sb("bias", [P, 3, D], F32)
        xn = sb("xn", [P, 2, D], F32)
        ident = sb("ident", [P, P], F32)
        ones = sb("ones", [P, P], F32)
        iota16 = sb("iota16", [P, NP], F16)
        edge_col = sb("edge_col", [P, 3 * CH * NG], F32)
        w_part = sb("w_part", [P, 3, CH, NG], BF16)
        hot_dst = sb("hot_dst", [P, HOT, CH, 4 * WIN], BF16)
        base_f = sb("base_f", [P, NG], F32)
        base_i = sb("base_i", [1, NG], I32)
        span = sb("span", [P, 2], F32)
        span_i = sb("span_i", [P, 2], I32)
        mnmx = sb("mnmx", [P, 4], F32)
        stats = sb("stats", [P, 2 * NT, 6], F32)
        mv = sb("mv", [P, 2 * NT, 2], F32)
        veps = sb("veps", [P, 2 * NT], F32)
        rstd = sb("rstd", [P, 2 * NT], F32)
        half = sb("half", [P, NT], F32)
        degs = sb("degs", [P, 4, NT], F32)
        rcnt = sb("rcnt", [P, 2, NT], F32)
        flag = sb("flag", [P, 4, NT], F32)
        nsmax = sb("nsmax", [P, HEADS * NT], F32)
        den = sb("den", [P, HEADS * NT], F32)
        rden = sb("rden", [P, HEADS * NT], F32)
        vec = sb("vec", [VECS, P], F32)
        cols = sb("cols", [P, VECS], F32)
        fcol = sb("fcol", [P, 4], F32)
        f_w1 = sb("f_w1", [2 * NF, C16], F32)
        f_w2 = sb("f_w2", [C16, P], F32)
        bn3 = sb("bn3", [P, KT, 2, 6], F32)
        mv3 = sb("mv3", [P, KT, 2], F32)
        bnc = sb("bnc", [P, 4, KT], F32)

        src_col, dst_rel, w_col = [edge_col[:, i * CH * NG:(i + 1) * CH * NG].rearrange("p (j g) -> p j g", j=CH) for i in range(3)]
        l3s = edge_col[:, 0:5 * NT * NJ].rearrange(
            "p (i t j) -> p i t j", i=5, t=NT)
        l3v = edge_col[:, 5 * NT * NJ:7 * NT * NJ].rearrange(
            "p (t j) -> p t j", t=NT)
        bqk = cols[:, 0:3 * BLOCKS * KT].rearrange("p (i n) -> p i n", i=3)
        l3col = cols[:, 3 * BLOCKS * KT:VECS - 1].rearrange("p (i n) -> p i n", i=4)
        bconv = cols[:, VECS - 1:VECS]
        freq_i = fcol[0:2 * NF, 0:1].bitcast(I32)
        edge = z
        yT = arena3[:, 0:2 * KT * NP].rearrange("p (s k n) -> p s k n", s=2, k=KT)
        pT = arena3[:, :].rearrange("p (s k n) -> p s k n", s=2, k=NT)
        staged = [raw[:, i, :] for i in range(OUTER)] + [xn[:, i, :] for i in range(STAGE - OUTER)]
        qT = arena1[:, 0:2 * HEADS * NP].rearrange("p (s k n) -> p s k n", s=2, k=HEADS)
        kT = arena1[:, 2 * HEADS * NP:4 * HEADS * NP].rearrange("p (s k n) -> p s k n", s=2, k=HEADS)
        adj = arena1[:, 0:2 * NT * NP].rearrange("p (s k n) -> p s k n", s=2, k=NT)
        vrow = arena2[:, :].rearrange("p (s k n) -> p s k n", s=2, k=NT)
        h0 = arena2[:, 0:2 * NT * P].rearrange("p (s k n) -> p s k n", s=2, k=NT)
        aT = arena2[:, 2 * NT * P:2 * NT * P + 2 * NP].rearrange("p (s n) -> p s n", s=2)
        bc_hl = arena2[:, 2 * NT * P + 2 * NP:2 * NT * P + 2 * NP + 2 * P].rearrange("p (s n) -> p s n", s=2)
        adjacc = acc[:, 0:NT * 2 * ACCW].rearrange("p (t c n) -> p t c n", t=NT, c=2)
        cnt_acc = adjacc[:, :, 0, 0:NP]
        w_acc = adjacc[:, :, 1, 0:NP]
        hot_src = [m[:, :, :].rearrange("p t n -> p (t n)").bitcast(BF16)[:, b * CH * NP:(b + 1) * CH * NP].rearrange(
            "p (j n) -> p j n", j=CH) for m in (mask, z) for b in range(2)]
        hot_abs = [mask[:, NT - 1, :].bitcast(BF16)[:, b * NP:(b + 1) * NP] for b in range(2)]
        tmp64 = [mask[0:2 * NF, i, :] for i in range(NT)]
        pbuf = acc[:, 0:4 * NP].rearrange("p (b n) -> p b n", b=4)
        rbuf = acc[:, 4 * NP:6 * NP].rearrange("p (b n) -> p b n", b=2)
        ybuf = acc[:, 6 * NP:6 * NP + 2 * D].rearrange("p (b n) -> p b n", b=2)
        vbuf = acc[:, 6 * NP + 2 * D:6 * NP + 4 * D].rearrange("p (b n) -> p b n", b=2)
        t1 = w_acc[:, 0:2, 0:D]
        t2 = w_acc[:, 2:4, 0:D]
        sg = z[:, 0:2, :]
        maskT = acc[:, 0:NT * NP].rearrange("p (t n) -> p t n", t=NT)
        ebuf = [xn[:, :, :].rearrange("p b n -> p (b n)")[:, 0:NP]] + [
            hot_dst[:, :, :, :].rearrange("p b j n -> p (b j n)").bitcast(F32)[:, i * NP:(i + 1) * NP] for i in range(2)] + [
            raw[:, :, :].rearrange("p b n -> p (b n)")[:, 0:NP]]
        vbrow = [bias[:, :, :].rearrange("p b n -> p (b n)")[:, i * NP:(i + 1) * NP] for i in range(2)]
        den_row = [b[:, :, :].rearrange("p b n -> p (b n)")[:, NP:NP + n] for b, n in zip((raw, xn), ROW_SPLIT)]
        l3rows = arena1[0:2 * NJ, 0:2 * NP].rearrange("p (s n) -> p s n", s=2)
        l3pick = arena1[0:2 * NJ, 2 * NP:2 * NP + 2 * NJ]
        l3pair = arena1[0:NJ, 2 * NP + 2 * NJ:2 * NP + 2 * NJ + NJ * L3C]
        Hx = acc[:, NT * NP:NT * NP + NT * NJ // 2 * 3 * L3C].rearrange("p (t k c) -> p t k c", t=NT, k=NJ // 2)
        fT = z[:, :, :].rearrange("p t n -> p (t n)").rearrange("p (k n) -> p k n", k=KT)
        comb = fT
        combT = yT

        psum = ctx.enter_context(nc.psum_tensor("psum", [P, 2 * NBIG + NROW, D], F32))
        big = [psum[:, 2 * i:2 * i + 2, :] for i in range(NBIG)]
        row = [psum[:, 2 * NBIG + i, :] for i in range(NROW)]
        den_col = psum[:, 2 * NBIG + 1, D - NT * NJ:D]

        def bwide(u):
            return big[u % NBIG][:, :, 0:HALF]

        def bflat(u):
            return big[u % NBIG][:, :, :].rearrange("p h n -> p (h n)")[:, 0:NP]

        def scat(b):
            return big[b // 2][:, b % 2, 0:NT * 2 * WIN]

        def brow(u):
            return row[u % NROW][:, :]

        big_full = sem("big_full")
        big_read = sem("big_read")
        row_full = sem("row_full")
        row_read = sem("row_read")
        raw_ld = [sem(f"raw_ld{i}") for i in range(STAGE)]
        split_done = sem("split_done")
        x_clear = sem("x_clear")
        x_ld = sem("x_ld")
        e_clear = sem("e_clear")
        e_ld = sem("e_ld")
        f_ld = sem("f_ld")
        cb_one = sem("cb_one")
        col_ld = sem("col_ld")
        vec_ld = sem("vec_ld")
        bias_ld = sem("bias_ld")
        const0 = sem("const0")
        const1 = sem("const1")
        dstep = sem("dstep")
        gstep = sem("gstep")
        diag_up = sem("diag_up")
        emb_up = sem("emb_up")
        sin_done = sem("sin_done")
        sig_done = sem("sig_done")
        silu_up = sem("silu_up")
        condT_up = sem("condT_up")
        hot_src_up = sem("hot_src_up")
        hot_abs_up = sem("hot_abs_up")
        hot_act_up = sem("hot_act_up")
        hot_dst_up = sem("hot_dst_up")
        hot_w_up = sem("hot_w_up")
        scat_full = sem("scat_full")
        scat_read = sem("scat_read")
        w_ready = sem("w_ready")
        w_up = sem("w_up")
        whi_up = sem("whi_up")
        wlo_up = sem("wlo_up")
        chi_up = sem("chi_up")
        clo_up = sem("clo_up")
        dpow_up = sem("dpow_up")
        dinv_up = sem("dinv_up")
        bconv_up = sem("bconv_up")
        st_up = sem("st_up")
        aggr_up = sem("aggr_up")
        eps_up = sem("eps_up")
        rstd_up = sem("rstd_up")
        xn_up = sem("xn_up")
        z_up = sem("z_up")
        y1_up = sem("y1_up")
        yhi_up = sem("yhi_up")
        h0hi_up = sem("h0hi_up")
        ahi_up = sem("ahi_up")
        zhi_up = sem("zhi_up")
        xb_up = sem("xb_up")
        gate_up = sem("gate_up")
        l1p_up = sem("l1p_up")
        x_up = sem("x_up")
        ln_up = sem("ln_up")
        clamp_up = sem("clamp_up")
        pen_up = sem("pen_up")
        mask_up = sem("mask_up")
        qkhi_up = sem("qkhi_up")
        vhi_up = sem("vhi_up")
        vlo_up = sem("vlo_up")
        exp_up = sem("exp_up")
        rden_up = sem("rden_up")
        pn_up = sem("pn_up")
        phi_up = sem("phi_up")
        ohi_up = sem("ohi_up")
        hhi_up = sem("hhi_up")
        hlo_up = sem("hlo_up")
        shi_up = sem("shi_up")
        pass_up = sem("pass_up")
        m3_up = sem("m3_up")
        one_up = sem("one_up")
        l3hi_up = sem("l3hi_up")
        hx_up = sem("hx_up")
        prod_up = sem("prod_up")
        att_up = sem("att_up")
        as_up = sem("as_up")
        am_up = sem("am_up")
        v_up = sem("v_up")
        e_up = sem("e_up")
        em_up = sem("em_up")
        p_up = sem("p_up")
        p_used = sem("p_used")
        den_up = sem("den_up")
        den_full = sem("den_full")
        rec_up = sem("rec_up")
        comb_lo_up = sem("comb_lo_up")
        comb_hi_up = sem("comb_hi_up")
        bn_up = sem("bn_up")
        bn_eps_up = sem("bn_eps_up")
        bn_rstd_up = sem("bn_rstd_up")
        sh_up = sem("sh_up")
        fn_up = sem("fn_up")
        stored = sem("stored")

        def slot(n):
            return (n - S_COND) % STAGE if S_COND <= n < S_L3 else n % OUTER

        def ld_count(n):
            dmas = {S_COND + i: 6 for i in range(4)}
            for b in range(BLOCKS):
                dmas |= {S_BLK + b * S_PERBLK + PERBLK + i: 6 for i in range(4)}
            return sum(16 * dmas.get(i, 1) for i in range(n + 1) if slot(i) == slot(n))

        LD_PERBLK = ld_count(S_BLK + S_PERBLK) - ld_count(S_BLK)

        PV_COLS = {"PVa": slice(0, ROW_SPLIT[0]), "PVb": slice(ROW_SPLIT[0], NP)}

        def ringpart(m):
            return ringw[:, m % RING, 0, :], ringw[:, m % RING, 1, :]

        def wait_apart(eng, semaphore, value):
            eng.wait_ge(semaphore, value)
            if not isinstance(value, int):
                eng.nop(nofuse=True)

        block = ctx.enter_context(nc.Block())

        def item_used(eng, n):
            j, st = divmod(n, NT)
            if st < NT - 1:
                eng.wait_ge(p_used, j * (NT - 1) + st + 1)
            else:
                eng.wait_ge(row_full, ROW3[f"P{j}b"] + 1)

        def pool_l3(g, rstd_of, rest):
            def item(i):
                rest(S_L3 + i, ringpart(RING_L3 + i))

            for i in range(3, NT):
                rstd_of(LN_L3 - NT + i, NT + i)
            for i in range(4):
                item(i)
                rstd_of(LN_L3 + i, i)
            rstd_of(LN_L3 + NT - 1, NT - 1)
            g.wait_ge(big_full, BIGB + BLOCKS * len(BLOCK_BIG) + AHEAD)
            for t in range(NT):
                g.tensor_scalar(mask[:, t, :], mask[:, t, :], DH ** -0.5, flag[:, 3, t:t + 1], ALU.mult, ALU.add).then_inc(m3_up, 1)
            g.memset(Hx[:, :, :, L3C:2 * L3C], 1.0).then_inc(one_up, 1)
            for i in range(KT):
                item(KT + i)
            for n in range(NJ * NT):
                j, st = divmod(n, NT)
                if st < NT - 1:
                    g.wait_ge(e_up, j * (NT - 1) + st + 1)
                else:
                    g.wait_ge(big_read, BIG3[f"va{j}"] + 1)
                m = mask[:, st, :] if j < L3H else maskT[:, st, :]
                g.tensor_tensor(ebuf[n % NE], ebuf[n % NE], m, ALU.add).then_inc(em_up, 1)
            for o in range(KT):
                g.wait_ge(bn_up, 3 * o + 3)
                g.tensor_scalar(bnc[:, 0, o:o + 1], mv3[:, o, 1:2], EPS, 1.0, ALU.add, ALU.mult).then_inc(bn_eps_up, 1)
                g.wait_ge(bn_eps_up, o + 1)
                g.tensor_tensor(bnc[:, 1, o:o + 1], bnc[:, 0, o:o + 1], half[:, 0:1], ALU.pow).then_inc(bn_rstd_up, 1)

        def act_l3(act, high, turned_relu):
            def item(i):
                high(S_L3 + i, ringpart(RING_L3 + i)[0])

            act.wait_ge(row_read, ROWB + BLOCKS * len(BLOCK_ROW))
            for i, n in enumerate(("L3_gnn_att_src_", "L3_gnn_att_dst_")):
                for d in range(2):
                    act.dma_start(bias[:, i, d * L3H * L3C:(d + 1) * L3H * L3C],
                                  a[n + "fb"[d]].rearrange("h c -> (h c)").partition_broadcast(P)).then_inc(bias_ld, 16)
            act.activation(l3pick, ident[0:2 * NJ, 0:2 * NJ], ACT.Copy).then_inc(l3hi_up, 1)
            act.activation(l3pair.rearrange("p (j c) -> p j c", j=NJ), ident[0:NJ, 0:NJ].unsqueeze(2).broadcast_to([NJ, NJ, L3C]),
                           ACT.Copy).then_inc(l3hi_up, 1)
            for t in range(NT):
                if t < 4:
                    item(2 + t)
                turned_relu(BIG3[f"l3_{t}"], 0, t)
            for t in range(NT):
                act.wait_ge(row_full, ROW3[f"H{t}"] + 1)
                act.activation(Hx[:, t, :, :].rearrange("p k (s c) -> p k s c", s=3)[:, :, 0:3:2, :],
                               brow(ROW3[f"H{t}"]).rearrange("p (k s c) -> p k s c", k=NJ // 2, s=2), ACT.Copy).then_inc(hx_up, 1)
            act.wait_ge(big_read, BIG3["mt0"])
            for t in range(NT):
                act.wait_ge(big_full, BIG3[f"mt{t}"] + 1)
                act.activation(maskT[:, t, :], bflat(BIG3[f"mt{t}"]), ACT.Copy).then_inc(big_read, 1)
            item(6)
            item(7)

            def rows_high(name, rows):
                act.wait_ge(big_full, BIG3[name] + 1)
                act.activation(l3rows[0:rows, 0, :], bflat(BIG3[name])[0:rows, :], ACT.Copy).then_inc(l3hi_up, 1)

            def sums(j):
                mine, other = (j % 2) * L3C, (1 - j % 2) * L3C
                act.wait_ge(row_full, ROW3[f"P{j}b"] + 1)
                if j >= 2:
                    act.wait_ge(den_full, j - 1)
                for h in range(2):
                    act.activation(den_row[h][other:other + 1], brow(ROW3[f"P{j}{'ab'[h]}"])[other:other + 1, 0:ROW_SPLIT[h]], ACT.Copy).then_inc(den_up, 1)
                for h in range(2):
                    act.activation(comb[mine:mine + L3C, j // 2, h * ROW_SPLIT[0]:h * ROW_SPLIT[0] + ROW_SPLIT[h]],
                                   brow(ROW3[f"P{j}{'ab'[h]}"])[mine:mine + L3C, 0:ROW_SPLIT[h]], ACT.Copy).then_inc(row_read, 1)

            rows_high("as", NJ)
            rows_high("vt", 2 * NJ)
            act.wait_ge(as_up, 2)

            def comb_high(k):
                act.wait_ge(big_read, BIG3[f"rb{k}"] + 1)
                act.activation(combT[:, 0, k, :], comb[:, k, :], ACT.Identity, bias=l3col[:, 0, k:k + 1]).then_inc(comb_hi_up, 1)

            for n in range(NJ * NT):
                j, st = divmod(n, NT)
                act.wait_ge(em_up, n + 1)
                act.activation(ebuf[n % NE], ebuf[n % NE], ACT.Exp, bias=l3s[:, 4, st, j:j + 1]).then_inc(p_up, 1)
                if st == 0 and j:
                    sums(j - 1)
            sums(NJ - 1)
            rows_high("rec", NJ)
            for k in range(KT):
                comb_high(k)
            for o in range(KT):
                act.wait_ge(sh_up, 3 * o + 3)
                act.activation(fT[:, o, :], fT[:, o, :], ACT.Relu, bias=bnc[:, 3, o:o + 1], scale=bnc[:, 2, o:o + 1]).then_inc(fn_up, 1)

        def pe_l3(pe, turn_norm):
            for t in range(NT):
                turn_norm(BIG3[f"l3_{t}"], XN_L3 + t, t)
            pe.wait_ge(split_done, S_L3 + KT)
            for t in range(NT):
                u = ROW3[f"H{t}"]
                free_row(pe, u)
                pe.wait_ge(big_read, BIG3[f"l3_{t}"] + 1)
                w = L3H * L3C
                for d in range(2):
                    def weight(k):
                        return [r[:, (k % 2) * w:(k % 2 + 1) * w] for r in ringpart(RING_L3 + 2 * d + k // 2)]
                    ins = row_mm(pe, brow(u)[:, d * w:(d + 1) * w], sum([parts(tile_of(yT, k, t), weight(k)) for k in range(KT)], []))
                ins.then_inc(row_full, 1)
            pe.wait_ge(m3_up, NT)
            for t in range(NT):
                u = BIG3[f"mt{t}"]
                free_big(pe, u)
                for st in range(NT):
                    ins = pe.transpose(bflat(u)[:, st * P:(st + 1) * P], mask[:, st, t * P:(t + 1) * P], ident[:, :])
                ins.then_inc(big_full, 1)
            u = BIG3["as"]
            free_big(pe, u)
            pe.wait_ge(att_up, 2 * NT)
            for t in range(NT):
                ins = pe.transpose(bflat(u)[0:NJ, t * P:(t + 1) * P], l3s[:, 0, t, :], ident[:, :])
            ins.then_inc(big_full, 1)
            pe.wait_ge(big_read, u + 1)

            def spread(u, i, n):
                free_big(pe, u)
                pick = l3pick[0:n, i:i + 1].broadcast_to([n, P])
                wide_mm(pe, u, [(pick, l3rows[0:n, part, :]) for part in range(2)]).then_inc(big_full, 1)

            for j in range(NJ):
                spread(BIG3[f"am{j}"], j, NJ)
            u = BIG3["vt"]
            free_big(pe, u)
            pe.wait_ge(v_up, 2)
            for t in range(NT):
                ins = pe.transpose(bflat(u)[0:2 * NJ, t * P:(t + 1) * P], l3v[:, t, :], ident[:, :])
            ins.then_inc(big_full, 1)
            pe.wait_ge(big_read, u + 1)
            pe.wait_ge(one_up, 1)

            def den_turn(j):
                at = (1 - j % 2) * L3C
                pe.wait_ge(den_up, 2 * j + 2)
                pe.wait_ge(row_read, ROW3[f"P{j}b"] + 1)
                for t in range(NT):
                    h, c = (0, t * P) if t < 3 else (1, t * P - ROW_SPLIT[0])
                    ins = pe.matmul(den_col[:, t * NJ + j:t * NJ + j + 1], den_row[h][at:at + 1, c:c + P], ident[at:at + 1, at:at + 1],
                                    start=True, stop=True, skip_group_check=True)
                ins.then_inc(den_full, 1)

            spread(BIG3["vb0"], NJ, 2 * NJ)
            spread(BIG3["vb1"], NJ + 1, 2 * NJ)
            spread(BIG3["va0"], 0, 2 * NJ)
            for n in range(NJ * NT):
                j, st = divmod(n, NT)
                if st == 0:
                    if j + 2 < NJ:
                        spread(BIG3[f"vb{j + 2}"], NJ + j + 2, 2 * NJ)
                    if j + 1 < NJ:
                        spread(BIG3[f"va{j + 1}"], j + 1, 2 * NJ)
                    free_row(pe, ROW3[f"P{j}b"])
                    if j:
                        den_turn(j - 1)
                pe.wait_ge(p_up, n + 1)
                lhs = Hx[:, st, j // 2, (j % 2) * L3C:(j % 2 + 2) * L3C]
                for h in range(2):
                    lo = h * ROW_SPLIT[0]
                    ins = pe.matmul(brow(ROW3[f"P{j}{'ab'[h]}"])[:, 0:ROW_SPLIT[h]], lhs, ebuf[n % NE][:, lo:lo + ROW_SPLIT[h]],
                                    start=(st == 0), stop=(st == NT - 1))
                ins.then_inc(*((p_used, 1) if st < NT - 1 else (row_full, 2)))
            den_turn(NJ - 1)
            u = BIG3["rec"]
            free_big(pe, u)
            pe.wait_ge(rec_up, 2)
            for t in range(NT):
                ins = pe.transpose(bflat(u)[0:NJ, t * P:(t + 1) * P], l3s[:, 2, t, :], ident[:, :])
            ins.then_inc(big_full, 1)
            pe.wait_ge(big_read, u + 1)
            for k in range(KT):
                u = BIG3[f"rb{k}"]
                free_big(pe, u)
                wide_mm(pe, u, [(l3pair[:, k * P:(k + 1) * P], l3rows[0:NJ, part, :]) for part in range(2)]).then_inc(big_full, 1)
            for o in range(KT):
                u = BIG3[f"f{o}"]
                free_big(pe, u)
                pe.wait_ge(comb_lo_up, KT)
                pe.wait_ge(split_done, S_L3 + KT + o + 1)
                wide_mm(pe, u, sum([parts(wcol(RING_L3 + KT + o, k), both(combT, k)) for k in range(KT)], [])).then_inc(big_full, 1)
            pe.wait_ge(fn_up, KT)
            for t in range(NT):
                u = ROW3[f"y{t}"]
                free_row(pe, u)
                for o in range(KT):
                    ins = pe.transpose(brow(u)[:, o * P:(o + 1) * P], fT[:, o, t * P:(t + 1) * P], ident[:, :])
                ins.then_inc(row_full, 1)

        def dve_l3(dve, tile_stats, relu_norm, step):
            f32 = lambda ap: ap.bitcast(F32)
            for t in range(NT):
                dve.wait_ge(x_up, NT + t + 1)
                tile_stats(LN_L3 + t, t, x[:, t, :])
            dve.wait_ge(split_done, S_L3)
            relu_norm(LN_L3, 0, [BIG3[f"l3_{t}"] for t in range(NT)], 2 * NT + BLOCKS * 2 * NT + 1)
            dve.wait_ge(bias_ld, 48 * BLOCKS + 64)
            for t in range(NT):
                u = ROW3[f"H{t}"]
                dve.wait_ge(hx_up, t + 1)
                if t:
                    dve.wait_ge(att_up, 2 * t)
                for i in range(2):
                    dve.tensor_tensor(ebuf[i][:, 0:D], brow(u), bias[:, i, :], ALU.mult).then_inc(*((row_read, 1) if i else (prod_up, 1)))
                dve.wait_ge(prod_up, t + 1)
                dve.wait_ge(row_read, u + 1)
                for i in range(2):
                    dve.tensor_reduce(l3s[:, i, t, :], ebuf[i][:, 0:D].rearrange("p (j c) -> p j c", j=NJ), AX.X, ALU.add).then_inc(att_up, 1)
            dve.wait_ge(att_up, 2 * NT)
            dve.tensor_scalar(l3s[:, 3, :, :], l3s[:, 0, :, :], 0.8, None, ALU.mult).then_inc(as_up, 1)
            dve.tensor_scalar(l3s[:, 4, :, :], l3s[:, 0, :, :], 0.2, None, ALU.mult).then_inc(as_up, 1)

            def rows_rest(name, rows, nth):
                u = BIG3[name]
                dve.wait_ge(big_read, u)
                dve.wait_ge(l3hi_up, nth)
                dve.tensor_tensor(l3rows[0:rows, 1, :], bflat(u)[0:rows, :], f32(l3rows[0:rows, 0, :]), ALU.subtract).then_inc(big_read, 1)

            rows_rest("as", NJ, 3)
            dve.wait_ge(m3_up, NT)
            for j in range(NJ):
                u = BIG3[f"am{j}"]
                dve.wait_ge(big_full, u + 1)
                if j:
                    dve.wait_ge(big_read, u)
                for t in range(NT):
                    if t >= 3:
                        dve.wait_ge(am_up, j * (NT - 1) + t - 2)
                    m = maskT[:, t, :] if j < L3H else mask[:, t, :]
                    ins = dve.tensor_tensor_reduce(wide(ebuf[t % 3]), bwide(u), wide(m), 1.0, -3e38, ALU.add, ALU.max, l3s[:, 2, t, j:j + 1])
                    ins.then_inc(*((am_up, 1) if t < NT - 1 else (big_read, 1)))
            dve.wait_ge(big_read, BIG3[f"am{NJ - 1}"] + 1)
            step(dve.tensor_tensor(l3s[:, 2, :, :], l3s[:, 2, :, :], l3s[:, 1, :, :], ALU.add))
            step(dve.scalar_tensor_tensor(l3s[:, 2, :, :], l3s[:, 2, :, :], 0.2, l3s[:, 2, :, :], ALU.mult, ALU.max))
            dve.tensor_tensor(l3v[:, :, 0:NJ], l3s[:, 1, :, :], l3s[:, 2, :, :], ALU.subtract).then_inc(v_up, 1)
            dve.scalar_tensor_tensor(l3v[:, :, NJ:2 * NJ], l3s[:, 1, :, :], 0.2, l3s[:, 2, :, :], ALU.mult, ALU.subtract).then_inc(v_up, 1)
            rows_rest("vt", 2 * NJ, 4)
            dve.wait_ge(split_done, S_L3 + 2 * KT)

            def comb_rest(k):
                dve.wait_ge(comb_hi_up, k + 1)
                dve.scalar_tensor_tensor(combT[:, 1, k, :], comb[:, k, :], l3col[:, 0, k:k + 1], f32(combT[:, 0, k, :]),
                                         ALU.add, ALU.subtract).then_inc(comb_lo_up, 1)

            def second_branch(j):
                u = BIG3[f"vb{j}"]
                dve.wait_ge(big_full, u + 1)
                if j >= 2:
                    dve.wait_ge(big_read, BIG3[f"va{j - 2}"] + 1)
                dve.tensor_copy(wide(vbrow[j % 2]), bwide(u)).then_inc(big_read, 1)

            second_branch(0)
            for n in range(NJ * NT):
                j, st = divmod(n, NT)
                u = BIG3[f"va{j}"]
                if st == 0:
                    if j < NJ - 1:
                        second_branch(j + 1)
                    dve.wait_ge(big_full, u + 1)
                    dve.wait_ge(big_read, BIG3[f"vb{j}"] + 1)
                if n >= NE:
                    item_used(dve, n - NE)
                ins = dve.scalar_tensor_tensor(wide(ebuf[n % NE]), bwide(u), l3s[:, 3, st, j:j + 1], wide(vbrow[j % 2]), ALU.add, ALU.max)
                ins.then_inc(*((e_up, 1) if st < NT - 1 else (big_read, 1)))
            dve.wait_ge(den_full, NJ)
            sums = l3s[:, 2, :, :].rearrange("p t j -> p (t j)")
            dve.tensor_scalar(sums, den_col, 1e-16, None, ALU.add).then_inc(rec_up, 1)
            dve.wait_ge(rec_up, 1)
            dve.reciprocal(sums, sums).then_inc(rec_up, 1)
            rows_rest("rec", NJ, 5)
            for k in range(KT + 1):
                if k < KT:
                    u = BIG3[f"rb{k}"]
                    dve.wait_ge(big_full, u + 1)
                    dve.wait_ge(row_read, ROW3[f"P{2 * k + 1}b"] + 1)
                    dve.tensor_tensor(wide(comb[:, k, :]), bwide(u), wide(comb[:, k, :]), ALU.mult).then_inc(big_read, 1)
                if k:
                    comb_rest(k - 1)
            for o in range(KT):
                u = BIG3[f"f{o}"]
                dve.wait_ge(big_full, u + 1)
                dve.tensor_scalar(wide(fT[:, o, :]), bwide(u), l3col[:, 1, o:o + 1], None, ALU.add).then_inc(big_read, 1)
                dve.wait_ge(big_read, u + 1)
                for i, (lo, hi) in enumerate(((0, HALF), (HALF, N))):
                    dve.bn_stats(bn3[:, o, i, :], fT[:, o, lo:hi]).then_inc(bn_up, 1)
                dve.wait_ge(bn_up, 3 * o + 2)
                dve.bn_aggr(mv3[:, o, :], bn3[:, o, :, :]).then_inc(bn_up, 1)
                dve.wait_ge(bn_up, 3 * o + 3)
                dve.wait_ge(bn_rstd_up, o + 1)
                dve.tensor_tensor(bnc[:, 2, o:o + 1], bnc[:, 1, o:o + 1], l3col[:, 2, o:o + 1], ALU.mult).then_inc(sh_up, 1)
                dve.wait_ge(sh_up, 3 * o + 1)
                dve.tensor_tensor(bnc[:, 3, o:o + 1], mv3[:, o, 0:1], bnc[:, 2, o:o + 1], ALU.mult).then_inc(sh_up, 1)
                dve.wait_ge(sh_up, 3 * o + 2)
                dve.tensor_tensor(bnc[:, 3, o:o + 1], l3col[:, 3, o:o + 1], bnc[:, 3, o:o + 1], ALU.subtract).then_inc(sh_up, 1)
            for t in range(NT):
                u = ROW3[f"y{t}"]
                dve.wait_ge(row_full, u + 1)
                dve.tensor_tensor(x[:, t, :], x[:, t, :], brow(u), ALU.add).then_inc(row_read, 1)

        def finish(sp):
            for t in range(NT):
                sp.wait_ge(row_read, ROW3[f"y{t}"] + 1)
                rows = TAIL if t == NT - 1 else P
                sp.dma_start(out[t * P:t * P + rows, :], x[0:rows, t, :]).then_inc(stored, 16)
            sp.wait_ge(stored, 16 * NT)

        @block.sync
        def _(sp):
            full = (NG - 1) * GROUP
            dst_to = edge[:, 1, :].bitcast(I32)
            sp.dma_start(dst_to[NG - 1:NG, ELAST:GROUP], a["dst"][E - (GROUP - ELAST):E].rearrange("(o e) -> o e", o=1)).then_inc(e_ld, 16)
            for i, lst in ((1, a["dst"]), (0, a["src"]), (2, a["edge_weight"])):
                if i == 0:
                    sp.wait_ge(e_clear, 2)
                to = edge[:, i, :] if i == 2 else edge[:, i, :].bitcast(I32)
                sp.dma_start(to[0:NG - 1, :], lst[0:full].rearrange("(g e) -> g e", e=GROUP)).then_inc(e_ld, 16)
                sp.dma_start(to[NG - 1:NG, 0:ELAST], lst[full:E].rearrange("(o e) -> o e", o=1)).then_inc(e_ld, 16)
            sp.wait_ge(x_clear, 1)
            sp.dma_start(x[:, 0:NT - 1, :], a["x"][0:(NT - 1) * P, :].rearrange("(t p) d -> p t d", p=P)).then_inc(x_ld, 16)
            sp.dma_start(x[0:TAIL, NT - 1, :], a["x"][(NT - 1) * P:N, :]).then_inc(x_ld, 16)

            def stage(n, src, it=0):
                if n >= OUTER:
                    before = n - (STAGE if S_COND <= n < S_L3 else OUTER)
                    sp.wait_ge(split_done, before + 1 + it * S_PERBLK)
                to = staged[slot(n)]
                if len(src.shape) == 3:
                    to = to.rearrange("p (k c) -> p k c", k=src.shape[1])
                sp.dma_start(to, src).then_inc(raw_ld[slot(n)], 16)

            def stage_cond(n, w, b, extra, it=0):
                before = n - (OUTER if slot(n) < OUTER else STAGE)
                sp.wait_ge(split_done, before + 1 + it * S_PERBLK)
                for i in range(4):
                    sp.dma_start(staged[slot(n)][32 * i:32 * i + C16, :], w).then_inc(raw_ld[slot(n)], 16)
                sp.dma_start(staged[slot(n)][C16:P:32, :], b.unsqueeze(0).broadcast_to([4, D])).then_inc(raw_ld[slot(n)], 16)
                c = extra.shape[1]
                sp.dma_start(staged[slot(n)][C16 + 1:P:32, :].rearrange("p (k c) -> p k c", c=c),
                             extra[0:4, :].unsqueeze(1).broadcast_to([4, D // c, c])).then_inc(raw_ld[slot(n)], 16)

            def columns(w, h):
                return w[:, h * P:(h + 1) * P].rearrange("(k p) c -> p k c", p=P)

            zeros = ident[:, P // 2:P]
            conds = [(a["L2_gnn_s1_w"], a["L2_gnn_s1_b"], ones), (a["L2_gnn_b1_w"], a["L2_gnn_b1_b"], zeros),
                     (a["L2_gnn_s2_w"], a["L2_gnn_s2_b"], ones), (a["L2_gnn_b2_w"], a["L2_gnn_b2_b"], zeros)]
            by_col = {WQ: a["L2_gnn_wq"], WK: a["L2_gnn_wk"], W1: a["L2_gnn_m_w1"]}
            by_row = {WV: a["L2_gnn_wv"], WO: a["L2_gnn_wo"], W2: a["L2_gnn_m_w2"]}

            stage(Q_CONV, columns(a["L0_gnn_W_conv"], 0))
            stage(Q_LIN, a["L0_gnn_W_lin"])
            v0 = 0
            for b in ("bq", "bk", "m_b1"):
                sp.dma_start(vec[v0:v0 + BLOCKS * KT, :], a["L2_gnn_" + b].rearrange("b (k p) -> (b k) p", p=P)).then_inc(vec_ld, 16)
                v0 += BLOCKS * KT
            for b in ("L3_gnn_bias_f", "L3_gnn_bias_b", "L3_gnn_b_fuse", "L3_gnn_bn_gamma", "L3_gnn_bn_beta", "L0_gnn_b_conv"):
                v = a[b].rearrange("(k p) -> k p", p=P)
                sp.dma_start(vec[v0:v0 + v.shape[0], :], v).then_inc(vec_ld, 16)
                v0 += v.shape[0]
            assert v0 == VECS
            sp.dma_start(bias[:, 0, :], a["L0_gnn_b_lin"].partition_broadcast(P)).then_inc(col_ld, 16)
            sp.dma_start(bias[:, 1, :], a["L1_gnn_b"].partition_broadcast(P)).then_inc(col_ld, 16)
            for k in range(KT):
                stage(Q_L + k, a["L1_gnn_W_l"][k * P:(k + 1) * P, :])
            for k in range(KT):
                stage(Q_R + k, a["L1_gnn_W_r"][k * P:(k + 1) * P, :])
            sp.wait_ge(const0, 3)
            sp.wait_ge(big_full, BIG0[f"l1_{NT - 1}"] + 1)
            with sp.Fori(0, BLOCKS) as it:
                for i, (w, b, extra) in enumerate(conds):
                    stage_cond(S_COND + i, w[it], b[it], extra, it)
                for q in (WV, WQ, WK, WO, W1, W2):
                    for i in range(KT):
                        src = columns(by_col[q][it], i) if q in by_col else by_row[q][it][i * P:(i + 1) * P, :]
                        stage(S_BLK + q + i, src, it)
            for i, (w, b, extra) in enumerate(conds):
                stage_cond(S_L3 - 4 + i, w[BLOCKS - 1], b[BLOCKS - 1], extra)
            for i, w in enumerate((a["L3_gnn_W_f"], a["L3_gnn_W_b"])):
                for j in range(2):
                    stage(S_L3 + 2 * i + j, w[2 * j * P:2 * (j + 1) * P].rearrange("(k p) h c -> p k (h c)", p=P))
            for i in range(KT):
                stage(S_L3 + KT + i, columns(a["L3_gnn_W_fuse"], i))
            finish(sp)

        def pool_l2(g, rstd_of, rest, rest_cond):
            for i in range(4):
                rest_cond(S_COND + i, i, behind=LN_IN + i - 1 if i else None)
                rstd_of(LN_IN + i, i)
            rstd_of(LN_IN + NT - 1, NT - 1)
            for t in range(3):
                rstd_of(LN_BLK + t, NT + t)
            with g.Fori(0, BLOCKS) as it:
                def rests(q, first, last):
                    for i in range(first, last):
                        rest(S_BLK + q + i, ringpart(RING_BLK + q + i), it)

                def add_bias(ln, t, b):
                    g.wait_ge(y1_up, it * 2 * NT + ln * NT + t + 1)
                    g.tensor_tensor(z[:, t, :], z[:, t, :], bias[:, b, :], ALU.add).then_inc(xb_up, 1)

                rests(WV, 0, 2)
                rstd_of(LN_BLK + it * 2 * NT + 3, NT + 3)
                rests(WV, 2, KT)
                rstd_of(LN_BLK + it * 2 * NT + 4, NT + 4)
                rests(WQ, 0, 2)
                for t in range(NT):
                    g.wait_ge(vhi_up, it * NT + t + 1)
                    g.tensor_tensor(vrow[:, 1, t, :], vbuf[:, t % 2, :], vrow[:, 0, t, :].bitcast(F32), ALU.subtract).then_inc(vlo_up, 1)
                rests(WQ, 2, KT)
                rests(WK, 0, 2)
                g.wait_ge(bias_ld, 48 * it + 48)
                for t in range(NT):
                    add_bias(0, t, 1)
                    rests(WK + 2 + t, 0, 1)
                rests(WO + NT - 2, 0, KT + 4 - NT)
                for k in range(HEADS * NT):
                    wait_apart(g, rden_up, it * HEADS * NT + k + 1)
                    g.tensor_scalar(pbuf[:, k % 4, :], pbuf[:, k % 4, :], rden[:, k:k + 1], flag[:, 1, k % NT:k % NT + 1],
                                    ALU.mult, ALU.mult).then_inc(pn_up, 1)
                for t in range(NT):
                    rstd_of(LN_BLK + it * 2 * NT + NT + t, t)
                rests(W1, 2, KT)
                for t in range(NT):
                    add_bias(1, t, 2)
                    if t in (1, 2):
                        rests(W2, t - 1, t)
                rests(W2, 2, KT)
                for i in range(4):
                    tile = LN_BLK + (it + 1) * 2 * NT + i
                    rest_cond(S_BLK + PERBLK + i, i, it, behind=tile - 2 if i >= 2 else None)
                    if i >= 1:
                        rstd_of(tile - 1, NT + i - 1)

        @block.gpsimd
        def _(g):
            own = [0]

            def step(ins):
                own[0] += 1
                ins.then_inc(gstep, 1)
                g.wait_ge(gstep, own[0])

            step(g.memset(ident[:, :], 0.0))
            g.affine_select(out=ident[:, :], in_=ident[:, :], compare_op=ALU.not_equal, fill=1.0, base=0,
                            pattern=[[-1, P]], channel_multiplier=1).then_inc(const0, 1)
            g.memset(ones[:, :], 1.0).then_inc(const0, 1)
            step(g.memset(half[:, :], -0.5))
            g.iota(iota16[:, :], [[1, NP]], base=0, channel_multiplier=0,
                   allow_small_or_imprecise_dtypes=True).then_inc(const0, 1)
            step(g.memset(fcol[:, :], 0.0))
            g.iota(fcol[0:NF, 0:1].bitcast(I32), [[1, 1]], base=1, channel_multiplier=1).then_inc(const1, 1)
            g.wait_ge(const1, 1)
            g.iota(fcol[NF:2 * NF, 0:1].bitcast(I32), [[1, 1]], base=1, channel_multiplier=1).then_inc(const1, 1)
            g.wait_ge(const1, 2)
            g.memset(tmp64[0][:, N:NP], 0.0).then_inc(const1, 1)
            g.wait_ge(const1, 3)
            g.memset(f_w2[:, :], 0.0).then_inc(const1, 1)
            g.memset(acc[:, 0:NT * ACCW], 0.0).then_inc(scat_read, HOT)
            g.memset(acc[:, NT * ACCW:2 * NT * ACCW], 0.0).then_inc(scat_full, HOT)
            g.wait_ge(f_ld, 16 * F_LOADS)
            for i in range(8):
                if i:
                    g.wait_ge(cb_one, i)
                g.affine_select(out=fcol[:, 2:3], in_=fcol[:, 2:3], compare_op=ALU.not_equal, fill=1.0,
                                base=-(32 * (i // 2) + C16 + i % 2), pattern=[[0, 1]], channel_multiplier=1).then_inc(cb_one, 1)

            def rstd_of(i, slot):
                wait_apart(g, aggr_up, i + 1)
                g.tensor_scalar(veps[:, slot:slot + 1], mv[:, slot, 1:2], EPS, 1.0, ALU.add, ALU.mult).then_inc(eps_up, 1)
                g.wait_ge(eps_up, i + 1)
                g.tensor_tensor(rstd[:, slot:slot + 1], veps[:, slot:slot + 1], half[:, 0:1], ALU.pow).then_inc(rstd_up, 1)

            def rest(n, to, it=0):
                g.wait_ge(shi_up, n + 1 + it * S_PERBLK)
                g.tensor_tensor(to[1], staged[slot(n)], to[0].bitcast(F32), ALU.subtract).then_inc(split_done, 1)

            def rest_cond(n, kind, it=0, behind=None):
                if behind is None:
                    g.wait_ge(split_done, n + it * S_PERBLK)
                else:
                    g.wait_ge(rstd_up, behind + 1)
                r = staged[slot(n)]
                to = condw[:, kind, :]
                g.wait_ge(shi_up, n + 1 + it * S_PERBLK)
                lo = slice(P // 2, P)
                g.tensor_tensor(to[lo, :], r[lo, :], to[lo, :].bitcast(F32), ALU.subtract).then_inc(split_done, 1)
                g.wait_ge(split_done, n + 1 + it * S_PERBLK)

            for t in range(NT):
                rstd_of(t, t)
            for m in range(2):
                rest(m, ringpart(m))
            g.wait_ge(w_ready, 2)
            passes = g.value_load(span_i[0:1, 1:2], min_val=0, max_val=NP // WIN)
            with g.Fori(0, passes + 1) as kp:
                with g.Fori(0, NG // HOT) as gi:
                    for b in range(HOT):
                        gr = gi * HOT + b
                        c = kp * NG + gr + 1
                        hot = hot_dst[:, b, :, 0:WIN]
                        g.wait_ge(hot_dst_up, c)
                        for i in range(3):
                            ins = g.tensor_tensor(
                                hot_dst[:, b, :, (i + 1) * WIN:(i + 2) * WIN], hot,
                                w_part[:, i, :, bass.ds(gr, 1)].broadcast_to([P, CH, WIN]), ALU.mult)
                        ins.then_inc(hot_w_up, 1)
            g.wait_ge(w_up, 1)
            g.tensor_tensor(degs[:, 2, :], degs[:, 1, :], half[:, :], ALU.pow).then_inc(dpow_up, 1)
            for m in range(2, 4):
                rest(m, ringpart(m))
            for t in range(NT):
                g.wait_ge(xn_up, t + 1)
                g.wait_ge(row_read, ROW0["brow"] + 1)
                g.tensor_tensor(x[:, t, :], x[:, t, :], bias[:, 0, :], ALU.add).then_inc(xb_up, 1)
            for m in range(4, RING + 1):
                rest(m, ringpart(m))
            for t in range(NT):
                rstd_of(LN_L1 + t, NT + t)
            for m in range(RING + 1, RING_BLK):
                rest(m, ringpart(m))
            pool_l2(g, rstd_of, rest, rest_cond)
            pool_l3(g, rstd_of, rest)

        def act_l2(act, high):
            def turned(ln, t, b):
                u = BIGBLK[f"t{ln}_{t}"]
                act.wait_ge(big_full, u + b * len(BLOCK_BIG) + 1)
                act.activation(yT[:, 0, :, t * P:(t + 1) * P], bflat(u)[:, 0:D].rearrange("p (k n) -> p k n", k=KT),
                               ACT.Copy).then_inc(yhi_up, 1)

            for i in range(2):
                high(S_BLK + i, ringpart(RING_BLK + i)[0])
            turned(0, 0, 0)
            with act.Fori(0, BLOCKS) as it:
                nb, nr = it * len(BLOCK_BIG), it * len(BLOCK_ROW)

                def highs(q, first, last):
                    for i in range(first, last):
                        high(S_BLK + q + i, ringpart(RING_BLK + q + i)[0], it)

                def value(t):
                    act.wait_ge(row_read, ROWBLK[f"v{t}"] + nr + 1)
                    act.activation(vrow[:, 0, t, :], vbuf[:, t % 2, :], ACT.Copy).then_inc(vhi_up, 1)

                act.wait_ge(row_full, ROWB + nr)
                highs(WV, 2, KT)
                turned(0, 1, it)
                act.wait_ge(row_read, ROWB + nr)
                for i, b in enumerate(("bv", "bo", "m_b2")):
                    act.dma_start(bias[:, i, :], a["L2_gnn_" + b][it].partition_broadcast(P)).then_inc(bias_ld, 16)
                highs(WQ, 0, 1)
                turned(0, 2, it)
                highs(WQ, 1, 2)
                for t in range(NT):
                    value(t)
                    if t + 3 < NT:
                        turned(0, t + 3, it)
                highs(WQ, 2, KT)
                highs(WK, 0, 2)
                for i, to in enumerate((qT, kT)):
                    for h in range(HEADS):
                        u = BIGBLK["qk"[i] + str(h)]
                        act.wait_ge(big_full, u + nb + 1)
                        act.activation(wide(to[:, 0, h, :]), bwide(u), ACT.Identity,
                                       bias=bqk[:, i, bass.ds(it * KT + h, 1)]).then_inc(qkhi_up, 1)
                        n = i * HEADS + h + 2
                        highs((WK, WO, W1)[n // KT], n % KT, n % KT + 1)
                for what, k in ATT_ACT:
                    if what == "S":
                        act.wait_ge(big_read, BIGBLK[f"S{k}"] + nb + 1)
                        act.activation(pbuf[:, k % 4, :], pbuf[:, k % 4, :], ACT.Exp, bias=nsmax[:, k:k + 1],
                                       scale=-1.0, accum_out=den[:, k:k + 1]).then_inc(exp_up, 1)
                    elif what == "T":
                        u = BIGBLK[f"T{k}"]
                        act.wait_ge(big_full, u + nb + 1)
                        act.activation(pT[:, 0, :, (k % NT) * P:(k % NT + 1) * P], bflat(u).rearrange("p (k n) -> p k n", k=NT),
                                       ACT.Copy).then_inc(phi_up, 1)
                    else:
                        u, at = BIGBLK[f"{what}{k}"], PV_COLS[what]
                        act.wait_ge(big_full, u + nb + 1)
                        act.activation(qT[:, 0, k, at], big[u % NBIG][:, 0, 0:at.stop - at.start], ACT.Copy).then_inc(ohi_up, 1)
                for t in range(NT):
                    turned(1, t, it)
                    if t == 2:
                        act.wait_ge(row_full, ROWBLK["wo4"] + nr + 1)
                    if t >= 2:
                        highs((W1, W1, W2)[t - 2], (2, 3, 0)[t - 2], (3, 4, 1)[t - 2])
                highs(W2, 1, 2)
                for o in range(KT):
                    act.wait_ge(big_read, BIGBLK[f"m{o}"] + nb + 1)
                    act.activation(kT[:, 0, o, :], rbuf[:, o % 2, :], ACT.Copy).then_inc(hhi_up, 1)
                    if o < 2:
                        highs(W2, 2 + o, 3 + o)
                    for i in ((), (), (0,), (1, 2, 3))[o]:
                        high(S_BLK + PERBLK + i, condw[:, i, :], it)
                for i in range(2):
                    high(S_BLK + S_PERBLK + i, ringpart(RING_BLK + i)[0], it)
                turned(0, 0, it + 1)

        @block.scalar
        def _(act):
            def high(n, to, it=0):
                act.wait_ge(raw_ld[slot(n)], ld_count(n) + it * LD_PERBLK)
                act.activation(to, staged[slot(n)], ACT.Copy).then_inc(shi_up, 1)

            act.wait_ge(const1, 4)
            act.dma_start(tmp64[0][:, 0:N], a["node_vec1"].rearrange("n o -> o n").broadcast_to([2 * NF, N])).then_inc(f_ld, 16)
            act.dma_start(f_w1[:, :], a["L2_gnn_f_w1"]).then_inc(f_ld, 16)
            act.dma_start(fcol[0:C16, 3:4], a["L2_gnn_f_b1"].unsqueeze(1)).then_inc(f_ld, 16)
            for i in range(4):
                act.dma_start(f_w2[:, 32 * i:32 * i + C16], a["L2_gnn_f_w2"]).then_inc(f_ld, 16)
                act.dma_start(fcol[32 * i:32 * i + C16, 2:3], a["L2_gnn_f_b2"].unsqueeze(1)).then_inc(f_ld, 16)
            for m in range(2):
                high(m, ringpart(m)[0])
            act.wait_ge(emb_up, 1)
            act.activation(tmp64[4], tmp64[3], ACT.Sin).then_inc(sin_done, 1)

            def turned_relu(u, i, t):
                act.wait_ge(big_full, u + 1)
                act.activation(yT[:, 0, :, t * P:(t + 1) * P], bflat(u)[:, 0:D].rearrange("p (k n) -> p k n", k=KT),
                               ACT.Relu).then_inc(yhi_up, 1)

            for t in range(NT):
                turned_relu(BIG0[f"l0_{t}"], t, t)
            act.wait_ge(big_read, BIG0["z1"] + 1)
            act.activation(mask[0:C16, 2, :], mask[0:C16, 1, :], ACT.Sigmoid).then_inc(sig_done, 1)
            act.wait_ge(big_full, BIG0["hall"] + 1)
            act.activation(h0[:, 0, :, :], bflat(BIG0["hall"]).rearrange("p (t n) -> p t n", t=NT), ACT.Copy).then_inc(h0hi_up, 1)
            for m in range(2, 4):
                high(m, ringpart(m)[0])
            act.wait_ge(condT_up, 2)
            act.wait_ge(w_ready, 2)
            passes = act.value_load(span_i[0:1, 1:2], min_val=0, max_val=NP // WIN)
            with act.Fori(0, passes + 1) as kp:
                with act.Fori(0, NG // HOT) as gi:
                    for b in range(HOT):
                        g = gi * HOT + b
                        act.wait_ge(scat_full, kp * NG + g + 1)
                        act.activation(hot_abs[b % 2], iota16[:, :], ACT.Abs, bias=src_col[:, CH - 1, bass.ds(g, 1)], scale=-1.0).then_inc(hot_abs_up, 1)
                        act.wait_ge(hot_abs_up, kp * NG + g + 1)
                        act.activation(hot_src[b][:, CH - 1, :], hot_abs[b % 2], ACT.Relu, bias=1.0, scale=-1.0).then_inc(hot_act_up, 1)
            act.wait_ge(dinv_up, 1)
            for t in range(NT):
                act.activation(adj[:, 0, t, :], w_acc[:, t, :], ACT.Copy, scale=degs[:, 3, t:t + 1]).then_inc(whi_up, 1)
            for m in range(4, RING):
                high(m, ringpart(m)[0])
            act.wait_ge(big_full, BIG0["agg"] + 1)
            act.activation(wide(aT[:, 0, :]), bwide(BIG0["agg"]), ACT.Copy).then_inc(ahi_up, 1)
            high(RING, ringpart(RING)[0])
            for t in range(NT):
                act.activation(adj[:, 0, t, :], cnt_acc[:, t, :], ACT.Copy,
                               accum_out=flag[:, 0, t:t + 1]).then_inc(chi_up, 1)
            act.wait_ge(row_full, ROW0["o4"] + 1)
            high(RING + 1, ringpart(RING + 1)[0])
            for t in range(NT):
                turned_relu(BIG0[f"l1_{t}"], NT + t, t)
            for t in range(NT):
                act.wait_ge(row_full, ROW0[f"z{t}"] + 1)
                act.activation(vrow[:, 0, t, :], brow(ROW0[f"z{t}"]), ACT.Copy).then_inc(zhi_up, 1)
                if t == NT - 1:
                    for m in range(RING + 2, RING_BLK):
                        high(m, ringpart(m)[0])
                act.wait_ge(clamp_up, t + 1)
                act.activation(mask[:, t, :], mask[:, t, :], ACT.Ln).then_inc(ln_up, 1)
            for t in range(NT):
                if t:
                    high(S_COND + t - 1, condw[:, t - 1, :])
                act.wait_ge(row_read, ROW0[f"a{t}"] + 1)
                if t >= 2:
                    act.wait_ge(l1p_up, t - 1)
                act.activation(sg[:, t % 2, :], t2[:, t % 2, :], ACT.Sigmoid).then_inc(gate_up, 1)
            act_l2(act, high)
            act_l3(act, high, turned_relu)

        def wide_mm(pe, u, terms):
            for i, (l, r) in enumerate(terms):
                for h in range(2):
                    ins = pe.matmul(big[u % NBIG][:, h, 0:HALF], l, r[:, h * HALF:(h + 1) * HALF],
                                    start=(i == 0), stop=(i == len(terms) - 1))
            return ins

        def row_mm(pe, to, terms):
            for i, (l, r) in enumerate(terms):
                ins = pe.matmul(to, l, r, start=(i == 0), stop=(i == len(terms) - 1))
            return ins

        def parts(l, r):
            return [(l[0], r[0]), (l[0], r[1]), (l[1], r[0])]

        def free_big(pe, u, it=0):
            if u >= NBIG:
                pe.wait_ge(big_read, u - NBIG + 1 + it)

        def free_row(pe, u, it=0):
            if u >= NROW:
                pe.wait_ge(row_read, u - NROW + 1 + it)

        def turn(pe, u, src, n):
            for k in range(n):
                ins = pe.transpose(bflat(u)[:, k * P:(k + 1) * P], src[:, k * P:(k + 1) * P], ident[:, :])
            return ins

        def wcol(m, k):
            return [w[:, k * P:(k + 1) * P] for w in ringpart(m)]

        def tile_of(t2, k, t):
            return [t2[:, s, k, t * P:(t + 1) * P] for s in range(2)]

        def both(t2, k):
            return [t2[:, s, k, :] for s in range(2)]

        def pe_l2(pe):
            pe.wait_ge(condT_up, 2)

            def cond(ln, t, b):
                u = BIGBLK[f"c{ln}_{t}"]
                free_big(pe, u, b * len(BLOCK_BIG))
                if t == 0:
                    pe.wait_ge(split_done, S_COND + 2 * ln + 2 + b * S_PERBLK)
                for i in range(2):
                    ins = pe.matmul(big[u % NBIG][:, i, :], condT[:, t * P:(t + 1) * P], condw[:, 2 * ln + i, :], start=True, stop=True)
                ins.then_inc(big_full, 1)

            def turn_y(ln, t, b):
                u = BIGBLK[f"t{ln}_{t}"]
                free_big(pe, u, b * len(BLOCK_BIG))
                pe.wait_ge(big_read, BIGBLK[f"c{ln}_{t}"] + b * len(BLOCK_BIG) + 1)
                turn(pe, u, ybuf[:, t % 2, :], KT).then_inc(big_full, 1)

            for t in range(2):
                cond(0, t, 0)
            for t in range(2):
                turn_y(0, t, 0)
            with pe.Fori(0, BLOCKS) as it:
                nb, nr, ns = it * len(BLOCK_BIG), it * len(BLOCK_ROW), it * S_PERBLK

                def values(t):
                    u = ROWBLK[f"v{t}"]
                    free_row(pe, u, nr)
                    pe.wait_ge(big_read, BIGBLK[f"t0_{t}"] + nb + 1)
                    if t == 0:
                        pe.wait_ge(split_done, S_BLK + WV + KT + ns)
                    row_mm(pe, brow(u)[:, :], sum([parts(tile_of(yT, k, t), ringpart(RING_BLK + WV + k)) for k in range(KT)], [])).then_inc(
                        row_full, 1 + ROW_SPARE * (t == NT - 1))

                for t in (2, 3):
                    cond(0, t, it)
                values(0)
                turn_y(0, 2, it)
                cond(0, 4, it)
                values(1)
                turn_y(0, 3, it)
                values(2)
                turn_y(0, 4, it)
                for t in (3, 4):
                    values(t)
                for i in range(2):
                    for h in range(HEADS):
                        u = BIGBLK["qk"[i] + str(h)]
                        free_big(pe, u, nb)
                        q = (WQ, WK)[i] + h
                        pe.wait_ge(split_done, S_BLK + q + 1 + ns)
                        wide_mm(pe, u, sum([parts(wcol(RING_BLK + q, k), both(yT, k)) for k in range(KT)], [])).then_inc(big_full, 1)
                def row_terms(name, t, left, w, pieces):
                    pe.wait_ge(split_done, S_BLK + w + pieces[-1] + 1 + ns)
                    terms = sum([parts(tile_of(left, k, t), ringpart(RING_BLK + w + k)) for k in pieces], [])
                    for i, (l, r) in enumerate(terms):
                        ins = pe.matmul(brow(ROWBLK[f"{name}{t}"]), l, r, start=(pieces[0] + i == 0),
                                        stop=(pieces[-1] == KT - 1 and i == len(terms) - 1))
                    return ins

                def row_begin(name, t, left, w):
                    free_row(pe, ROWBLK[f"{name}{t}"], nr)
                    row_terms(name, t, left, w, range(KT - 1))

                def out_end(t):
                    pe.wait_ge(big_read, BIGBLK["PVa3" if t < 3 else "PVb3"] + nb + 1)
                    row_terms("wo", t, qT, WO, range(KT - 1, KT)).then_inc(row_full, 1)

                def hidden_end(t):
                    pe.wait_ge(hlo_up, (it + 1) * KT)
                    row_terms("m2_", t, kT, W2, range(KT - 1, KT)).then_inc(row_full, 1)

                for what, k in ATT:
                    if (what, k) == ("PVa", HEADS - 1):
                        row_begin("wo", 0, qT, WO)
                    elif (what, k) == ("PVb", HEADS - 1):
                        out_end(0)
                        row_begin("wo", 1, qT, WO)
                    u = BIGBLK[f"{what}{k}"]
                    free_big(pe, u, nb)
                    if what == "S":
                        h, t = k // NT, k % NT
                        pe.wait_ge(big_read, BIGBLK[f"k{h}"] + nb + 1)
                        wide_mm(pe, u, parts(tile_of(qT, h, t), both(kT, h))).then_inc(big_full, 1)
                    elif what == "T":
                        pe.wait_ge(pn_up, it * HEADS * NT + k + 1)
                        turn(pe, u, pbuf[:, k % 4, :], NT).then_inc(big_full, 1)
                    else:
                        at = PV_COLS[what]
                        last = k * NT + at.stop // P - 1
                        pe.wait_ge(big_read, BIGBLK[f"T{last}"] + nb + 1)
                        pe.wait_ge(vlo_up, (it + 1) * NT)
                        row_mm(pe, big[u % NBIG][:, 0, 0:at.stop - at.start],
                               sum([parts([vrow[:, s, st, k * DH:(k + 1) * DH] for s in range(2)], [pT[:, s, st, at] for s in range(2)])
                                    for st in range(NT)], [])).then_inc(big_full, 1)
                out_end(1)
                for n in norm_order(1):
                    t = int(n[3])
                    (cond if n[0] == "c" else turn_y)(1, t, it)
                    if n[0] == "c" and 1 <= t < NT - 1:
                        row_begin("wo", t + 1, qT, WO)
                        out_end(t + 1)
                for o in range(KT):
                    u = BIGBLK[f"m{o}"]
                    free_big(pe, u, nb)
                    pe.wait_ge(split_done, S_BLK + W1 + o + 1 + ns)
                    terms = sum([parts(wcol(RING_BLK + W1 + o, k), both(yT, k)) for k in range(KT)], [])
                    for h in range(2):
                        if o == 0:
                            pe.wait_ge(big_read, BIGBLK[f"t1_{2 * (h + 1)}"] + nb + 1)
                        ins = row_mm(pe, big[u % NBIG][:, h, 0:HALF], [(l, r[:, h * HALF:(h + 1) * HALF]) for l, r in terms])
                    ins.then_inc(big_full, 1 + BIG_SPARE * (o == KT - 1))
                pe.wait_ge(hlo_up, (it + 1) * KT - 1)
                for t in range(2):
                    row_begin("m2_", t, kT, W2)
                for t in range(NT):
                    if t >= 2:
                        row_begin("m2_", t, kT, W2)
                    hidden_end(t)
                    if t == 2:
                        cond(0, 0, it + 1)
                        cond(0, 1, it + 1)
                    elif t > 2:
                        turn_y(0, t - 3, it + 1)

        @block.tensor
        def _(pe):
            pe.wait_ge(const0, 3)
            pe.wait_ge(dstep, 5)
            for name, i in (("src", 3), ("w", 2)):
                u = BIG0[name]
                for j in range(CH):
                    ins = pe.transpose(bflat(u)[:, j * NG:(j + 1) * NG], edge[0:NG, i, j * P:(j + 1) * P], ident[0:NG, 0:NG])
                ins.then_inc(big_full, 1)
            pe.wait_ge(dstep, 7)
            pe.matmul(bflat(BIG0["base"])[:, 0:2 * NG], ones[0:NG, :], xn[0:NG, 0, 0:2 * NG],
                      start=True, stop=True).then_inc(big_full, 1)
            u = BIG0["dst"]
            free_big(pe, u)
            for j in range(CH):
                ins = pe.transpose(bflat(u)[:, j * NG:(j + 1) * NG], edge[0:NG, 4, j * P:(j + 1) * P], ident[0:NG, 0:NG])
            ins.then_inc(big_full, 1)
            def turn_norm(u, i, t):
                free_big(pe, u)
                pe.wait_ge(xn_up, i + 1)
                turn(pe, u, xn[:, t % 2, :], KT).then_inc(big_full, 1)

            for t in range(NT):
                turn_norm(BIG0[f"l0_{t}"], t, t)
            u = ROW0["vec"]
            pe.wait_ge(vec_ld, 16 * 9)
            pe.transpose(brow(u)[:, 0:VECS], vec[:, :], ident[0:VECS, 0:VECS]).then_inc(row_full, 1)
            u = BIG0["z1"]
            free_big(pe, u)
            pe.wait_ge(sin_done, 1)
            pe.wait_ge(f_ld, 16 * F_LOADS)
            for h in range(2):
                ins = pe.matmul(big[u % NBIG][0:C16, h, 0:HALF], f_w1[:, :], tmp64[4][:, h * HALF:(h + 1) * HALF], start=True, stop=True)
            ins.then_inc(big_full, 1)
            u = ROW0["brow"]
            free_row(pe, u)
            pe.wait_ge(bconv_up, 1)
            pe.wait_ge(split_done, Q_LIN + 1)
            row_mm(pe, brow(u)[:, :], parts([bc_hl[:, 0, :], bc_hl[:, 1, :]], ringpart(Q_LIN))).then_inc(row_full, 1)
            u = BIG0["cond"]
            free_big(pe, u)
            pe.wait_ge(silu_up, 1)
            wide_mm(pe, u, [(f_w2[:, :], mask[0:C16, 3, :])]).then_inc(big_full, 1)
            u = BIG0["hall"]
            free_big(pe, u)
            pe.wait_ge(split_done, Q_CONV + 1)
            pe.wait_ge(big_read, BIG0[f"l0_{NT - 1}"] + 1)
            for t in range(NT):
                ins = row_mm(pe, bflat(u)[:, t * P:(t + 1) * P], sum([parts(tile_of(yT, k, t), wcol(Q_CONV, k)) for k in range(KT)], []))
            ins.then_inc(big_full, 1)
            pe.wait_ge(big_read, BIG0["hall"])
            pe.wait_ge(w_ready, 2)
            passes = pe.value_load(span_i[0:1, 1:2], min_val=0, max_val=NP // WIN)
            with pe.Fori(0, passes + 1) as kp:
                with pe.Fori(0, NG // HOT) as gi:
                    for b in range(HOT):
                        c = kp * NG + gi * HOT + b + 1
                        to = scat(b)
                        pe.wait_ge(hot_src_up, c)
                        pe.wait_ge(hot_act_up, c)
                        pe.wait_ge(hot_w_up, c)
                        pe.wait_ge(scat_read, c)
                        for j in range(CH):
                            for t in range(NT):
                                s = hot_src[b][:, j, t * P:(t + 1) * P]
                                o = t * 2 * WIN
                                pe.matmul(to[:, o:o + 2 * WIN], s, hot_dst[:, b, j, 0:2 * WIN],
                                          start=(j == 0 and t == 0), stop=False, skip_group_check=True)
                                for i in (2, 3):
                                    ins = pe.matmul(to[:, o + WIN:o + 2 * WIN], s, hot_dst[:, b, j, i * WIN:(i + 1) * WIN],
                                                    start=False, stop=(j == CH - 1 and i == 3), skip_group_check=True)
                        ins.then_inc(scat_full, 1)
            pe.wait_ge(diag_up, NT)
            for name, m in (("degw", w_acc), ("degc", cnt_acc)):
                u = BIG0[name]
                free_big(pe, u)
                for cols640 in (slice(0, D), slice(D, NP)):
                    ins = row_mm(pe, bflat(u)[:, cols640], [(ones[:, :], m[:, st, cols640]) for st in range(NT)])
                ins.then_inc(big_full, 1)
            u = BIG0["agg"]
            free_big(pe, u)
            pe.wait_ge(wlo_up, NT)
            pe.wait_ge(big_read, BIG0["hall"] + 1)
            wide_mm(pe, u, sum([parts(both(h0, st), both(adj, st)) for st in range(NT)], [])).then_inc(big_full, 1)
            pe.wait_ge(big_read, u + 1)
            for t in range(NT):
                u = ROW0[f"o{t}"]
                free_row(pe, u)
                row_mm(pe, brow(u)[:, :], parts([aT[:, s, t * P:(t + 1) * P] for s in range(2)], ringpart(Q_LIN))).then_inc(row_full, 1)
            for t in range(NT):
                turn_norm(BIG0[f"l1_{t}"], LN_L1 + t, t)
            pe.wait_ge(split_done, Q_L + KT)
            for t in range(NT):
                u = ROW0[f"z{t}"]
                free_row(pe, u)
                pe.wait_ge(big_read, BIG0[f"l1_{t}"] + 1)
                row_mm(pe, brow(u)[:, :], sum([parts(tile_of(yT, k, t), ringpart(Q_L + k)) for k in range(KT)], [])).then_inc(row_full, 1)
            pe.wait_ge(split_done, Q_R + KT)
            pe.wait_ge(clo_up, NT)
            for t in range(NT):
                u = ROW0[f"r{t}"]
                free_row(pe, u)
                row_mm(pe, brow(u)[:, :], sum([parts(tile_of(yT, k, t), ringpart(Q_R + k)) for k in range(KT)], [])).then_inc(row_full, 1)
                u = ROW0[f"a{t}"]
                pe.wait_ge(row_read, ROW0["z4"] + 1)
                free_row(pe, u)
                row_mm(pe, brow(u)[:, :], sum([parts(tile_of(adj, st, t), both(vrow, st)) for st in range(NT)], [])).then_inc(row_full, 1)
            pe_l2(pe)
            pe_l3(pe, turn_norm)

        def dve_l2(dve, tile_sums, tile_moments, tile_stats, normalise, f32):
            dve.wait_ge(mask_up, NT)
            for t in range(NT):
                normalise(LN_IN + t, t, x[:, t, :], z[:, t, :])
                dve.wait_ge(xn_up, LN_IN + t + 1)
                dve.tensor_scalar(z[:, t, :], z[:, t, :], 0.0, None, ALU.max).then_inc(z_up, 1)
                dve.wait_ge(z_up, t + 1)
                tile_stats(LN_BLK + t, NT + t, z[:, t, :])
            def norm_tile(ln, t, b):
                return LN_BLK + b * 2 * NT + ln * NT + t, (NT + ln * NT + t) % (2 * NT)

            def centred(ln, t, b):
                i, slot = norm_tile(ln, t, b)
                u = BIGBLK[f"c{ln}_{t}"]
                if t >= 2:
                    dve.wait_ge(big_full, BIGBLK[f"t{ln}_{t - 2}"] + b * len(BLOCK_BIG) + 1)
                dve.wait_ge(aggr_up, i + 1)
                wait_apart(dve, big_full, u + b * len(BLOCK_BIG) + 1)
                dve.scalar_tensor_tensor(ybuf[:, t % 2, :], z[:, t, :], mv[:, slot, 0:1], big[u % NBIG][:, 0, :],
                                         ALU.subtract, ALU.mult).then_inc(y1_up, 1)

            def scaled(ln, t, b):
                i, slot = norm_tile(ln, t, b)
                u = BIGBLK[f"c{ln}_{t}"]
                dve.wait_ge(rstd_up, i + 1)
                wait_apart(dve, y1_up, b * 2 * NT + ln * NT + t + 1)
                dve.scalar_tensor_tensor(ybuf[:, t % 2, :], ybuf[:, t % 2, :], rstd[:, slot:slot + 1], big[u % NBIG][:, 1, :],
                                         ALU.mult, ALU.add).then_inc(big_read, 1)

            def turned_rest(ln, t, b):
                u = BIGBLK[f"t{ln}_{t}"]
                dve.wait_ge(yhi_up, 2 * NT + b * 2 * NT + ln * NT + t + 1)
                dve.tensor_tensor(yT[:, 1, :, t * P:(t + 1) * P], bflat(u)[:, 0:D].rearrange("p (k n) -> p k n", k=KT),
                                  f32(yT[:, 0, :, t * P:(t + 1) * P]), ALU.subtract).then_inc(big_read, 1)

            for step in (centred, scaled):
                for t in range(2):
                    step(0, t, 0)
            turned_rest(0, 0, 0)
            with dve.Fori(0, BLOCKS) as it:
                nb, nr = it * len(BLOCK_BIG), it * len(BLOCK_ROW)

                def residual(name, t, xb):
                    u = ROWBLK[f"{name}{t}"]
                    dve.wait_ge(row_full, u + nr + 1)
                    dve.wait_ge(xb_up, xb)
                    dve.tensor_tensor(z[:, t, :], brow(u)[:, :], z[:, t, :], ALU.add).then_inc(row_read, 1)

                def out_row(t):
                    residual("wo", t, it * 2 * NT + NT + 1 + t)

                def out_sums(t):
                    dve.wait_ge(row_read, ROWBLK[f"wo{t}"] + nr + 1)
                    tile_sums(norm_tile(1, t, it)[1], z[:, t, :])

                def out_moments(t):
                    tile_moments(*norm_tile(1, t, it))

                def values(t):
                    u = ROWBLK[f"v{t}"]
                    dve.wait_ge(bias_ld, 48 * it + 48)
                    dve.wait_ge(row_full, u + nr + 1)
                    if t >= 2:
                        dve.wait_ge(vlo_up, it * NT + t - 1)
                    dve.tensor_tensor(vbuf[:, t % 2, :], brow(u), bias[:, 0, :], ALU.add).then_inc(
                        row_read, 1 + ROW_SPARE * (t == NT - 1))

                centred(0, 2, it)
                turned_rest(0, 1, it)
                scaled(0, 2, it)
                centred(0, 3, it)
                values(0)
                scaled(0, 3, it)
                turned_rest(0, 2, it)
                centred(0, 4, it)
                values(1)
                scaled(0, 4, it)
                for t in (3, 4):
                    turned_rest(0, t, it)
                    values(t - 1)
                values(4)
                for i, to in enumerate((qT, kT)):
                    for h in range(HEADS):
                        u = BIGBLK["qk"[i] + str(h)]
                        dve.wait_ge(qkhi_up, it * 2 * HEADS + i * HEADS + h + 1)
                        dve.scalar_tensor_tensor(wide(to[:, 1, h, :]), bwide(u), bqk[:, i, bass.ds(it * KT + h, 1)],
                                                 wide(f32(to[:, 0, h, :])), ALU.add, ALU.subtract).then_inc(big_read, 1)
                heads = it * HEADS * NT
                for what, k in ATT + [("last", 0)]:
                    if what == "S":
                        u = BIGBLK[f"S{k}"]
                        t = k % NT
                        if k >= 4:
                            dve.wait_ge(big_full, BIGBLK[f"T{k - 4}"] + nb + 1)
                        wait_apart(dve, big_full, u + nb + 1)
                        dve.tensor_tensor_reduce(wide(pbuf[:, k % 4, :]), bwide(u), wide(mask[:, t, :]), -DH ** -0.5, 3e38,
                                                 ALU.add, ALU.min, nsmax[:, k:k + 1]).then_inc(big_read, 1)
                    if what == "S" and k >= 1 or (what, k) == ("T", HEADS * NT - LAG):
                        j = k - 1 if what == "S" else HEADS * NT - 1
                        dve.wait_ge(exp_up, heads + j + 1)
                        dve.reciprocal(rden[:, j:j + 1], den[:, j:j + 1]).then_inc(rden_up, 1)
                    if what == "T":
                        u, t = BIGBLK[f"T{k}"], k % NT
                        dve.wait_ge(phi_up, heads + k + 1)
                        dve.tensor_tensor(pT[:, 1, :, t * P:(t + 1) * P], bflat(u).rearrange("p (k n) -> p k n", k=NT),
                                          f32(pT[:, 0, :, t * P:(t + 1) * P]), ALU.subtract).then_inc(big_read, 1)
                    elif what in PV_COLS:
                        if (what, k) == ATT[-1]:
                            out_row(0)
                            out_sums(0)
                        u, at = BIGBLK[f"{what}{k}"], PV_COLS[what]
                        dve.wait_ge(ohi_up, it * 2 * HEADS + 2 * k + 1 + (what == "PVb"))
                        dve.tensor_tensor(qT[:, 1, k, at], big[u % NBIG][:, 0, 0:at.stop - at.start], f32(qT[:, 0, k, at]), ALU.subtract).then_inc(big_read, 1)
                out_moments(0)
                for t in range(NT):
                    centred(1, t, it)
                    if t < NT - 1:
                        out_row(t + 1)
                    else:
                        turned_rest(1, t - 2, it)
                    scaled(1, t, it)
                    if t < NT - 1:
                        out_sums(t + 1)
                    if 1 <= t < NT - 2:
                        turned_rest(1, t - 1, it)
                    if t < NT - 1:
                        out_moments(t + 1)
                for t in range(NT - 2, NT):
                    turned_rest(1, t, it)
                for o in range(KT + 1):
                    if o >= 1:
                        dve.wait_ge(hhi_up, it * KT + o)
                        dve.tensor_tensor(kT[:, 1, o - 1, :], rbuf[:, (o - 1) % 2, :], f32(kT[:, 0, o - 1, :]), ALU.subtract).then_inc(hlo_up, 1)
                    if o < KT:
                        u = BIGBLK[f"m{o}"]
                        dve.wait_ge(big_full, u + nb + 1)
                        if o >= 2:
                            dve.wait_ge(hlo_up, it * KT + o - 1)
                        dve.tensor_scalar(wide(rbuf[:, o % 2, :]), bwide(u), bqk[:, 2, bass.ds(it * KT + o, 1)], 0.0,
                                          ALU.add, ALU.max).then_inc(big_read, 1 + BIG_SPARE * (o == KT - 1))

                def hidden_row(t):
                    residual("m2_", t, (it + 1) * 2 * NT + 1 + t)

                def hidden_sums(t):
                    dve.wait_ge(row_read, ROWBLK[f"m2_{t}"] + nr + 1)
                    tile_sums(NT + t, z[:, t, :])

                for t in range(NT):
                    hidden_row(t)
                    if t == NT - 1:
                        turned_rest(0, 0, it + 1)
                    if 2 <= t < 4:
                        centred(0, t - 2, it + 1)
                    hidden_sums(t)
                    if 2 <= t < 4:
                        scaled(0, t - 2, it + 1)
                    tile_moments(*norm_tile(0, t, it + 1))
            dve.memset(nsmax[:, 0:1], 0.0).then_inc(big_read, 1)
            for t in range(NT):
                dve.tensor_tensor(x[:, t, :], x[:, t, :], z[:, t, :], ALU.add).then_inc(x_up, 1)
        @block.vector
        def _(dve):
            own = [0]

            def step(ins):
                own[0] += 1
                ins.then_inc(dstep, 1)
                dve.wait_ge(dstep, own[0])

            def f32(ap):
                return ap.bitcast(F32)

            dve.memset(edge[0:NG, 0, :].bitcast(I32), 9999).then_inc(e_clear, 1)
            dve.memset(edge[0:NG, 2, :], 0.0).then_inc(e_clear, 1)
            dve.memset(x[:, NT - 1, :], 0.0).then_inc(x_clear, 1)
            dve.wait_ge(e_ld, 16 * 7)
            step(dve.tensor_copy(edge[0:NG, 3, :], edge[0:NG, 0, :].bitcast(I32)))
            step(dve.tensor_copy(edge[0:NG, 4, :], edge[0:NG, 1, :].bitcast(I32)))
            step(dve.tensor_reduce(mnmx[0:NG, 0:1], edge[0:NG, 4, :], AX.X, ALU.min))
            step(dve.tensor_reduce(mnmx[0:NG, 1:2], edge[0:NG, 4, :], AX.X, ALU.max))
            step(dve.tensor_tensor(mnmx[0:NG, 2:3], mnmx[0:NG, 1:2], mnmx[0:NG, 0:1], ALU.subtract))
            dve.wait_ge(const0, 3)
            step(dve.tensor_scalar(xn[0:NG, 0, 0:NG], ident[0:NG, 0:NG], mnmx[0:NG, 0:1], None, ALU.mult))
            step(dve.tensor_scalar(xn[0:NG, 0, NG:2 * NG], ident[0:NG, 0:NG], mnmx[0:NG, 2:3], None, ALU.mult))
            for name, to in (("src", src_col), ("w", w_col)):
                dve.wait_ge(big_full, BIG0[name] + 1)
                dve.tensor_copy(to[:, :, :], bflat(BIG0[name])[:, 0:CH * NG].rearrange("p (j g) -> p j g", j=CH)).then_inc(big_read, 1)
            u = BIG0["base"]
            dve.wait_ge(big_full, u + 1)
            step(dve.tensor_copy(base_f[:, :], bflat(u)[:, 0:NG]))
            dve.tensor_reduce(span[:, 0:1], bflat(u)[:, NG:2 * NG], AX.X, ALU.max).then_inc(big_read, 1)
            u = BIG0["dst"]
            dve.wait_ge(big_full, u + 1)
            dve.tensor_tensor(dst_rel[:, :, :], bflat(u)[:, 0:CH * NG].rearrange("p (j g) -> p j g", j=CH),
                              base_f[:, :].unsqueeze(1).broadcast_to([P, CH, NG]), ALU.subtract).then_inc(big_read, 1)
            step(dve.tensor_copy(base_i[:, :], base_f[0:1, :]))
            dve.wait_ge(big_read, u + 1)
            step(dve.tensor_scalar(span[:, 1:2], span[:, 0:1], float(PASS_MUL), None, ALU.mult))
            step(dve.tensor_copy(span_i[:, 0:1], span[:, 1:2]))
            dve.tensor_scalar(span_i[:, 1:2], span_i[:, 0:1], 16, None, ALU.arith_shift_right).then_inc(w_ready, 1)
            step(dve.tensor_copy(w_part[:, 0, :, :], w_col[:, :, :]))
            for i in (1, 2):
                step(dve.tensor_tensor(w_col[:, :, :], w_col[:, :, :], w_part[:, i - 1, :, :], ALU.subtract))
                ins = dve.tensor_copy(w_part[:, i, :, :], w_col[:, :, :])
                if i == 1:
                    step(ins)
            ins.then_inc(w_ready, 1)
            def tile_sums(slot, src):
                dve.bn_stats(stats[:, slot, :], src).then_inc(st_up, 1)

            def tile_moments(i, slot):
                wait_apart(dve, st_up, i + 1)
                dve.bn_aggr(mv[:, slot, :], stats[:, slot, :]).then_inc(aggr_up, 1)

            def tile_stats(i, slot, src):
                tile_sums(slot, src)
                tile_moments(i, slot)

            def normalise(i, slot, src, to):
                dve.wait_ge(rstd_up, i + 1)
                dve.tensor_scalar(to, src, mv[:, slot, 0:1], rstd[:, slot:slot + 1],
                                  ALU.subtract, ALU.mult).then_inc(xn_up, 1)

            def turned_rest(u, i, t):
                dve.wait_ge(yhi_up, i + 1)
                dve.scalar_tensor_tensor(yT[:, 1, :, t * P:(t + 1) * P], bflat(u)[:, 0:D].rearrange("p (k n) -> p k n", k=KT),
                                         0.0, f32(yT[:, 0, :, t * P:(t + 1) * P]), ALU.max, ALU.subtract).then_inc(big_read, 1)

            def relu_norm(first, slot0, names, yfirst):
                for t in range(NT + 1):
                    if t < NT:
                        if t >= 2:
                            dve.wait_ge(big_full, names[t - 2] + 1)
                        normalise(first + t, slot0 + t, x[:, t, :], xn[:, t % 2, :])
                    if t >= 1:
                        turned_rest(names[t - 1], yfirst + t - 1, t - 1)

            dve.wait_ge(x_ld, 32)
            for t in range(NT):
                tile_stats(t, t, x[:, t, :])
            dve.wait_ge(const1, 3)
            dve.wait_ge(f_ld, 16 * F_LOADS)
            step(dve.tensor_scalar(fcol[0:2 * NF, 1:2], freq_i, float(np.float32(2.0 * np.pi / 16)), None, ALU.mult))
            noise, ph, kf, r = tmp64[0:4]
            step(dve.tensor_scalar(ph, noise, fcol[0:2 * NF, 1:2], None, ALU.mult))
            MAGIC = 1.5 * 2.0 ** 23
            step(dve.tensor_scalar(kf, ph, float(1 / (2 * np.pi)), MAGIC, ALU.mult, ALU.add))
            step(dve.tensor_scalar(kf, kf, MAGIC, None, ALU.subtract))
            TURN_HI = 6.28125
            step(dve.scalar_tensor_tensor(r, kf, -TURN_HI, ph, ALU.mult, ALU.add))
            step(dve.scalar_tensor_tensor(r, kf, -float(2 * np.pi - TURN_HI), r, ALU.mult, ALU.add))
            step(dve.tensor_scalar(r, r, 3.1415925, -3.1415925, ALU.min, ALU.max))
            c = r[NF:2 * NF]
            step(dve.scalar_tensor_tensor(c, c, -1.0, c, ALU.mult, ALU.max))
            dve.tensor_scalar(c, c, -1.0, float(np.pi / 2), ALU.mult, ALU.add).then_inc(emb_up, 1)
            relu_norm(0, 0, [BIG0[f"l0_{t}"] for t in range(NT)], 0)
            u = ROW0["vec"]
            dve.wait_ge(row_full, u + 1)
            dve.tensor_copy(cols[:, :], brow(u)[:, 0:VECS]).then_inc(row_read, 1)
            dve.wait_ge(row_read, u + 1)
            u = BIG0["z1"]
            dve.wait_ge(big_full, u + 1)
            z1 = mask[0:C16, 1, :]
            dve.tensor_scalar(wide(z1), big[u % NBIG][0:C16, :, 0:HALF], fcol[0:C16, 3:4], None, ALU.add).then_inc(big_read, 1)
            step(dve.tensor_scalar(bc_hl[:, 0, :], ones[:, :], bconv[:, 0:1], None, ALU.mult))
            dve.scalar_tensor_tensor(bc_hl[:, 1, :], ones[:, :], bconv[:, 0:1], f32(bc_hl[:, 0, :]), ALU.mult, ALU.subtract).then_inc(bconv_up, 1)
            dve.wait_ge(sig_done, 1)
            dve.tensor_tensor(mask[0:C16, 3, :], z1, mask[0:C16, 2, :], ALU.mult).then_inc(silu_up, 1)
            u = ROW0["brow"]
            dve.wait_ge(col_ld, 16 * 2)
            dve.wait_ge(row_full, u + 1)
            dve.tensor_tensor(bias[:, 0, :], brow(u)[:, :], bias[:, 0, :], ALU.add).then_inc(row_read, 1)
            u = BIG0["cond"]
            dve.wait_ge(cb_one, 8)
            dve.wait_ge(big_full, u + 1)
            ct = mask[:, 4, :]
            dve.tensor_scalar(wide(ct), bwide(u), fcol[:, 2:3], None, ALU.add).then_inc(big_read, 1)
            dve.wait_ge(big_read, u + 1)
            step(dve.tensor_copy(condT[:, :], ct))
            for lo in (slice(32, 64), slice(96, P)):
                dve.tensor_tensor(condT[lo, :], ct[lo], f32(condT[lo, :]), ALU.subtract).then_inc(condT_up, 1)

            dve.wait_ge(w_ready, 2)
            passes = dve.value_load(span_i[0:1, 1:2], min_val=0, max_val=NP // WIN)
            with dve.Fori(0, passes + 1) as kp:
                def hot(g, b):
                    dve.wait_ge(scat_full, kp * NG + g + 1)
                    for j in range(CH - 1):
                        ins = dve.tensor_scalar(hot_src[b][:, j, :], iota16[:, :], src_col[:, j, bass.ds(g, 1)], None, ALU.is_equal)
                    ins.then_inc(hot_src_up, 1)
                    dve.tensor_tensor(hot_dst[:, b, :, 0:WIN], iota16[:, 0:WIN].unsqueeze(1).broadcast_to([P, CH, WIN]),
                                      dst_rel[:, :, bass.ds(g, 1)].broadcast_to([P, CH, WIN]), ALU.is_equal).then_inc(hot_dst_up, 1)

                def add(g, b):
                    w0 = dve.value_load(base_i[0:1, bass.ds(g, 1)], min_val=0, max_val=NP)
                    dve.wait_ge(scat_full, kp * NG + g + HOT + 1)
                    dve.wait_ge(scat_read, kp * NG + g + HOT)
                    win = adjacc[:, :, :, bass.ds(w0, WIN)]
                    dve.tensor_tensor(win, scat(b).rearrange("p (t c n) -> p t c n", t=NT, c=2), win, ALU.add).then_inc(scat_read, 1)

                for b in range(HOT - 1):
                    hot(b, b)
                with dve.Fori(0, NG // HOT - 1) as gi:
                    for b in range(HOT):
                        hot(gi * HOT + b + HOT - 1, (b + HOT - 1) % HOT)
                        add(gi * HOT + b, b)
                hot(NG - 1, HOT - 1)
                for b in range(HOT):
                    add(NG - HOT + b, b)
                dve.tensor_scalar(dst_rel[:, :, :], dst_rel[:, :, :], float(WIN), None, ALU.subtract).then_inc(pass_up, 1)
                dve.tensor_scalar(base_f[0:1, :], base_f[0:1, :], float(WIN), float(NP), ALU.add, ALU.min).then_inc(pass_up, 1)
                dve.wait_ge(pass_up, kp * 3 + 2)
                dve.tensor_copy(base_i[:, :], base_f[0:1, :]).then_inc(pass_up, 1)
                dve.wait_ge(pass_up, kp * 3 + 3)
            dve.wait_ge(scat_read, (passes + 1) * NG + HOT)

            for t in range(NT):
                d = w_acc[:, t, t * P:(t + 1) * P]
                dve.tensor_tensor(d, d, ident[:, :], ALU.add).then_inc(diag_up, 1)
            def own_sums(name, to):
                u = BIG0[name]
                dve.wait_ge(big_full, u + 1)
                for t in range(NT):
                    ins = dve.tensor_tensor_reduce(xn[:, t // KT, (t % KT) * P:(t % KT + 1) * P], bflat(u)[:, t * P:(t + 1) * P],
                                                   ident[:, :], 1.0, 0.0, ALU.mult, ALU.add, to[:, t:t + 1])
                ins.then_inc(big_read, 1)
                dve.wait_ge(big_read, u + 1)

            u = BIG0["hall"]
            dve.wait_ge(h0hi_up, 1)
            dve.tensor_tensor(h0[:, 1, :, :], bflat(u).rearrange("p (t n) -> p t n", t=NT), f32(h0[:, 0, :, :]), ALU.subtract).then_inc(big_read, 1)
            own_sums("degw", degs[:, 0, :])
            dve.tensor_scalar(degs[:, 1, :], degs[:, 0, :], 1e-30, None, ALU.max).then_inc(w_up, 1)
            dve.wait_ge(dpow_up, 1)
            dve.scalar_tensor_tensor(degs[:, 3, :], degs[:, 0, :], 0.0, degs[:, 2, :], ALU.is_gt, ALU.mult).then_inc(dinv_up, 1)
            dve.wait_ge(dinv_up, 1)
            for t in range(NT):
                dve.wait_ge(whi_up, t + 1)
                dve.scalar_tensor_tensor(adj[:, 1, t, :], w_acc[:, t, :], degs[:, 3, t:t + 1], f32(adj[:, 0, t, :]),
                                         ALU.mult, ALU.subtract).then_inc(wlo_up, 1)
            own_sums("degc", rcnt[:, 0, :])
            dve.tensor_scalar(rcnt[:, 0, :], rcnt[:, 0, :], 1.0, None, ALU.max).then_inc(w_up, 1)
            dve.wait_ge(w_up, 2)
            dve.reciprocal(rcnt[:, 1, :], rcnt[:, 0, :]).then_inc(w_up, 1)
            u = BIG0["agg"]
            dve.wait_ge(ahi_up, 1)
            dve.tensor_tensor(wide(aT[:, 1, :]), bwide(u), wide(f32(aT[:, 0, :])), ALU.subtract).then_inc(big_read, 1)
            for t in range(NT):
                u = ROW0[f"o{t}"]
                dve.wait_ge(row_full, u + 1)
                dve.wait_ge(xb_up, t + 1)
                dve.scalar_tensor_tensor(x[:, t, :], brow(u)[:, :], degs[:, 3, t:t + 1], x[:, t, :], ALU.mult, ALU.add).then_inc(row_read, 1)
                dve.wait_ge(row_read, u + 1)
                tile_stats(LN_L1 + t, NT + t, x[:, t, :])
            relu_norm(LN_L1, NT, [BIG0[f"l1_{t}"] for t in range(NT)], NT)
            for t in range(NT):
                u = ROW0[f"z{t}"]
                dve.wait_ge(zhi_up, t + 1)
                dve.tensor_tensor(vrow[:, 1, t, :], brow(u)[:, :], f32(vrow[:, 0, t, :]), ALU.subtract).then_inc(row_read, 1)
                dve.tensor_scalar(mask[:, t, :], cnt_acc[:, t, :], 1.0, None, ALU.max).then_inc(clamp_up, 1)
                dve.wait_ge(chi_up, t + 1)
                dve.tensor_tensor(adj[:, 1, t, :], cnt_acc[:, t, :], f32(adj[:, 0, t, :]), ALU.subtract).then_inc(clo_up, 1)
            step(dve.tensor_scalar(flag[:, 1, :], flag[:, 0, :], 0.5, None, ALU.is_gt))
            step(dve.tensor_scalar(flag[:, 2, :], flag[:, 1, :], NOEDGE, None, ALU.mult))
            step(dve.tensor_scalar(flag[:, 3, :], flag[:, 2, :], -1.0, NOEDGE, ALU.mult, ALU.add))
            for t in range(NT):
                u = ROW0[f"r{t}"]
                dve.wait_ge(row_full, u + 1)
                dve.tensor_tensor(t1[:, t % 2, :], brow(u)[:, :], bias[:, 1, :], ALU.add).then_inc(row_read, 1)
                dve.wait_ge(row_read, u + 1)
                dve.wait_ge(clo_up, NT)
                dve.tensor_scalar(cnt_acc[:, t, :], cnt_acc[:, t, :], 0.5, flag[:, 2, t:t + 1], ALU.is_lt, ALU.mult).then_inc(pen_up, 1)
                dve.wait_ge(pen_up, t + 1)
                dve.wait_ge(ln_up, t + 1)
                dve.scalar_tensor_tensor(mask[:, t, :], mask[:, t, :], DH ** 0.5, cnt_acc[:, t, :], ALU.mult, ALU.add).then_inc(mask_up, 1)
                u = ROW0[f"a{t}"]
                dve.wait_ge(row_full, u + 1)
                if t >= 2:
                    dve.wait_ge(l1p_up, t - 1)
                dve.scalar_tensor_tensor(t2[:, t % 2, :], brow(u)[:, :], rcnt[:, 1, t:t + 1], t1[:, t % 2, :],
                                         ALU.mult, ALU.add).then_inc(row_read, 1)
                dve.wait_ge(gate_up, t + 1)
                dve.tensor_tensor(t1[:, t % 2, :], t2[:, t % 2, :], sg[:, t % 2, :], ALU.mult).then_inc(l1p_up, 1)
                dve.wait_ge(l1p_up, t + 1)
                dve.tensor_tensor(x[:, t, :], x[:, t, :], t1[:, t % 2, :], ALU.add).then_inc(x_up, 1)
                dve.wait_ge(x_up, t + 1)
                tile_stats(LN_IN + t, t, x[:, t, :])
            dve_l2(dve, tile_sums, tile_moments, tile_stats, normalise, f32)
            dve_l3(dve, tile_stats, relu_norm, step)



NAMES = (
    ["x", "src", "dst", "edge_weight", "node_vec1"]
    + ["L0_gnn_" + n for n in ("W_conv", "b_conv", "W_lin", "b_lin")]
    + ["L1_gnn_" + n for n in ("W_l", "W_r", "b")]
    + ["L2_gnn_" + n for n in ("f_w1", "f_b1", "f_w2", "f_b2", "s1_w", "s1_b", "b1_w", "b1_b", "wq", "bq", "wk", "bk",
                               "wv", "bv", "wo", "bo", "s2_w", "s2_b", "b2_w", "b2_b", "m_w1", "m_b1", "m_w2", "m_b2")]
    + ["L3_gnn_" + n for n in ("W_f", "att_src_f", "att_dst_f", "bias_f", "W_b", "att_src_b", "att_dst_b", "bias_b",
                               "W_fuse", "b_fuse", "bn_gamma", "bn_beta")]
)


def kernel(**inputs):
    import numpy as np
    import concourse.bacc as bacc
    from concourse import mybir
    from concourse.bass_utils import run_bass_kernel_spmd as run

    nc = bacc.Bacc("TRN2", target_bir_lowering=False, num_devices=1)
    arrays, aps = {}, {}
    for name in NAMES:
        v = np.ascontiguousarray(inputs[name])
        arrays["in_" + name] = v
        aps[name] = nc.dram_tensor("in_" + name, v.shape, mybir.dt.from_np(v.dtype), kind="ExternalInput").ap()
    out = nc.dram_tensor("out_x", (N, D), F32, kind="ExternalOutput").ap()
    build(nc, aps, out)
    r = run(nc, [arrays], core_ids=[0])
    return r.results[0]["out_x"]
```
